# Optimizing a Trainium2 kernel written in Bass

```python
import numpy as np
import jax
import jax.numpy as jnp

def _softmax(x, axis=-1):
    return jax.nn.softmax(x, axis=axis)

def _gelu(x):
    return jax.nn.gelu(x, approximate=True)

def _silu(x):
    return jax.nn.silu(x)

def _sigmoid(x):
    return jax.nn.sigmoid(x)

def _layernorm(x, axis=-1, eps=1e-05):
    m = jnp.mean(x, axis=axis, keepdims=True)
    v = jnp.var(x, axis=axis, keepdims=True)
    return (x - m) / jnp.sqrt(v + eps)

def _scatter_add(tgt, idx, src, axis=0):
    return tgt.at[idx].add(src)

def _segment_sum(src, seg, n):
    return jax.ops.segment_sum(src, seg, n)
kernel_name = 'mk_gnn_preln_d4_gnn_r32_ef31b1'

def setup_inputs(seed: int=0):
    np.random.seed(seed)
    _w = jnp.asarray

    def _rec_inputs():
        import jax
        import jax.numpy as jnp
        _gk = jax.random.key(seed)
        x = 0.0004528 + 0.9998 * jax.random.normal(jax.random.fold_in(_gk, 1), (3125, 16), jnp.float32)
        src = jax.random.randint(jax.random.fold_in(_gk, 2), (100000,), 0, 3125, jnp.int32)
        dst = jax.random.randint(jax.random.fold_in(_gk, 3), (100000,), 0, 3125, jnp.int32)
        _o = jnp.argsort(dst, stable=True)
        src = src[_o]
        dst = dst[_o]
        edge_attr_8 = -5.3897e-05 + 0.999841 * jax.random.normal(jax.random.fold_in(_gk, 13), (100000, 8), jnp.float32)
        edge_type_230 = jax.random.randint(jax.random.fold_in(_gk, 15), (100000,), 0, 230, jnp.int32)
        edge_type_8 = jax.random.randint(jax.random.fold_in(_gk, 16), (100000,), 0, 8, jnp.int32)
        node_vec1 = -0.00472126 + 0.997171 * jax.random.normal(jax.random.fold_in(_gk, 17), (3125, 1), jnp.float32)
        return (x, src, dst, edge_attr_8, edge_type_230, edge_type_8, node_vec1)
    x, src, dst, edge_attr_8, edge_type_230, edge_type_8, node_vec1 = _rec_inputs()

    def _L0_gnn_setup():
        import jax, jax.numpy as jnp
        import numpy as np
        NUM_ENTITIES = 3125
        NUM_RELATIONS = 8
        NUM_CLASSES = 16
        HIDDEN = 16
        NUM_EDGES = 100000

        def rgcn_conv(x, src, dst, edge_type, W, root, bias):
            num_nodes = x.shape[0]
            x_src = x[src]
            msg = jnp.zeros((src.shape[0], W.shape[2]), x.dtype)
            for r in range(NUM_RELATIONS):
                msg = msg + jnp.where((edge_type == r)[:, None], x_src @ W[r], jnp.zeros((), x.dtype))
            cnt = jnp.zeros((num_nodes, NUM_RELATIONS), x.dtype).at[dst, edge_type].add(1.0)
            norm = 1.0 / jnp.maximum(cnt[dst, edge_type], 1.0)
            agg = jax.ops.segment_sum(msg * norm[:, None], dst, num_segments=num_nodes)
            return agg + x @ root + bias
        key = jax.random.key(seed)
        ks = jax.random.split(key, 9)
        s = 1.0 / np.sqrt(HIDDEN)
        edge_index = jax.random.randint(ks[0], (2, NUM_EDGES), 0, NUM_ENTITIES, dtype=jnp.int32)
        edge_type = jax.random.randint(ks[1], (NUM_EDGES,), 0, NUM_RELATIONS, dtype=jnp.int32)
        return {'embed': jax.random.normal(ks[2], (NUM_ENTITIES, HIDDEN), jnp.float32), 'W1': jax.random.normal(ks[3], (NUM_RELATIONS, HIDDEN, HIDDEN), jnp.float32) * s, 'root1': jax.random.normal(ks[4], (HIDDEN, HIDDEN), jnp.float32) * s, 'b1': jnp.zeros((HIDDEN,), jnp.float32), 'W2': jax.random.normal(ks[5], (NUM_RELATIONS, HIDDEN, NUM_CLASSES), jnp.float32) * s, 'root2': jax.random.normal(ks[6], (HIDDEN, NUM_CLASSES), jnp.float32) * s, 'b2': jnp.zeros((NUM_CLASSES,), jnp.float32), 'edge_index': edge_index, 'edge_type': edge_type}
    _L0_gnn_all = _L0_gnn_setup()
    _L0_gnn_in = {k: v for k, v in _L0_gnn_all.items() if k in ('W1', 'root1', 'b1', 'W2', 'root2', 'b2')}
    del _L0_gnn_all

    def _L1_gnn_setup():
        import jax, jax.numpy as jnp
        import numpy as np
        N_NODES = 3125
        N_EDGES = 100000
        D_NODE = 16
        D_EDGE = 8
        D_HIDDEN = 16
        key = jax.random.key(seed)
        ks = jax.random.split(key, 8)
        node_features = jax.random.normal(ks[0], (N_NODES, D_NODE), dtype=jnp.float32)
        edge_attr_e3nn = jax.random.normal(ks[1], (N_EDGES, D_EDGE), dtype=jnp.float32)
        node_attr_scalar_raw = jax.random.normal(ks[2], (N_NODES, 1), dtype=jnp.float32)
        W_msg_tp = jax.random.normal(ks[3], (D_NODE, D_EDGE, D_HIDDEN), dtype=jnp.float32)
        W_msg_lin = jax.random.normal(ks[4], (D_HIDDEN, D_HIDDEN), dtype=jnp.float32)
        W_upd_tp = jax.random.normal(ks[5], (D_NODE, D_HIDDEN, D_HIDDEN), dtype=jnp.float32)
        W_upd_lin = jax.random.normal(ks[6], (D_HIDDEN, D_NODE), dtype=jnp.float32)
        edge_index = jax.random.randint(ks[7], (2, N_EDGES), 0, N_NODES, dtype=jnp.int64)
        return {'node_features': node_features, 'edge_attr_e3nn': edge_attr_e3nn, 'node_attr_scalar_raw': node_attr_scalar_raw, 'W_msg_tp': W_msg_tp, 'W_msg_lin': W_msg_lin, 'W_upd_tp': W_upd_tp, 'W_upd_lin': W_upd_lin, 'edge_index': edge_index}
    _L1_gnn_all = _L1_gnn_setup()
    _L1_gnn_in = {k: v for k, v in _L1_gnn_all.items() if k in ('W_msg_tp', 'W_msg_lin', 'W_upd_tp', 'W_upd_lin')}
    del _L1_gnn_all

    def _L2_gnn_setup():
        import jax, jax.numpy as jnp
        import numpy as np
        C = 0.01
        EPS = 1e-06
        MIN_NORM = 1e-10
        BALL_EPS = 1e-05

        def _norm(x):
            return jnp.sqrt(jnp.clip(jnp.sum(x * x, axis=-1, keepdims=True), MIN_NORM))

        def log_map_zero(x, c):
            sc = jnp.sqrt(c)
            n = _norm(x)
            return jnp.arctanh(jnp.clip(sc * n, -1.0 + BALL_EPS, 1.0 - BALL_EPS)) * x / (sc * n)

        def exp_map_zero(v, c):
            sc = jnp.sqrt(c)
            n = _norm(v)
            return jnp.tanh(sc * n) * v / (sc * n)

        def project_to_ball(x, c):
            n = _norm(x)
            maxn = (1.0 - BALL_EPS) / jnp.sqrt(c)
            return jnp.where(n > maxn, x * (maxn / n), x)

        def mobius_add(x, y, c):
            x2 = jnp.sum(x * x, axis=-1, keepdims=True)
            y2 = jnp.sum(y * y, axis=-1, keepdims=True)
            xy = jnp.sum(x * y, axis=-1, keepdims=True)
            num = (1.0 + 2.0 * c * xy + c * y2) * x + (1.0 - c * x2) * y
            den = 1.0 + 2.0 * c * xy + c * c * x2 * y2
            return num / jnp.clip(den, MIN_NORM)
        N, E, R, D = (50000, 12500, 230, 16)
        key = jax.random.key(seed)
        ks = jax.random.split(key, 8)
        h_hyper = project_to_ball(0.1 * jax.random.normal(ks[0], (N, D), dtype=jnp.float32), C)
        node_norm = jax.random.uniform(ks[1], (N, 1), dtype=jnp.float32)
        xav = float(np.sqrt(2.0 / (D + D)))
        rel_weight = xav * jax.random.normal(ks[2], (R, D, D), dtype=jnp.float32)
        loop_weight = xav * jax.random.normal(ks[3], (D, D), dtype=jnp.float32)
        rel_emb = 0.1 * jax.random.normal(ks[4], (R, D), dtype=jnp.float32)
        src = jax.random.randint(ks[5], (E,), 0, N, dtype=jnp.int32)
        dst = jax.random.randint(ks[6], (E,), 0, N, dtype=jnp.int32)
        etype = jax.random.randint(ks[7], (E,), 0, R, dtype=jnp.int32)
        return {'h_hyper': h_hyper, 'node_norm': node_norm, 'rel_weight': rel_weight, 'loop_weight': loop_weight, 'rel_emb': rel_emb, 'src': src, 'dst': dst, 'etype': etype}
    _L2_gnn_all = _L2_gnn_setup()
    _L2_gnn_in = {k: v for k, v in _L2_gnn_all.items() if k in ('rel_weight', 'loop_weight', 'rel_emb')}
    del _L2_gnn_all

    def _L3_gnn_setup():
        import jax, jax.numpy as jnp
        import numpy as np
        STALK_DIM = 16
        N_NODES = 50000
        N_EDGES = 12500
        HIDDEN = 64
        key = jax.random.key(seed)
        k1, k2, k3, k4 = jax.random.split(key, 4)
        d = STALK_DIM
        x = jax.random.normal(k1, (N_NODES, d), dtype=jnp.float32)
        edge_index = jax.random.randint(k2, (2, N_EDGES), 0, N_NODES, dtype=jnp.int64)
        W1 = jax.random.normal(k3, (HIDDEN, 2 * d), dtype=jnp.float32) * (1.0 / np.sqrt(2 * d))
        b1 = jnp.zeros((HIDDEN,), dtype=jnp.float32)
        W2 = jax.random.normal(k4, (d, HIDDEN), dtype=jnp.float32) * (1.0 / np.sqrt(HIDDEN))
        b2 = jnp.zeros((d,), dtype=jnp.float32)
        return {'x': x, 'edge_index': edge_index, 'W1': W1, 'b1': b1, 'W2': W2, 'b2': b2}
    _L3_gnn_all = _L3_gnn_setup()
    _L3_gnn_in = {k: v for k, v in _L3_gnn_all.items() if k in ('W1', 'b1', 'W2', 'b2')}
    del _L3_gnn_all
    return {'x': x, 'src': src, 'dst': dst, 'edge_attr_8': edge_attr_8, 'edge_type_230': edge_type_230, 'edge_type_8': edge_type_8, 'node_vec1': node_vec1, 'L0_gnn_W1': _L0_gnn_in['W1'], 'L0_gnn_root1': _L0_gnn_in['root1'], 'L0_gnn_b1': _L0_gnn_in['b1'], 'L0_gnn_W2': _L0_gnn_in['W2'], 'L0_gnn_root2': _L0_gnn_in['root2'], 'L0_gnn_b2': _L0_gnn_in['b2'], 'L1_gnn_W_msg_tp': _L1_gnn_in['W_msg_tp'], 'L1_gnn_W_msg_lin': _L1_gnn_in['W_msg_lin'], 'L1_gnn_W_upd_tp': _L1_gnn_in['W_upd_tp'], 'L1_gnn_W_upd_lin': _L1_gnn_in['W_upd_lin'], 'L2_gnn_rel_weight': _L2_gnn_in['rel_weight'], 'L2_gnn_loop_weight': _L2_gnn_in['loop_weight'], 'L2_gnn_rel_emb': _L2_gnn_in['rel_emb'], 'L3_gnn_W1': _L3_gnn_in['W1'], 'L3_gnn_b1': _L3_gnn_in['b1'], 'L3_gnn_W2': _L3_gnn_in['W2'], 'L3_gnn_b2': _L3_gnn_in['b2']}

def reference(x, src, dst, edge_attr_8, edge_type_230, edge_type_8, node_vec1, L0_gnn_W1, L0_gnn_root1, L0_gnn_b1, L0_gnn_W2, L0_gnn_root2, L0_gnn_b2, L1_gnn_W_msg_tp, L1_gnn_W_msg_lin, L1_gnn_W_upd_tp, L1_gnn_W_upd_lin, L2_gnn_rel_weight, L2_gnn_loop_weight, L2_gnn_rel_emb, L3_gnn_W1, L3_gnn_b1, L3_gnn_W2, L3_gnn_b2):
    import jax
    import jax.numpy as jnp

    def _L0_gnn_ref(embed, W1, root1, b1, W2, root2, b2, edge_index, edge_type):
        import jax, jax.numpy as jnp
        import numpy as np
        NUM_ENTITIES = 3125
        NUM_RELATIONS = 8
        NUM_CLASSES = 16
        HIDDEN = 16
        NUM_EDGES = 100000

        def rgcn_conv(x, src, dst, edge_type, W, root, bias):
            num_nodes = x.shape[0]
            x_src = x[src]
            msg = jnp.zeros((src.shape[0], W.shape[2]), x.dtype)
            for r in range(NUM_RELATIONS):
                msg = msg + jnp.where((edge_type == r)[:, None], x_src @ W[r], jnp.zeros((), x.dtype))
            cnt = jnp.zeros((num_nodes, NUM_RELATIONS), x.dtype).at[dst, edge_type].add(1.0)
            norm = 1.0 / jnp.maximum(cnt[dst, edge_type], 1.0)
            agg = jax.ops.segment_sum(msg * norm[:, None], dst, num_segments=num_nodes)
            return agg + x @ root + bias
        src, dst = (edge_index[0], edge_index[1])
        h = rgcn_conv(embed, src, dst, edge_type, W1, root1, b1)
        h = jax.nn.relu(h)
        h = rgcn_conv(h, src, dst, edge_type, W2, root2, b2)
        return jax.nn.log_softmax(h, axis=1)

    def _L1_gnn_ref(node_features, edge_attr_e3nn, node_attr_scalar_raw, W_msg_tp, W_msg_lin, W_upd_tp, W_upd_lin, edge_index):
        import jax, jax.numpy as jnp
        import numpy as np
        N_NODES = 3125
        N_EDGES = 100000
        D_NODE = 16
        D_EDGE = 8
        D_HIDDEN = 16
        n_nodes = node_features.shape[0]
        row = edge_index[0]
        col = edge_index[1]
        norm_msg_tp = 1.0 / np.float32(np.sqrt(D_NODE * D_EDGE))
        norm_upd_tp = 1.0 / np.float32(np.sqrt(D_NODE * D_HIDDEN))
        norm_lin = 1.0 / np.float32(np.sqrt(D_HIDDEN))
        x_j = node_features[col]
        m = jnp.einsum('ei,ej,ijh->eh', x_j, edge_attr_e3nn, W_msg_tp) * norm_msg_tp
        m = jax.nn.silu(m)
        m = m @ W_msg_lin * norm_lin
        agg = jax.ops.segment_sum(m, row, num_segments=n_nodes)
        u = jnp.einsum('ni,nh,ihk->nk', node_features, agg, W_upd_tp) * norm_upd_tp
        u = jax.nn.silu(u)
        u = u @ W_upd_lin * norm_lin
        return node_features + u

    def _L2_gnn_ref(h_hyper, node_norm, rel_weight, loop_weight, rel_emb, src, dst, etype):
        import jax, jax.numpy as jnp
        import numpy as np
        C = 0.01
        EPS = 1e-06
        MIN_NORM = 1e-10
        BALL_EPS = 1e-05

        def _norm(x):
            return jnp.sqrt(jnp.clip(jnp.sum(x * x, axis=-1, keepdims=True), MIN_NORM))

        def log_map_zero(x, c):
            sc = jnp.sqrt(c)
            n = _norm(x)
            return jnp.arctanh(jnp.clip(sc * n, -1.0 + BALL_EPS, 1.0 - BALL_EPS)) * x / (sc * n)

        def exp_map_zero(v, c):
            sc = jnp.sqrt(c)
            n = _norm(v)
            return jnp.tanh(sc * n) * v / (sc * n)

        def project_to_ball(x, c):
            n = _norm(x)
            maxn = (1.0 - BALL_EPS) / jnp.sqrt(c)
            return jnp.where(n > maxn, x * (maxn / n), x)

        def mobius_add(x, y, c):
            x2 = jnp.sum(x * x, axis=-1, keepdims=True)
            y2 = jnp.sum(y * y, axis=-1, keepdims=True)
            xy = jnp.sum(x * y, axis=-1, keepdims=True)
            num = (1.0 + 2.0 * c * xy + c * y2) * x + (1.0 - c * x2) * y
            den = 1.0 + 2.0 * c * xy + c * c * x2 * y2
            return num / jnp.clip(den, MIN_NORM)
        c = C
        N = h_hyper.shape[0]
        h_tan = log_map_zero(h_hyper, c)
        msg_tan = jnp.einsum('ei,eio->eo', h_tan[src], rel_weight[etype])
        msg_tan = msg_tan + rel_emb[etype]
        msg = exp_map_zero(msg_tan, c)
        en = node_norm[dst, 0]
        norm_sum = jax.ops.segment_sum(en, dst, num_segments=N)
        w = en / (norm_sum[dst] + EPS)
        lam = 2.0 / (1.0 - c * jnp.sum(msg * msg, axis=-1) + EPS)
        wl = w * lam
        numer = jax.ops.segment_sum(wl[:, None] * msg, dst, num_segments=N)
        denom = jax.ops.segment_sum(wl, dst, num_segments=N) + EPS
        h_agg = project_to_ball(numer / denom[:, None], c)
        loop_hyp = exp_map_zero(h_tan @ loop_weight, c)
        h_new = mobius_add(h_agg, loop_hyp, c)
        return h_new

    def _L3_gnn_ref(x, edge_index, W1, b1, W2, b2):
        import jax, jax.numpy as jnp
        import numpy as np
        STALK_DIM = 16
        N_NODES = 50000
        N_EDGES = 12500
        HIDDEN = 64
        d = x.shape[1]
        n = x.shape[0]
        src, dst = (edge_index[0], edge_index[1])
        xs, xd = (x[src], x[dst])

        def reflection(a, b):
            h = jax.nn.relu(jnp.concatenate([a, b], axis=1) @ W1.T + b1)
            return h @ W2.T + b2

        def householder(v):
            vn = v / jnp.maximum(jnp.linalg.norm(v, axis=1, keepdims=True), 1e-12)
            return jnp.eye(d, dtype=v.dtype)[None] - 2.0 * vn[:, :, None] * vn[:, None, :]
        F_s = householder(reflection(xs, xd))
        F_d = householder(reflection(xd, xs))
        L_sd = -jnp.einsum('eki,ekj->eij', F_s, F_d)
        ones_e = jnp.ones(src.shape[0], dtype=x.dtype)
        deg = jnp.zeros(n, dtype=x.dtype).at[src].add(ones_e).at[dst].add(ones_e)
        deg_inv_sqrt = 1.0 / jnp.sqrt(jnp.maximum(deg, 1e-05))
        coef = deg_inv_sqrt[src] * deg_inv_sqrt[dst]
        msg_s = coef[:, None] * jnp.einsum('eij,ej->ei', L_sd, xd)
        msg_d = coef[:, None] * jnp.einsum('eji,ej->ei', L_sd, xs)
        out = x - jnp.zeros_like(x).at[src].add(msg_s) - jnp.zeros_like(x).at[dst].add(msg_d)
        return jax.nn.relu(out)
    edge_index = jnp.stack([src, dst])
    deg = jnp.maximum(jax.ops.segment_sum(jnp.ones(dst.shape, jnp.float32), dst, num_segments=3125), 1.0)
    deg_isqrt = deg ** (-0.5)
    h = jnp.maximum(_layernorm(x, axis=-1), 0.0)
    x = x + _L0_gnn_ref(h, L0_gnn_W1, L0_gnn_root1, L0_gnn_b1, L0_gnn_W2, L0_gnn_root2, L0_gnn_b2, edge_index, edge_type_8)
    h = jnp.maximum(_layernorm(x, axis=-1), 0.0)
    x = x + _L1_gnn_ref(h, edge_attr_8, node_vec1, L1_gnn_W_msg_tp, L1_gnn_W_msg_lin, L1_gnn_W_upd_tp, L1_gnn_W_upd_lin, edge_index)
    h = jnp.maximum(_layernorm(x, axis=-1), 0.0)
    x = x + _L2_gnn_ref(h, deg_isqrt[:, None], L2_gnn_rel_weight, L2_gnn_loop_weight, L2_gnn_rel_emb, src, dst, edge_type_230)
    h = jnp.maximum(_layernorm(x, axis=-1), 0.0)
    x = x + _L3_gnn_ref(h, edge_index, L3_gnn_W1, L3_gnn_b1, L3_gnn_W2, L3_gnn_b2)
    return x

_drawn_inputs = setup_inputs


def setup_inputs(seed=0):
    import zlib

    import numpy as np

    out = dict(_drawn_inputs(seed))
    spreads = {'L0_gnn_b1': (0.0, 0.1),
     'L0_gnn_b2': (0.0, 0.1),
     'L3_gnn_b1': (0.0, 2.0),
     'L3_gnn_b2': (0.0, 2.0)}
    factors = {'L2_gnn_rel_emb': 8.0, 'L3_gnn_W1': 4.143, 'L3_gnn_W2': 3.577}
    for name, (base, spread) in spreads.items():
        noise = np.random.default_rng([zlib.crc32(name.encode()), seed]).standard_normal(out[name].shape)
        drawn = base * np.exp(spread * noise) if base else spread * noise
        out[name] = jnp.asarray(drawn.astype(out[name].dtype))
    for name, factor in factors.items():
        out[name] = (out[name] * factor).astype(out[name].dtype)
    return out
```

```python
import concourse.bass as bass
from concourse import mybir
from contextlib import ExitStack
import numpy as np

N, E, D = 3125, 100000, 16
P = 128
T = 784
G = 14
SLOTS = 2
GROUPS = T // G
ITERS = GROUPS // SLOTS
FULL = E // T
REST = E - FULL * T
NP_, NJ = 98, 32
NPAD = NP_ * NJ
NLAST = N - (NJ - 1) * NP_
REL, TYPES, DE, HID = 8, 230, 8, 64
Q8, R8 = 8, 392
Q7, R7 = 7, 448
CHUNK8, CHUNK7 = R8 // 4, R7 // 4
RC = 196
CQ = NPAD // RC
W5 = 2 * HID + D + 1
EC = 8
ECOLS = TYPES * D // EC
PAD_KEY = -1000.0
BIG = 2 * TYPES * D
RING = 7


def gnn(nc, x, src, dst, ea, t230, t8, cW1, croot1, cb1, cW2, croot2, cb2,
        mtp, mlin, utp, ulin, relw, loopw, relemb, sW1, sb1, sW2, sb2, out):
    f32, i32, bf16, f16 = mybir.dt.float32, mybir.dt.int32, mybir.dt.bfloat16, mybir.dt.float16
    ALU, ACT, AX = mybir.AluOpType, mybir.ActivationFunctionType, mybir.AxisListType.X

    with ExitStack() as ctx:
        def sb(name, shape, dt=f32):
            return ctx.enter_context(nc.sbuf_tensor(name, shape, dt))

        def dram(name, shape):
            return nc.dram_tensor(name, shape, f32).ap()

        def sem(name):
            return ctx.enter_context(nc.semaphore(name))

        tabs = {"c1": dram("tab_c1", (NPAD * REL, D)), "c2": dram("tab_c2", (NPAD * REL, D)),
                "l1": dram("tab_l1", (NPAD, DE * D)), "l2": dram("tab_l2", (NPAD * TYPES, D)),
                "l3": dram("tab_l3", (NPAD, W5)), "norm": dram("tab_norm", (REL * NPAD, 1))}
        relay = {"l1": dram("relay_l1", (NPAD, D + 1)), "l2": dram("relay_l2", (NPAD, D + 2))}

        ident = sb("ident", [P, P])
        iota_r = sb("iota_r", [P, R7])
        iota_q = sb("iota_q", [P, Q8])
        zeros = sb("zeros", [P, R7], bf16)
        src_i, dst_i = sb("src_i", [P, T], i32), sb("dst_i", [P, T], i32)
        rel_row = sb("rel_row", [P, T], i32)
        norm_row = sb("norm_row", [P, T], i32)
        type_row = sb("type_row", [P, T], i32)
        ea_sb = sb("ea_sb", [P, T, DE])
        norm_sb = sb("norm_sb", [P, T])
        keys = {k: sb("key_" + k, [P, GROUPS, 2, G], f16) for k in ("cnt", "dst8", "dst7", "src7", "src8")}
        idx = [sb(f"idx{s}", [P, 2, G], i32) for s in range(SLOTS)]
        kf = [sb(f"kf{s}", [P, 4, G]) for s in range(SLOTS)]
        ga = [sb(f"ga{s}", [P, G, W5]) for s in range(SLOTS)]
        gb = [sb(f"gb{s}", [P, G, W5]) for s in range(SLOTS)]
        msg = [sb(f"msg{s}", [P, 2, G, D + 2]) for s in range(SLOTS)]
        sq = sb("sq", [P, G, D])
        sg = [sb(f"sg{s}", [P, G, D]) for s in range(SLOTS)]
        sm = [sb(f"sm{s}", [P, 8, G]) for s in range(SLOTS)]
        ea_flat = ea_sb[:, :, :].rearrange("p t j -> p (t j)")
        hid = ea_flat[:, 0:G * 2 * HID].rearrange("p (g c) -> p g c", g=G)
        hidT = ea_flat[:, G * 2 * HID:G * 2 * HID + 8 * P].rearrange("p (a g e) -> p a g e", a=2, g=4)
        S = sb("S", [P, RING, P])
        O = sb("O", [P, RING, R7])
        Sc = S[:, :, :].rearrange("p g c -> p (g c)").bitcast(bf16).rearrange("p (g c) -> p g c", g=RING)
        Oc = O[:, :, :].rearrange("p g c -> p (g c)").bitcast(bf16).rearrange("p (g c) -> p g c", g=RING)
        big = sb("big", [P, BIG])
        X, H17, HT = sb("X", [NP_, NJ, D]), sb("H17", [NP_, NJ, D + 1]), sb("HT", [NP_, NJ, D + 1])
        A, B, C_, V = (sb(n, [NP_, NJ, D]) for n in ("A", "B", "C_", "V"))
        AGR = sb("AGR", [NP_, NJ, D + 2])
        degs = sb("degs", [NP_, NJ])
        n1, n2, n3, n4, n5, n6 = (sb(f"n{k}", [NP_, NJ]) for k in range(1, 7))
        AG = sb("AG", [P, R7])
        AGT = sb("AGT", [CHUNK7, 4 * Q7, D + 2])
        XT = sb("XT", [D + 1, NPAD + NP_])
        XTj = sb("XTj", [D + 1, 2, NP_])
        prod = sb("prod", [NP_, 2, D * D])
        wc = [sb(f"wc{k}", [D + 1, REL * D + D]) for k in range(2)]
        wl1 = sb("wl1", [D + 1, DE * D])
        wupd = sb("wupd", [D + 1, D * D])
        wlin, wulin, wloop = (sb(n, [D + 1, D]) for n in ("wlin", "wulin", "wloop"))
        wrel = sb("wrel", [D + 1, TYPES * D])
        wpq = sb("wpq", [D + 1, 2 * HID])
        w2 = sb("w2", [P, 2 * D])
        b2 = sb("b2", [P, D])

        agg = ctx.enter_context(nc.psum_tensor("agg", [P, 512], f32))
        psT = [ctx.enter_context(nc.psum_tensor(f"psT{k}", [P, 512], f32)) for k in range(2)]
        psM = [ctx.enter_context(nc.psum_tensor(f"psM{k}", [P, 512], f32)) for k in range(4)]
        psV = ctx.enter_context(nc.psum_tensor("psV", [P, 512], f32))

        LAYERS = ("c1", "c2", "l1", "l2", "l3")
        consts_made, ident_made = sem("consts_made"), sem("ident_made")
        zeroed, edges_in, ea_in, weights_in, x_in = (sem(n) for n in ("zeroed", "edges_in", "ea_in", "weights_in", "x_in"))
        dve_step = sem("dve_step")
        keys_made = sem("keys_made")
        cnt_keys, cnt_free, cnt_ready, cnt_done, norm_made, norm_out = (sem(n) for n in (
            "cnt_keys", "cnt_free", "cnt_ready", "cnt_done", "norm_made", "norm_out"))
        cnt_used = [sem(f"cnt_used{s}") for s in range(SLOTS)]
        xt_in, xt_ps, xt_sb, proj_ps, proj_sb, table_made, table_out = ({L: sem(f"{n}_{L}") for L in LAYERS} for n in (
            "xt_in", "xt_ps", "xt_sb", "proj_ps", "proj_sb", "table_made", "table_out"))
        idx_set, gathered, key_set, key_used = ({(L, s): sem(f"{n}_{L}{s}") for L in LAYERS for s in range(SLOTS)} for n in (
            "idx_set", "gathered", "key_set", "key_used"))
        tile_free, tile_ready, agg_done, agg_sb, aggT = ({L: sem(f"{n}_{L}") for L in LAYERS} for n in (
            "tile_free", "tile_ready", "agg_done", "agg_sb", "aggT"))
        var_made, std_made = sem("var_made"), sem("std_made")
        act_in, act_out = sem("act_in"), sem("act_out")
        relay_made, relay_out, relay_in = sem("relay_made"), sem("relay_out"), sem("relay_in")
        lin_in, lin_ps, lin_sb, lin_mm, lin_read = (sem(n) for n in ("lin_in", "lin_ps", "lin_sb", "lin_mm", "lin_read"))
        upd_ps, upd_read = sem("upd_ps"), sem("upd_read")
        xtj_set, rel_ps, rel_act, rel_dve = (sem(n) for n in ("xtj_set", "rel_ps", "rel_act", "rel_dve"))
        row_free = [sem(f"row_free{h}") for h in range(2)]
        rel_row_out = [sem(f"rel_row_out{h}") for h in range(2)]
        m_made, sig_made, sq_made, tanh_made = (sem(n) for n in ("m_made", "sig_made", "sq_made", "tanh_made"))
        hid_made, hidT_ps, hidT_sb, v_ps, v_read = (sem(n) for n in ("hid_made", "hidT_ps", "hidT_sb", "v_ps", "v_read"))
        gathers_begun = sem("gathers_begun")
        x_made, x_out = sem("x_made"), sem("x_out")

        block = ctx.enter_context(nc.Block())

        def nodes(dr):
            return (dr[0:(NJ - 1) * NP_, :].rearrange("(j p) d -> p j d", p=NP_), dr[(NJ - 1) * NP_:N, :])

        SCATTER = {"c1": (Q8, R8, D, 1), "c2": (Q8, R8, D, 1), "l1": (Q7, R7, D + 1, 1),
                   "l2": (Q7, R7, D + 2, 1), "l3": (Q8, R8, D, 2)}

        def relay_out_and_in(sp, L, nth):
            d = SCATTER[L][2]
            sp.wait_ge(relay_made, nth)
            sp.dma_start(relay[L].rearrange("(j p) d -> p j d", p=CHUNK7), AGT[:, :, 0:d]).then_inc(relay_out, 16)
            sp.wait_ge(relay_out, 16 * nth)
            sp.dma_start(AGR[:, :, 0:d], relay[L].rearrange("(j p) d -> p j d", p=NP_)).then_inc(relay_in, 16)

        @block.sync
        def _(sp):
            sp.wait_ge(zeroed, 1)
            for tile, dr in ((src_i, src), (dst_i, dst), (rel_row, t8), (type_row, t230)):
                for a, b in ((0, 112), (112, FULL)):
                    sp.dma_start(tile[a:b, :], dr[a * T:b * T].rearrange("(p t) -> p t", t=T)).then_inc(edges_in, 16)
                sp.dma_start(tile[FULL:FULL + 1, 0:REST], dr[FULL * T:E].rearrange("(p t) -> p t", p=1)).then_inc(edges_in, 16)
            full, last = nodes(x)
            sp.dma_start(X[:, 0:NJ - 1, :], full).then_inc(x_in, 16)
            sp.dma_start(X[0:NLAST, NJ - 1, :], last).then_inc(x_in, 16)
            for a, b in ((0, 112), (112, FULL)):
                sp.dma_start(ea_sb[a:b, :, :], ea[a * T:b * T, :].rearrange("(p t) d -> p t d", t=T)).then_inc(ea_in, 16)
            sp.dma_start(ea_sb[FULL:FULL + 1, 0:REST, :], ea[FULL * T:E, :].rearrange("(p t) d -> p t d", p=1)).then_inc(ea_in, 16)
            sp.wait_ge(norm_made, 1)
            sp.dma_start(tabs["norm"].rearrange("(q r) a -> q (r a)", r=RC), big[:, 0:RC]).then_inc(norm_out, 16)
            for L, cols, pitch in (("c1", REL * D, REL * D + D), ("c2", REL * D, REL * D + D), ("l1", DE * D, DE * D), ("l3", W5, W5)):
                if L == "l3":
                    relay_out_and_in(sp, "l2", 2)
                sp.wait_ge(table_made[L], 1)
                view = tabs[L] if L in ("l1", "l3") else tabs[L].rearrange("(n r) d -> n (r d)", r=REL)
                rows = big[0:NP_, 0:NJ * pitch].rearrange("p (j c) -> p j c", j=NJ)[:, :, 0:cols]
                sp.dma_start(view.rearrange("(j p) c -> p j c", p=NP_), rows).then_inc(table_out[L], 16)
                if L == "l1":
                    relay_out_and_in(sp, "l1", 1)
                    wide = tabs["l2"].rearrange("(j p t) d -> j p (t d)", p=NP_, t=TYPES)
                    for h in range(2):
                        sp.sem_inc(row_free[h], 1)
                    with sp.Fori(0, NJ // 2, 1) as i:
                        for h in range(2):
                            sp.wait_ge(rel_act, i * EC + (EC // 2) * (h + 1) + 2)
                            sp.wait_ge(rel_dve, i * EC + (EC // 2) * (h + 1) + 2)
                            sp.dma_start(wide[bass.ds(i * 2 + h, 1), :, :].rearrange("a p c -> p (a c)"),
                                         big[0:NP_, h * TYPES * D:(h + 1) * TYPES * D]).then_inc(rel_row_out[h], 16)
                            sp.wait_ge(rel_row_out[h], i * 16 + 16)
                            sp.sem_inc(row_free[h], 1)
            sp.wait_ge(x_made, 1)
            full, last = nodes(out)
            sp.dma_start(full, X[:, 0:NJ - 1, :]).then_inc(x_out, 16)
            sp.dma_start(last, X[0:NLAST, NJ - 1, :]).then_inc(x_out, 16)
            sp.wait_ge(x_out, 32)

        @block.gpsimd
        def _(pool):
            nc.gpsimd.iota(iota_r[:, :], pattern=[[1, R7]], base=0, channel_multiplier=0,
                           allow_small_or_imprecise_dtypes=True).then_inc(consts_made, 1)
            nc.gpsimd.iota(iota_q[:, :], pattern=[[1, Q8]], base=0, channel_multiplier=0,
                           allow_small_or_imprecise_dtypes=True).then_inc(consts_made, 1)
            nc.gpsimd.iota(norm_row[:, :], pattern=[[1, T]], base=0, channel_multiplier=T).then_inc(consts_made, 1)
            nc.gpsimd.memset(ident[:, :], 0.0).then_inc(ident_made, 1)
            pool.wait_ge(ident_made, 1)
            nc.gpsimd.affine_select(out=ident[:, :], in_=ident[:, :], compare_op=ALU.not_equal, fill=1.0, base=0,
                                    pattern=[[-1, P]], channel_multiplier=1).then_inc(ident_made, 1)
            pool.wait_ge(keys_made, 1)
            for L, rows, cols in (("c1", (rel_row, norm_row), (D, 1)), ("c2", (rel_row,), (D,)), ("l1", (dst_i,), (DE * D,)),
                                  ("l2", (type_row,), (D,)), ("l3", (src_i, dst_i), (W5, W5))):
                if L == "l2":
                    for h in range(2):
                        pool.wait_ge(rel_row_out[h], 16 * NJ // 2)
                else:
                    pool.wait_ge(table_out[L], 16)
                if L == "c1":
                    pool.wait_ge(norm_out, 16)
                table = {"c1": (tabs["c1"], tabs["norm"]), "l3": (tabs["l3"], tabs["l3"])}.get(L, (tabs[L],))
                with pool.Fori(0, ITERS, 1) as i:
                    for s in range(SLOTS):
                        pool.wait_ge(key_used[L, s], i + 1)
                        for k, r in enumerate(rows):
                            nc.gpsimd.tensor_copy(idx[s][:, k, :], r[:, bass.ds(i * (SLOTS * G) + s * G, G)]).then_inc(idx_set[L, s], 1)
                        pool.wait_ge(idx_set[L, s], i * len(rows) + len(rows))
                        pool.sem_inc(gathers_begun, 1)
                        for k in range(len(rows)):
                            to = (ga, gb)[k][s]
                            for g in range(G):
                                pool.indirect_dma_start(
                                    out=to[:, g, 0:cols[k]], out_offset=None, in_=table[k],
                                    in_offset=bass.IndirectOffsetOnAxis(ap=idx[s][:, k, g:g + 1], axis=0)).then_inc(gathered[L, s], 16)

        act_calls, lin_calls = [0], [0]

        def node_functions(act, L, where):
            for fn, o, a, scale in NODE_FUNCS.get((L, where), ()):
                if fn == "T":
                    for k in range(NJ // 4):
                        lin_calls[0] += 1
                        act.wait_ge(lin_ps, lin_calls[0])
                        nc.scalar.copy(XT[:, k * 4 * NP_:(k + 1) * 4 * NP_], psT[k % 2][0:D + 1, 0:4 * NP_]).then_inc(lin_sb, 1)
                    continue
                act_calls[0] += 1
                act.wait_ge(act_in, act_calls[0])
                t = {"n1": n1[:, :], "n2": n2[:, :], "n3": n3[:, :], "B": B[:, :, :], "C": C_[:, :, :]}
                nc.scalar.activation(t[o], t[a], fn, scale=scale).then_inc(act_out, 1)

        @block.scalar
        def _(act):
            act.wait_ge(zeroed, 2)
            for k, (W, root, b) in enumerate(((cW1, croot1, cb1), (cW2, croot2, cb2))):
                act.dma_start(wc[k][0:D, 0:REL * D].rearrange("i (r o) -> i r o", r=REL), W.rearrange("r i o -> i r o")).then_inc(weights_in, 16)
                act.dma_start(wc[k][0:D, REL * D:], root).then_inc(weights_in, 16)
                act.dma_start(wc[k][D:D + 1, REL * D:], b.rearrange("(a n) -> a n", a=1)).then_inc(weights_in, 16)
            act.dma_start(wl1[0:D, :], mtp.rearrange("i j h -> i (j h)")).then_inc(weights_in, 16)
            act.dma_start(wupd[0:D, :], utp.rearrange("i h k -> i (h k)")).then_inc(weights_in, 16)
            for w, dr in ((wlin, mlin), (wulin, ulin), (wloop, loopw)):
                act.dma_start(w[0:D, :], dr).then_inc(weights_in, 16)
            act.dma_start(wrel[0:D, :].rearrange("i (t o) -> i t o", t=TYPES), relw.rearrange("t i o -> i t o")).then_inc(weights_in, 16)
            act.dma_start(wrel[D:D + 1, :], relemb.rearrange("(a t) o -> a (t o)", a=1)).then_inc(weights_in, 16)
            for k in range(2):
                act.dma_start(wpq[0:D, k * HID:(k + 1) * HID], sW1[k * D:(k + 1) * D, :]).then_inc(weights_in, 16)
                act.dma_start(w2[k * HID:(k + 1) * HID, k * D:(k + 1) * D], sW2).then_inc(weights_in, 16)
            act.dma_start(wpq[D:D + 1, HID:], sb1.rearrange("(a n) -> a n", a=1)).then_inc(weights_in, 16)
            act.dma_start(b2[:, :], sb2.rearrange("(a n) -> a n", a=1).broadcast_to([P, D])).then_inc(weights_in, 16)

            act.wait_ge(keys_made, 1)
            with act.Fori(0, ITERS, 1) as i:
                for s in range(SLOTS):
                    act.wait_ge(cnt_used[s], i + 1)
                    nc.scalar.copy(kf[s][:, 0:2, :], keys["cnt"][:, bass.ds(i * SLOTS + s, 1), :, :].rearrange("p a k g -> p (a k) g")).then_inc(cnt_keys, 1)

            nth_std = 0
            for L in LAYERS:
                if L != "c2":
                    nth_std += 1
                    act.wait_ge(var_made, nth_std)
                    nc.scalar.activation(n2[:, :], n1[:, :], ACT.Sqrt).then_inc(std_made, 1)
                node_functions(act, L, "start")
                for k in range(NJ // 4):
                    act.wait_ge(xt_ps[L], k + 1)
                    nc.scalar.copy(XT[:, k * 4 * NP_:(k + 1) * 4 * NP_], psT[k % 2][0:D + 1, 0:4 * NP_]).then_inc(xt_sb[L], 1)
                if L != "l2":
                    cols, per = PROJ[L]
                    for k in range(-(-NJ // per)):
                        m = min(per, NJ - k * per)
                        act.wait_ge(proj_ps[L], k + 1)
                        pitch = W5 if L == "l3" else cols
                        rows = big[0:NP_, 0:NJ * pitch].rearrange("p (j c) -> p j c", j=NJ)
                        nc.scalar.copy(rows[:, k * per:k * per + m, 0:cols],
                                       psM[k % 4][0:NP_, 0:m * cols].rearrange("p (j c) -> p j c", j=m)).then_inc(proj_sb[L], 1)
                else:
                    act.sem_inc(rel_act, 2)
                    nc.scalar.copy(XTj[:, 0, :], XT[:, 0:NP_]).then_inc(xtj_set, 1)
                    with act.Fori(0, NJ // 2, 1) as i:
                        for h in range(2):
                            act.wait_ge(row_free[h], i + 1)
                            for c in range(0, EC, 2):
                                act.wait_ge(rel_ps, i * (2 * EC) + h * EC + c + 1)
                                nc.scalar.copy(big[0:NP_, (h * EC + c) * ECOLS:(h * EC + c + 1) * ECOLS], psM[c % 4][0:NP_, 0:ECOLS]).then_inc(rel_act, 1)
                                if c == 0:
                                    nc.scalar.copy(XTj[:, 1 - h, :], XT[:, bass.ds(i * (2 * NP_) + (h + 1) * NP_, NP_)]).then_inc(xtj_set, 1)
                node_functions(act, L, "table")
                q, r, d, per_edge = SCATTER[L]
                names = {"c1": ("dst8",), "c2": ("dst8",), "l1": ("src7",), "l2": ("dst7",), "l3": ("src8", "dst8")}[L]
                with act.Fori(0, ITERS, 1) as i:
                    for s in range(SLOTS):
                        k = i * SLOTS + s
                        act.wait_ge(key_used[L, s], i + 1)
                        for a, name in enumerate(names):
                            nc.scalar.copy(kf[s][:, 2 * a:2 * a + 2, :], keys[name][:, bass.ds(k, 1), :, :].rearrange("p a k g -> p (a k) g")).then_inc(key_set[L, s], 1)
                        if L == "l1":
                            act.wait_ge(m_made, k + 1)
                            nc.scalar.activation(sg[s][:, :, :], sq[:, :, :], ACT.Sigmoid, scale=NORM_MSG).then_inc(sig_made, 1)
                        if L == "l2":
                            act.wait_ge(sq_made, k + 1)
                            nc.scalar.activation(sm[s][:, 2, :], sm[s][:, 1, :], ACT.Sqrt).then_inc(tanh_made, 1)
                            act.wait_ge(tanh_made, k * 2 + 1)
                            nc.scalar.activation(sm[s][:, 3, :], sm[s][:, 2, :], ACT.Tanh, scale=SC).then_inc(tanh_made, 1)
                        if L == "l3":
                            for c in range(4):
                                m = min(4, G - 4 * c)
                                act.wait_ge(hidT_ps, k * 4 + c + 1)
                                nc.scalar.activation(hidT[:, c % 2, 0:m, :], psT[c % 2][:, 0:m * P].rearrange("p (g e) -> p g e", g=m), ACT.Relu).then_inc(hidT_sb, 1)
                act.wait_ge(agg_done[L], 1)
                nc.scalar.copy(AG[0:q * d, 0:r], agg[0:q * d, 0:r]).then_inc(agg_sb[L], 1)
                node_functions(act, L, "end")

        def second_layer(pe, k, c):
            m = min(4, G - 4 * c)
            pe.wait_ge(hidT_sb, k * 4 + c + 1)
            if c == 0:
                pe.wait_ge(v_read, k + 1)
            for g in range(m):
                last = nc.tensor.matmul(psV[:, (4 * c + g) * 2 * D:(4 * c + g + 1) * 2 * D], hidT[:, c % 2, g, :], w2[:, :], start=True, stop=True)
            last.then_inc(v_ps, 1)

        @block.tensor
        def _(pe):
            pe.wait_ge(zeroed, 2)
            nc.tensor.matmul(agg[:, 0:RC], zeros[:, 0:P], zeros[:, 0:RC], start=True, stop=False, skip_group_check=True).then_inc(cnt_free, RING)
            with pe.Fori(0, ITERS, 1) as i:
                for s in range(SLOTS):
                    for g in range(G):
                        pe.wait_ge(cnt_ready, i * (SLOTS * G * 2) + 2 * (s * G + g + 1))
                        nc.tensor.matmul(agg[:, 0:RC], Sc[:, g % RING, 0:P], Oc[:, g % RING, 0:RC], start=False, stop=False,
                                         skip_group_check=True).then_inc(cnt_free, 1)
            nc.tensor.matmul(agg[:, 0:RC], zeros[:, 0:P], zeros[:, 0:RC], start=False, stop=True, skip_group_check=True).then_inc(cnt_done, 1)
            pe.wait_ge(ident_made, 2)
            pe.wait_ge(weights_in, 16 * WEIGHT_LOADS)

            lin = [0, 0]

            def linear(src17, w):
                pe.wait_ge(lin_in, lin[1] + 1)
                for k in range(NJ // 4):
                    if k >= 2:
                        pe.wait_ge(lin_sb, lin[0] + k - 1)
                    for j in range(4):
                        last = nc.tensor.transpose(psT[k % 2][0:D + 1, j * NP_:(j + 1) * NP_], src17[:, 4 * k + j, 0:D + 1], ident[0:NP_, 0:NP_])
                    last.then_inc(lin_ps, 1)
                pe.wait_ge(lin_sb, lin[0] + NJ // 4)
                for j in range(NJ):
                    last = nc.tensor.matmul(psV[0:NP_, j * D:(j + 1) * D], XT[:, j * NP_:(j + 1) * NP_], w[:, :], start=True, stop=True)
                last.then_inc(lin_mm, 1)
                lin[0] += NJ // 4
                lin[1] += 1

            for L in LAYERS:
                pe.wait_ge(xt_in[L], 1)
                for k in range(NJ // 4):
                    if k >= 2:
                        pe.wait_ge(xt_sb[L], k - 1)
                    for j in range(4):
                        last = nc.tensor.transpose(psT[k % 2][0:D + 1, j * NP_:(j + 1) * NP_],
                                                   (HT if L == "l2" else H17)[:, 4 * k + j, :], ident[0:NP_, 0:NP_])
                    last.then_inc(xt_ps[L], 1)
                pe.wait_ge(xt_sb[L], NJ // 4)
                if L != "l2":
                    cols, per = PROJ[L]
                    w = {"c1": wc[0], "c2": wc[1], "l1": wl1, "l3": wpq}[L]
                    for k in range(-(-NJ // per)):
                        if k >= 4:
                            pe.wait_ge(proj_sb[L], k - 3)
                        for j in range(k * per, min(NJ, (k + 1) * per)):
                            last = nc.tensor.matmul(psM[k % 4][0:NP_, (j % per) * cols:(j % per + 1) * cols],
                                                    XT[:, j * NP_:(j + 1) * NP_], w[:, :], start=True, stop=True)
                        last.then_inc(proj_ps[L], 1)
                else:
                    for j in range(NJ):
                        last = nc.tensor.matmul(psV[0:NP_, j * D:(j + 1) * D], XT[:, j * NP_:(j + 1) * NP_], wloop[:, :], start=True, stop=True)
                    last.then_inc(proj_ps[L], 1)
                    with pe.Fori(0, NJ // 2, 1) as i:
                        for h in range(2):
                            pe.wait_ge(xtj_set, i * 2 + h + 1)
                            for c in range(EC):
                                pe.wait_ge((rel_act, rel_dve)[c % 2], i * EC + h * (EC // 2) + c // 2 + 1)
                                last = nc.tensor.matmul(psM[c % 4][0:NP_, 0:ECOLS], XTj[:, h, :], wrel[:, c * ECOLS:(c + 1) * ECOLS],
                                                        start=True, stop=True)
                                last.then_inc(rel_ps, 1)
                q, r, d, per_edge = SCATTER[L]
                nc.tensor.matmul(agg[0:q * d, 0:r], zeros[:, 0:q * d], zeros[:, 0:r], start=True, stop=False,
                                 skip_group_check=True).then_inc(tile_free[L], RING)
                with pe.Fori(0, ITERS, 1) as i:
                    for s in range(SLOTS):
                        k = i * SLOTS + s
                        if L == "l3":
                            pe.wait_ge(hid_made, k + 1)
                            for c in range(4):
                                m = min(4, G - 4 * c)
                                if c >= 2:
                                    pe.wait_ge(hidT_sb, k * 4 + c - 1)
                                for g in range(m):
                                    last = nc.tensor.transpose(psT[c % 2][:, g * P:(g + 1) * P], hid[:, 4 * c + g, :], ident[:, :])
                                last.then_inc(hidT_ps, 1)
                                if c >= 1:
                                    second_layer(pe, k, c - 1)
                            second_layer(pe, k, 3)
                        for t in range(per_edge * G):
                            pe.wait_ge(tile_ready[L], k * (2 * per_edge * G) + 2 * (t + 1))
                            nc.tensor.matmul(agg[0:q * d, 0:r], S[:, t % RING, 0:q * d], O[:, t % RING, 0:r], start=False, stop=False,
                                             skip_group_check=True).then_inc(tile_free[L], 1)
                nc.tensor.matmul(agg[0:q * d, 0:r], zeros[:, 0:q * d], zeros[:, 0:r], start=False, stop=True,
                                 skip_group_check=True).then_inc(agg_done[L], 1)
                pe.wait_ge(agg_sb[L], 1)
                for c in range(4):
                    last = nc.tensor.transpose(psT[0][0:r // 4, c * q * d:(c + 1) * q * d], AG[0:q * d, c * (r // 4):(c + 1) * (r // 4)],
                                               ident[0:q * d, 0:q * d])
                last.then_inc(aggT[L], 1)
                if L == "l1":
                    linear(HT, wlin)
                    pe.wait_ge(lin_in, lin[1] + 1)
                    for k in range(NJ // 4):
                        if k >= 2:
                            pe.wait_ge(lin_sb, lin[0] + k - 1)
                        for j in range(4):
                            last = nc.tensor.transpose(psT[k % 2][0:D + 1, j * NP_:(j + 1) * NP_], H17[:, 4 * k + j, :], ident[0:NP_, 0:NP_])
                        last.then_inc(lin_ps, 1)
                    pe.wait_ge(lin_sb, lin[0] + NJ // 4)
                    lin[0] += NJ // 4
                    lin[1] += 1
                    for j in range(NJ):
                        if j >= 4:
                            pe.wait_ge(upd_read, j - 3)
                        nc.tensor.matmul(psM[j % 4][0:NP_, 0:D * D], XT[:, j * NP_:(j + 1) * NP_], wupd[:, :], start=True, stop=True).then_inc(upd_ps, 1)
                    linear(HT, wulin)

        def relay_back(dve, v, link, L, nth):
            q, r, d, _ = SCATTER[L]
            dve.wait_ge(aggT[L], 1)
            v.tensor_copy(AGT[:, :, 0:d].rearrange("p (q c) d -> p q c d", q=q),
                          psT[0][0:CHUNK7, 0:4 * q * d].rearrange("p (c q d) -> p q c d", c=4, q=q)).then_inc(relay_made, 1)
            dve.wait_ge(relay_in, 16 * nth)


        @block.vector
        def _(dve):
            v = nc.vector
            step = [0, 0, 0]

            def link(ins):
                ins.then_inc(dve_step, 1)
                step[0] += 1
                dve.wait_ge(dve_step, step[2] + step[0])

            def loop_begin(i, per_round):
                step[1] = step[0]
                step[2] = i * per_round

            def loop_end(per_round):
                assert step[0] - step[1] == per_round, (step, per_round)
                step[0] = step[1] + per_round * ITERS
                step[2] = 0

            def bc(ap2, n, d):
                return ap2.rearrange("p (n a) -> p n a", a=1).broadcast_to([ap2.shape[0], n, d])

            def tt(o, a, b, op):
                link(v.tensor_tensor(o, a, b, op))

            def ts(o, a, s1, op0, s2=None, op1=None):
                link(v.tensor_scalar(o, a, s1, s2, op0, op1) if op1 is not None else v.tensor_scalar(o, a, s1, None, op0))

            def red(o, a, op=ALU.add):
                link(v.tensor_reduce(o, a, axis=AX, op=op))

            for free in list(key_used.values()) + cnt_used:
                dve.sem_inc(free, 1)
            for t in (src_i, dst_i, rel_row, type_row, X):
                link(v.memset(t[tuple(slice(None) for _ in t.shape)], 0))
            link(v.memset(ea_sb[:, :, :], 0.0))
            v.memset(zeros[:, 0:1], 0.0).then_inc(zeroed, 1)
            for t in (wc[0], wc[1], wl1, wupd, wlin, wulin, wloop, wrel, wpq, w2):
                link(v.memset(t[:, :], 0.0))
            link(v.memset(H17[:, :, D:D + 1], 1.0))
            link(v.memset(HT[:, :, :], 1.0))
            link(v.memset(XT[:, NPAD:], 0.0))
            for s in range(SLOTS):
                link(v.memset(msg[s][:, :, :, D:D + 2], 1.0))
            v.memset(zeros[:, :], 0.0).then_inc(zeroed, 1)
            dve.wait_ge(zeroed, 2)

            sf, df, pad, hi, lo, t_f, c16, lo2 = (big[:, k * T:(k + 1) * T] for k in range(8))

            def grp(a):
                return a.rearrange("p (k g) -> p k g", g=G)

            dve.wait_ge(consts_made, 3)
            dve.wait_ge(edges_in, 16 * 12)
            ts(pad, norm_row[:, :], float(E), ALU.is_ge, PAD_KEY, ALU.mult)
            link(v.tensor_copy(sf, src_i[:, :]))
            link(v.tensor_copy(df, dst_i[:, :]))
            link(v.tensor_copy(t_f, rel_row[:, :]))

            def split(val, q, r):
                ts(hi, val, float(r), ALU.is_ge)
                for k in range(2, q):
                    link(v.scalar_tensor_tensor(out=hi, in0=val, scalar=float(k * r), in1=hi, op0=ALU.is_ge, op1=ALU.add))
                link(v.scalar_tensor_tensor(out=lo, in0=hi, scalar=float(-r), in1=val, op0=ALU.mult, op1=ALU.add))

            for name, val, q, r in (("src8", sf, Q8, R8), ("src7", sf, Q7, R7), ("dst7", df, Q7, R7), ("dst8", df, Q8, R8)):
                split(val, q, r)
                link(v.tensor_tensor(keys[name][:, :, 0, :], grp(hi), grp(pad), ALU.add))
                link(v.tensor_copy(keys[name][:, :, 1, :], grp(lo)))
            ts(c16, lo, float(RC), ALU.is_ge)
            link(v.scalar_tensor_tensor(out=lo2, in0=c16, scalar=-float(RC), in1=lo, op0=ALU.mult, op1=ALU.add))
            link(v.tensor_copy(keys["cnt"][:, :, 1, :], grp(lo2)))
            link(v.scalar_tensor_tensor(out=hi, in0=hi, scalar=2.0, in1=c16, op0=ALU.mult, op1=ALU.add))
            link(v.scalar_tensor_tensor(out=hi, in0=t_f, scalar=float(CQ), in1=hi, op0=ALU.mult, op1=ALU.add))
            tt(keys["cnt"][:, :, 0, :], grp(hi), grp(pad), ALU.add)
            link(v.scalar_tensor_tensor(out=norm_row[:, :], in0=t_f, scalar=float(NPAD), in1=df, op0=ALU.mult, op1=ALU.add))
            link(v.scalar_tensor_tensor(out=rel_row[:, :], in0=sf, scalar=float(REL), in1=t_f, op0=ALU.mult, op1=ALU.add))
            link(v.tensor_copy(t_f, type_row[:, :]))
            v.scalar_tensor_tensor(out=type_row[:, :], in0=sf, scalar=float(TYPES), in1=t_f, op0=ALU.mult, op1=ALU.add).then_inc(keys_made, 1)
            dve.wait_ge(keys_made, 1)

            with dve.Fori(0, ITERS, 1) as i:
                for s in range(SLOTS):
                    dve.wait_ge(cnt_keys, i * SLOTS + s + 1)
                    for g in range(G):
                        dve.wait_ge(cnt_free, i * (SLOTS * G) + s * G + g + 1)
                        v.tensor_scalar(Sc[:, g % RING, 0:P], iota_r[:, 0:P], kf[s][:, 0, g:g + 1], None, ALU.is_equal).then_inc(cnt_ready, 1)
                        v.tensor_scalar(Oc[:, g % RING, 0:RC], iota_r[:, 0:RC], kf[s][:, 1, g:g + 1], None, ALU.is_equal).then_inc(cnt_ready, 1)
                    dve.wait_ge(cnt_ready, i * (SLOTS * G * 2) + 2 * (s + 1) * G)
                    dve.sem_inc(cnt_used[s], 1)
            dve.wait_ge(cnt_done, 1)
            ts(big[:, 0:RC], agg[:, 0:RC], 1.0, ALU.max)
            v.reciprocal(big[:, 0:RC], big[:, 0:RC]).then_inc(norm_made, 1)
            dve.wait_ge(norm_made, 1)

            n_std = [0]
            n_act = [0]
            n_lin = [0]

            def relu_layernorm(dest):
                red(n3[:, :], X[:, :, :])
                ts(n3[:, :], n3[:, :], 1.0 / D, ALU.mult)
                tt(A[:, :, :], X[:, :, :], bc(n3[:, :], NJ, D), ALU.subtract)
                tt(B[:, :, :], A[:, :, :], A[:, :, :], ALU.mult)
                red(n4[:, :], B[:, :, :])
                v.tensor_scalar(n1[:, :], n4[:, :], 1.0 / D, 1e-5, ALU.mult, ALU.add).then_inc(var_made, 1)
                n_std[0] += 1
                dve.wait_ge(std_made, n_std[0])
                link(v.reciprocal(n3[:, :], n2[:, :]))
                tt(A[:, :, :], A[:, :, :], bc(n3[:, :], NJ, D), ALU.mult)
                ts(dest, A[:, :, :], 0.0, ALU.max)

            def call_act():
                n_act[0] += 1
                dve.sem_inc(act_in, 1)
                dve.wait_ge(act_out, n_act[0])

            def norm_of(o, val, sq_buf=B):
                tt(sq_buf[:, :, :], val, val, ALU.mult)
                red(o, sq_buf[:, :, :])

            def fill_tiles(L, i, s, a):
                q, r, d, per_edge = SCATTER[L]
                for g in range(G):
                    n = a * G + g
                    dve.wait_ge(tile_free[L], i * (SLOTS * per_edge * G) + (s * per_edge + a) * G + g + 1)
                    v.scalar_tensor_tensor(
                        out=S[:, g % RING, 0:q * d].rearrange("p (q d) -> p q d", q=q), in0=bc(iota_q[:, 0:q], q, d),
                        scalar=kf[s][:, 2 * a, g:g + 1],
                        in1=msg[s][:, a, g, 0:d].rearrange("p (a d) -> p a d", a=1).broadcast_to([P, q, d]),
                        op0=ALU.is_equal, op1=ALU.mult).then_inc(tile_ready[L], 1)
                    v.tensor_scalar(O[:, g % RING, 0:r], iota_r[:, 0:r], kf[s][:, 2 * a + 1, g:g + 1], None,
                                    ALU.is_equal).then_inc(tile_ready[L], 1)
                dve.wait_ge(tile_ready[L], i * (SLOTS * per_edge * G * 2) + (s * per_edge + a + 1) * G * 2)

            def edge_pass(L):
                per_round = SLOTS * {"c1": 2, "c2": 1, "l1": 2, "l2": 10, "l3": 33}[L]
                per_slot_dma = 16 * G * (2 if L in ("c1", "l3") else 1)
                per_key = 2 if L == "l3" else 1
                with dve.Fori(0, ITERS, 1) as i:
                    loop_begin(i, per_round)
                    for s in range(SLOTS):
                        k = i * SLOTS + s
                        here = bass.ds(i * (SLOTS * G) + s * G, G)
                        m = msg[s]
                        dve.wait_ge(gathered[L, s], i * per_slot_dma + per_slot_dma)
                        if L == "c1":
                            link(v.tensor_copy(norm_sb[:, here], gb[s][:, :, 0]))
                            tt(m[:, 0, :, 0:D], ga[s][:, :, 0:D], gb[s][:, :, 0:1].broadcast_to([P, G, D]), ALU.mult)
                        if L == "c2":
                            tt(m[:, 0, :, 0:D], ga[s][:, :, 0:D], norm_sb[:, here].rearrange("p (g a) -> p g a", a=1).broadcast_to([P, G, D]), ALU.mult)
                        if L == "l1":
                            z = ga[s][:, :, 0:DE * D].rearrange("p g (j h) -> p g j h", j=DE)
                            tt(z, z, ea_sb[:, here, :].rearrange("p g (j a) -> p g j a", a=1).broadcast_to([P, G, DE, D]), ALU.mult)
                            v.tensor_reduce(sq[:, :, :], z.rearrange("p g j h -> p g h j"), axis=AX, op=ALU.add).then_inc(m_made, 1)
                            dve.wait_ge(sig_made, k + 1)
                            link(v.scalar_tensor_tensor(out=m[:, 0, :, 0:D], in0=sq[:, :, :], scalar=NORM_MSG, in1=sg[s][:, :, :], op0=ALU.mult, op1=ALU.mult))
                        if L == "l2":
                            hyperbolic_messages(i, s, k, m)
                        if L == "l3":
                            sheaf_messages(i, s, k, m)
                        dve.wait_ge(key_set[L, s], i * per_key + per_key)
                        for a in range(SCATTER[L][3]):
                            fill_tiles(L, i, s, a)
                        dve.sem_inc(key_used[L, s], 1)
                loop_end(per_round)

            def hyperbolic_messages(i, s, k, m):
                row, z = ga[s][:, :, 0:D], sm[s]
                tt(sq[:, :, :], row, row, ALU.mult)
                red(z[:, 0, :], sq[:, :, :])
                v.tensor_scalar(z[:, 1, :], z[:, 0, :], 1e-10, None, ALU.max).then_inc(sq_made, 1)
                dve.wait_ge(tanh_made, k * 2 + 2)
                ts(z[:, 4, :], z[:, 2, :], SC, ALU.mult)
                link(v.reciprocal(z[:, 4, :], z[:, 4, :]))
                tt(z[:, 4, :], z[:, 4, :], z[:, 3, :], ALU.mult)
                tt(z[:, 5, :], z[:, 4, :], z[:, 4, :], ALU.mult)
                tt(z[:, 5, :], z[:, 5, :], z[:, 0, :], ALU.mult)
                ts(z[:, 5, :], z[:, 5, :], -0.5 * C, ALU.mult, 0.5 * (1.0 + EPS), ALU.add)
                link(v.reciprocal(m[:, 0, :, D], z[:, 5, :]))
                tt(z[:, 4, :], z[:, 4, :], m[:, 0, :, D], ALU.mult)
                v.tensor_tensor(m[:, 0, :, 0:D], row, bc(z[:, 4, :], G, D), ALU.mult).then_inc(m_made, 1)
                dve.wait_ge(m_made, GROUPS + k + 1)

            def sheaf_messages(i, s, k, m):
                rs, rd, z = ga[s], gb[s], sm[s]
                tt(hid[:, :, 0:HID], rs[:, :, 0:HID], rd[:, :, HID:2 * HID], ALU.add)
                v.tensor_tensor(hid[:, :, HID:], rd[:, :, 0:HID], rs[:, :, HID:2 * HID], ALU.add).then_inc(hid_made, 1)
                dve.wait_ge(v_ps, k * 4 + 4)
                vv = psV[:, 0:G * 2 * D].rearrange("p (g a d) -> p g a d", g=G, a=2)
                vec = [rs[:, :, 0:D], rs[:, :, D:2 * D]]
                for a in range(2):
                    tt(vec[a], vv[:, :, a, :], b2[:, :].rearrange("p (a d) -> p a d", a=1).broadcast_to([P, G, D]), ALU.add)
                dve.sem_inc(v_read, 1)
                for a in range(2):
                    tt(sq[:, :, :], vec[a], vec[a], ALU.mult)
                    red(z[:, a, :], sq[:, :, :])
                    ts(z[:, a, :], z[:, a, :], 1e-24, ALU.max, 0.5, ALU.mult)
                    link(v.reciprocal(z[:, a, :], z[:, a, :]))
                xs_, xd_ = rs[:, :, 2 * HID:2 * HID + D], rd[:, :, 2 * HID:2 * HID + D]

                def reflect(o, val, a):
                    tt(sq[:, :, :], vec[a], val, ALU.mult)
                    red(z[:, 2, :], sq[:, :, :])
                    tt(z[:, 2, :], z[:, 2, :], z[:, a, :], ALU.mult)
                    tt(sq[:, :, :], vec[a], bc(z[:, 2, :], G, D), ALU.mult)
                    tt(o, val, sq[:, :, :], ALU.subtract)

                for a, val in ((0, xd_), (1, xs_)):
                    tmp = rd[:, :, a * D:(a + 1) * D]
                    reflect(tmp, val, 1 - a)
                    reflect(tmp, tmp, a)
                    tt(m[:, a, :, 0:D], tmp, (rd, rs)[a][:, :, W5 - 1:W5].broadcast_to([P, G, D]), ALU.mult)

            def agg_nodes(L):
                return psT[0][0:CHUNK8, 0:4 * Q8 * D].rearrange("p (c q d) -> p q c d", c=4, q=Q8)

            def j4(t):
                return t[:, :, 0:D].rearrange("p (q c) d -> p q c d", q=Q8)

            rows = lambda pitch: big[0:NP_, 0:NJ * pitch].rearrange("p (j c) -> p j c", j=NJ)

            dve.wait_ge(x_in, 32)
            for L in ("c1", "c2"):
                if L == "c1":
                    relu_layernorm(H17[:, :, 0:D])
                    dve.wait_ge(norm_out, 16)
                dve.sem_inc(xt_in[L], 1)
                dve.wait_ge(proj_sb[L], -(-NJ // PROJ[L][1]))
                dve.sem_inc(table_made[L], 1)
                link(v.tensor_copy(A[:, :, :], rows(REL * D + D)[:, :, REL * D:]))
                edge_pass(L)
                dve.wait_ge(aggT[L], 1)
                tt(j4(B), agg_nodes(L), j4(A), ALU.add)
                if L == "c1":
                    ts(H17[:, :, 0:D], B[:, :, :], 0.0, ALU.max)
            red(n3[:, :], B[:, :, :], ALU.max)
            tt(B[:, :, :], B[:, :, :], bc(n3[:, :], NJ, D), ALU.subtract)
            call_act()
            red(n1[:, :], C_[:, :, :])
            call_act()
            tt(B[:, :, :], B[:, :, :], bc(n2[:, :], NJ, D), ALU.subtract)
            tt(X[:, :, :], X[:, :, :], B[:, :, :], ALU.add)

            L = "l1"
            relu_layernorm(H17[:, :, 0:D])
            dve.sem_inc(xt_in[L], 1)
            dve.wait_ge(proj_sb[L], -(-NJ // PROJ[L][1]))
            dve.sem_inc(table_made[L], 1)
            dve.wait_ge(ea_in, 48)
            edge_pass(L)
            relay_back(dve, v, link, L, 1)
            link(v.tensor_copy(degs[:, :], AGR[:, :, D]))
            link(v.tensor_copy(HT[:, :, 0:D], AGR[:, :, 0:D]))
            dve.sem_inc(lin_in, 1)
            dve.wait_ge(lin_mm, 1)
            psVn = psV[0:NP_, 0:NJ * D].rearrange("p (j d) -> p j d", j=NJ)
            ts(A[:, :, :], psVn, NORM_LIN, ALU.mult)
            dve.sem_inc(lin_in, 1)
            for j in range(NJ):
                dve.wait_ge(upd_ps, j + 1)
                v.tensor_tensor(prod[:, j % 2, :].rearrange("p (h k) -> p h k", h=D), psM[j % 4][0:NP_, 0:D * D].rearrange("p (h k) -> p h k", h=D),
                                A[:, j, :].rearrange("p (h a) -> p h a", a=1).broadcast_to([NP_, D, D]), ALU.mult).then_inc(upd_read, 1)
                dve.wait_ge(upd_read, j + 1)
                link(v.tensor_reduce(B[:, j, :], prod[:, j % 2, :].rearrange("p (h k) -> p k h", h=D), axis=AX, op=ALU.add))
            call_act()
            link(v.scalar_tensor_tensor(out=HT[:, :, 0:D], in0=B[:, :, :], scalar=NORM_UPD, in1=C_[:, :, :], op0=ALU.mult, op1=ALU.mult))
            dve.sem_inc(lin_in, 1)
            tt(X[:, :, :], X[:, :, :], H17[:, :, 0:D], ALU.add)
            dve.wait_ge(lin_mm, 2)
            link(v.scalar_tensor_tensor(out=X[:, :, :], in0=psVn, scalar=NORM_LIN, in1=X[:, :, :], op0=ALU.mult, op1=ALU.add))

            L = "l2"
            relu_layernorm(H17[:, :, 0:D])
            norm_of(n1[:, :], H17[:, :, 0:D])
            ts(n1[:, :], n1[:, :], 1e-10, ALU.max)
            call_act()
            ts(n2[:, :], n2[:, :], SC, ALU.mult)
            ts(n3[:, :], n2[:, :], -1.0 + BALL, ALU.max, 1.0 - BALL, ALU.min)
            tt(n4[:, :], n3[:, :], n3[:, :], ALU.mult)
            ts(n5[:, :], n4[:, :], 1.0 / 23, ALU.mult, 1.0 / 21, ALU.add)
            for t in range(19, 0, -2):
                tt(n5[:, :], n5[:, :], n4[:, :], ALU.mult)
                ts(n5[:, :], n5[:, :], 1.0 / t, ALU.add)
            tt(HT[:, :, 0:D], H17[:, :, 0:D], bc(n5[:, :], NJ, D), ALU.mult)
            dve.sem_inc(xt_in[L], 1)
            dve.wait_ge(proj_ps[L], 1)
            link(v.tensor_copy(V[:, :, :], psVn))
            dve.sem_inc(rel_dve, 2)
            with dve.Fori(0, NJ // 2, 1) as i:
                for h in range(2):
                    dve.wait_ge(row_free[h], i + 1)
                    for c in range(1, EC, 2):
                        dve.wait_ge(rel_ps, i * (2 * EC) + h * EC + c + 1)
                        v.tensor_copy(big[0:NP_, (h * EC + c) * ECOLS:(h * EC + c + 1) * ECOLS], psM[c % 4][0:NP_, 0:ECOLS]).then_inc(rel_dve, 1)
            edge_pass(L)
            relay_back(dve, v, link, L, 2)
            deg = AGR[:, :, D + 1]
            ts(n1[:, :], deg, 1.0, ALU.max)
            call_act()
            link(v.reciprocal(n2[:, :], n2[:, :]))
            tt(n3[:, :], deg, n2[:, :], ALU.mult)
            ts(n3[:, :], n3[:, :], EPS, ALU.add)
            link(v.reciprocal(n3[:, :], n3[:, :]))
            tt(n3[:, :], n3[:, :], n2[:, :], ALU.mult)
            tt(n4[:, :], n3[:, :], AGR[:, :, D], ALU.mult)
            ts(n4[:, :], n4[:, :], EPS, ALU.add)
            link(v.reciprocal(n4[:, :], n4[:, :]))
            tt(A[:, :, :], AGR[:, :, 0:D], bc(n3[:, :], NJ, D), ALU.mult)
            tt(A[:, :, :], A[:, :, :], bc(n4[:, :], NJ, D), ALU.mult)
            tt(degs[:, :], degs[:, :], deg, ALU.add)
            norm_of(n1[:, :], A[:, :, :])
            ts(n1[:, :], n1[:, :], 1e-10, ALU.max)
            call_act()
            link(v.reciprocal(n2[:, :], n2[:, :]))
            ts(n2[:, :], n2[:, :], (1.0 - BALL) / SC, ALU.mult, 1.0, ALU.min)
            tt(A[:, :, :], A[:, :, :], bc(n2[:, :], NJ, D), ALU.mult)
            norm_of(n1[:, :], V[:, :, :])
            ts(n1[:, :], n1[:, :], 1e-10, ALU.max)
            call_act()
            ts(n2[:, :], n2[:, :], SC, ALU.mult)
            call_act()
            link(v.reciprocal(n2[:, :], n2[:, :]))
            tt(n3[:, :], n3[:, :], n2[:, :], ALU.mult)
            tt(V[:, :, :], V[:, :, :], bc(n3[:, :], NJ, D), ALU.mult)
            norm_of(n1[:, :], A[:, :, :])
            norm_of(n2[:, :], V[:, :, :])
            tt(B[:, :, :], A[:, :, :], V[:, :, :], ALU.mult)
            red(n3[:, :], B[:, :, :])
            ts(n3[:, :], n3[:, :], 2.0 * C, ALU.mult, 1.0, ALU.add)
            link(v.scalar_tensor_tensor(out=n4[:, :], in0=n2[:, :], scalar=C, in1=n3[:, :], op0=ALU.mult, op1=ALU.add))
            ts(n5[:, :], n1[:, :], -C, ALU.mult, 1.0, ALU.add)
            tt(n6[:, :], n1[:, :], n2[:, :], ALU.mult)
            link(v.scalar_tensor_tensor(out=n6[:, :], in0=n6[:, :], scalar=C * C, in1=n3[:, :], op0=ALU.mult, op1=ALU.add))
            ts(n6[:, :], n6[:, :], 1e-10, ALU.max)
            link(v.reciprocal(n6[:, :], n6[:, :]))
            tt(A[:, :, :], A[:, :, :], bc(n4[:, :], NJ, D), ALU.mult)
            tt(V[:, :, :], V[:, :, :], bc(n5[:, :], NJ, D), ALU.mult)
            tt(A[:, :, :], A[:, :, :], V[:, :, :], ALU.add)
            tt(A[:, :, :], A[:, :, :], bc(n6[:, :], NJ, D), ALU.mult)
            tt(X[:, :, :], X[:, :, :], A[:, :, :], ALU.add)

            L = "l3"
            relu_layernorm(H17[:, :, 0:D])
            dve.sem_inc(xt_in[L], 1)
            ts(n1[:, :], degs[:, :], 1e-5, ALU.max)
            dve.wait_ge(proj_sb[L], -(-NJ // PROJ[L][1]))
            call_act()
            link(v.reciprocal(n2[:, :], n2[:, :]))
            link(v.tensor_copy(rows(W5)[:, :, 2 * HID:2 * HID + D], H17[:, :, 0:D]))
            link(v.tensor_copy(rows(W5)[:, :, W5 - 1], n2[:, :]))
            dve.sem_inc(table_made[L], 1)
            dve.sem_inc(v_read, 1)
            edge_pass(L)
            dve.wait_ge(aggT[L], 1)
            link(v.tensor_copy(j4(A), agg_nodes(L)))
            tt(A[:, :, :], A[:, :, :], bc(n2[:, :], NJ, D), ALU.mult)
            tt(A[:, :, :], A[:, :, :], H17[:, :, 0:D], ALU.add)
            ts(A[:, :, :], A[:, :, :], 0.0, ALU.max)
            v.tensor_tensor(X[:, :, :], X[:, :, :], A[:, :, :], ALU.add).then_inc(x_made, 1)

NORM_MSG = float(np.float32(1.0) / np.float32(np.sqrt(D * DE)))
NORM_UPD = float(np.float32(1.0) / np.float32(np.sqrt(D * D)))
NORM_LIN = float(np.float32(1.0) / np.float32(np.sqrt(D)))
SC, C, EPS, BALL = 0.1, 0.01, 1e-6, 1e-5
PROJ = {"c1": (REL * D + D, 3), "c2": (REL * D + D, 3), "l1": (DE * D, 4), "l3": (2 * HID, 4)}
WEIGHT_LOADS = 6 + 2 + 3 + 2 + 4 + 2
_A = mybir.ActivationFunctionType
SQ = (_A.Sqrt, "n2", "n1", 1.0)
LIN = ("T", None, None, None)
NODE_FUNCS = {("c2", "end"): [(_A.Exp, "C", "B", 1.0), (_A.Ln, "n2", "n1", 1.0)],
              ("l1", "end"): [LIN, LIN, (_A.Sigmoid, "C", "B", NORM_UPD), LIN],
              ("l2", "start"): [SQ], ("l2", "end"): [SQ, SQ, SQ, (_A.Tanh, "n3", "n2", 1.0)], ("l3", "table"): [SQ]}

_INS = ["x", "src", "dst", "edge_attr_8", "edge_type_230", "edge_type_8",
        "L0_gnn_W1", "L0_gnn_root1", "L0_gnn_b1", "L0_gnn_W2", "L0_gnn_root2", "L0_gnn_b2",
        "L1_gnn_W_msg_tp", "L1_gnn_W_msg_lin", "L1_gnn_W_upd_tp", "L1_gnn_W_upd_lin",
        "L2_gnn_rel_weight", "L2_gnn_loop_weight", "L2_gnn_rel_emb",
        "L3_gnn_W1", "L3_gnn_b1", "L3_gnn_W2", "L3_gnn_b2"]

_TRANSPOSED = ("L3_gnn_W1", "L3_gnn_W2")


def kernel(**inputs):
    import numpy as _np
    import concourse.bacc as _bacc
    from concourse import mybir as _mybir
    from concourse.bass_utils import run_bass_kernel_spmd as _run

    nc = _bacc.Bacc("TRN2", target_bir_lowering=False, num_devices=1)
    arrays, args = {}, []
    for name in _INS:
        a = _np.ascontiguousarray(inputs[name].T if name in _TRANSPOSED else inputs[name])
        arrays[f"in_{name}"] = a
        args.append(nc.dram_tensor(f"in_{name}", a.shape, _mybir.dt.from_np(a.dtype), kind="ExternalInput").ap())
    args.append(nc.dram_tensor("out_x", (N, D), _mybir.dt.float32, kind="ExternalOutput").ap())
    gnn(nc, *args)
    r = _run(nc, [arrays], core_ids=[0])
    return r.results[0]["out_x"]
```

```python
import concourse.bass as bass
from concourse import mybir
from contextlib import ExitStack
import numpy as np

N, E, D = 3125, 100000, 16
P = 128
T = 784
G = 14
SLOTS = 2
GROUPS = T // G
ITERS = GROUPS // SLOTS
GE = P * G
FULL = E // GE
TAIL = E - FULL * GE
WIN = P
NP_, NJ = 98, 32
NPAD = NP_ * NJ
NLAST = N - (NJ - 1) * NP_
REL, TYPES, DE, HID = 8, 230, 8, 64
Q8, R8 = 8, 392
Q7, R7 = 7, 448
CHUNK8, CHUNK7 = R8 // 4, R7 // 4
W5 = D + 1 + 2 * HID
W5W = W5 + HID
XD = D + 1
EC = 8
ECOLS = TYPES * D // EC
PAD_KEY = -1000.0
BIG = 2 * TYPES * D
ACT_TILES = 5
RING = 7


def gnn(nc, x, src, dst, ea, t230, t8, cW1, croot1, cb1, cW2, croot2, cb2,
        mtp, mlin, utp, ulin, relw, loopw, relemb, sW1, sb1, sW2, sb2, out):
    f32, i32, bf16, f16 = mybir.dt.float32, mybir.dt.int32, mybir.dt.bfloat16, mybir.dt.float16
    ALU, ACT, AX = mybir.AluOpType, mybir.ActivationFunctionType, mybir.AxisListType.X

    with ExitStack() as ctx:
        def sb(name, shape, dt=f32):
            return ctx.enter_context(nc.sbuf_tensor(name, shape, dt))

        def dram(name, shape):
            return nc.dram_tensor(name, shape, f32).ap()

        def sem(name):
            return ctx.enter_context(nc.semaphore(name))

        tabs = {"c1": dram("tab_c1", (NPAD * REL, D)), "c2": dram("tab_c2", (NPAD * REL, D)),
                "l1": dram("tab_l1", (NPAD, DE * D)), "l2": dram("tab_l2", (NPAD * TYPES, D)),
                "l3": dram("tab_l3", (NPAD, W5W)), "norm": dram("tab_norm", (NPAD, REL))}
        relay = {"l1": dram("relay_l1", (NPAD, D + 1)), "l2": dram("relay_l2", (NPAD, D + 1))}

        ident, ident_b = sb("ident", [P, P]), sb("ident_b", [P, P], bf16)
        iota_r = sb("iota_r", [P, R7])
        iota_q = sb("iota_q", [P, Q8])
        zeros = sb("zeros", [P, R7], bf16)
        src_i, dst_i = sb("src_i", [P, T], i32), sb("dst_i", [P, T], i32)
        rel_row = sb("rel_row", [P, T], i32)
        type_row = sb("type_row", [P, T], i32)
        ea_sb = sb("ea_sb", [P, T, DE])
        norm_sb = sb("norm_sb", [P, T])
        keys = {k: sb("key_" + k, [P, GROUPS, 2, G], f16) for k in ("dst8", "dst7", "src7", "src8")}
        loc = sb("loc", [P, GROUPS, G], f16)
        typ = sb("typ", [P, GROUPS, G], f16)
        win_row = sb("win_row", [P, GROUPS], i32)
        win_key = {k: sb("win_key" + k, [P, GROUPS, 2]) for k in ("8", "7")}
        flag = sb("flag", [1, 1], i32)
        iota_p = sb("iota_p", [P, 1])
        ones = sb("ones", [GROUPS, P])
        wa, wb, wc_ = (sb(f"wtmp{k}", [P, GROUPS]) for k in range(3))
        idx = [sb(f"idx{s}", [P, 2, G], i32) for s in range(SLOTS)]
        kf = [sb(f"kf{s}", [P, 4, G]) for s in range(SLOTS)]
        idx_w = [sb(f"idx_w{s}", [P, 1], i32) for s in range(SLOTS)]
        kw = [sb(f"kw{s}", [P, 1, 2]) for s in range(SLOTS)]
        win = [sb(f"win{s}", [P, W5W]) for s in range(SLOTS)]
        win_parts = [sb(f"win_parts{s}", [P, 3, W5W], bf16) for s in range(SLOTS)]
        hot = [sb(f"hot{s}", [P, G, WIN], bf16) for s in range(SLOTS)]
        hotT = [sb(f"hotT{s}", [P, G, P], bf16) for s in range(SLOTS)]
        msg_parts = [sb(f"msg_parts{s}", [P, G, 3 * (D + 1)], bf16) for s in range(SLOTS)]
        res = sb("res", [P, G, D + 1])
        vec, sq2, y2 = (sb(n, [P, G, 2, D]) for n in ("vec", "sq2", "y2"))
        c2 = sb("c2", [P, 2, 2 * G])
        wsum = [sb(f"wsum{s}", [P, D + 1]) for s in range(SLOTS)]
        S2 = [sb(f"S2{s}", [P, P]) for s in range(SLOTS)]
        O2 = [sb(f"O2{s}", [P, R7]) for s in range(SLOTS)]
        ga = [sb(f"ga{s}", [P, G, W5]) for s in range(SLOTS)]
        gb = [sb(f"gb{s}", [P, G, W5]) for s in range(SLOTS)]
        msg = [sb(f"msg{s}", [P, 2, G, D + 1]) for s in range(SLOTS)]
        sq = sb("sq", [P, G, D])
        sg = [sb(f"sg{s}", [P, G, D]) for s in range(SLOTS)]
        sm = [sb(f"sm{s}", [P, 8, G]) for s in range(SLOTS)]
        ea_flat = ea_sb[:, :, :].rearrange("p t j -> p (t j)")
        hid = ea_flat[:, 0:G * 2 * HID].rearrange("p (g c) -> p g c", g=G)
        hidT = ea_flat[:, G * 2 * HID:G * 2 * HID + 8 * P].rearrange("p (a g e) -> p a g e", a=2, g=4)
        S = sb("S", [P, RING, P])
        O_XT = sb("O_XT", [P, NPAD + NP_])
        O = O_XT[:, 0:RING * R7].rearrange("p (g r) -> p g r", g=RING)
        XT = O_XT[0:D + 1, :]
        wrel = ea_flat[0:D + 1, 0:TYPES * D]
        big = sb("big", [P, BIG])
        X, H17, HT = sb("X", [NP_, NJ, D]), sb("H17", [NP_, NJ, D + 1]), sb("HT", [NP_, NJ, D + 1])
        A, B, C_, V = (sb(n, [NP_, NJ, D]) for n in ("A", "B", "C_", "V"))
        AGR = sb("AGR", [NP_, NJ, D + 1])
        degs, deg_dst = sb("degs", [NP_, NJ]), sb("deg_dst", [NP_, NJ])
        cnt = sb("cnt", [NP_, NJ, REL])
        n1, n2, n3, n4, n5, n6 = (sb(f"n{k}", [NP_, NJ]) for k in range(1, 7))
        AG = sb("AG", [P, R7])
        AGT = sb("AGT", [CHUNK7, 4 * Q7, D + 1])
        XTj = sb("XTj", [D + 1, 2, NP_])
        prod = big[0:NP_, 0:2 * D * D].rearrange("p (a c) -> p a c", a=2)
        lane = big[:, 8 * T:9 * T].bitcast(i32)
        wc = [sb(f"wc{k}", [D + 1, REL * D + D]) for k in range(2)]
        wl1 = sb("wl1", [D + 1, DE * D])
        wupd = sb("wupd", [D + 1, D * D])
        wlin, wulin, wloop = (sb(n, [D + 1, D]) for n in ("wlin", "wulin", "wloop"))
        wpq = sb("wpq", [D + 1, 2 * HID])
        w2 = sb("w2", [P, 2 * D])
        b2 = sb("b2", [P, 2 * D])

        agg = ctx.enter_context(nc.psum_tensor("agg", [P, 512], f32))
        psT = [ctx.enter_context(nc.psum_tensor(f"psT{k}", [P, 512], f32)) for k in range(2)]
        psM = [ctx.enter_context(nc.psum_tensor(f"psM{k}", [P, 512], f32)) for k in range(4)]
        psTb = [t[:, 0:G // 2 * P // 2].bitcast(bf16) for t in psT]
        psV = ctx.enter_context(nc.psum_tensor("psV", [P, 512], f32))

        LAYERS = ("cn", "c1", "c2", "l1", "l2", "l3")
        consts_made, ident_made = sem("consts_made"), sem("ident_made")
        zeroed, edges_in, ea_in, weights_in, x_in = (sem(n) for n in ("zeroed", "edges_in", "ea_in", "weights_in", "x_in"))
        dve_step = sem("dve_step")
        norm_made, norm_out, flag_made, wrel_in = (sem(n) for n in ("norm_made", "norm_out", "flag_made", "wrel_in"))
        prep_dve, prep_pe = sem("prep_dve"), sem("prep_pe")
        step_front = sem("step_front")
        tile_act = {L: sem(f"tile_act_{L}") for L in LAYERS}
        step_of = {L: sem(f"step_{L}") for L in LAYERS}
        win_in = {(L, s): sem(f"win_in_{L}{s}") for L in ("c1", "l1", "l3") for s in range(SLOTS)}
        hot_made, win_split, hotT_ps, hotT_sb = (sem(n) for n in ("hot_made", "win_split", "hotT_ps", "hotT_sb"))
        rows_ps, rows_sb = ({L: sem(f"{n}_{L}") for L in ("c1", "l1", "l3")} for n in ("rows_ps", "rows_sb"))
        groups_before = {"c1": 0, "l1": GROUPS, "l3": 2 * GROUPS}
        parts_made, wsum_ps, wsum_read, tile2_free, tile2_ready = ({L: sem(f"{n}_{L}") for L in LAYERS if L != "l1"} for n in (
            "parts_made", "wsum_ps", "wsum_read", "tile2_free", "tile2_ready"))
        TABLES = LAYERS[1:]
        xt_in, xt_ps, xt_sb, table_made, table_out, agg_done, agg_sb, aggT = (sem(n) for n in (
            "xt_in", "xt_ps", "xt_sb", "table_made", "table_out", "agg_done", "agg_sb", "aggT"))
        nth = {L: n + 1 for n, L in enumerate(LAYERS)}
        nth_xt = {L: n + 1 for n, L in enumerate(TABLES)}
        nth_tab = {L: n + 1 for n, L in enumerate(("c1", "c2", "l1", "l3"))}
        xt_before = {L: n * (NJ // 4) for n, L in enumerate(TABLES)}
        idx_set = {L: sem(f"idx_set_{L}") for L in TABLES}
        proj_ps, proj_sb, loop_ps = sem("proj_ps"), sem("proj_sb"), sem("loop_ps")
        proj_banks = {L: -(-NJ // PROJ[L][1]) for L in nth_tab}
        proj_before = {L: sum(proj_banks[M] for M in nth_tab if nth_tab[M] < nth_tab[L]) for L in nth_tab}
        gathered = {(L, s): sem(f"gathered_{L}{s}") for L in TABLES for s in range(SLOTS)}
        key_set, key_used, tile_free, tile_ready = ({L: sem(f"{n}_{L}") for L in LAYERS} for n in (
            "key_set", "key_used", "tile_free", "tile_ready"))
        var_made, std_made = sem("var_made"), sem("std_made")
        act_in, act_out = sem("act_in"), sem("act_out")
        relay_made, relay_out, relay_in = sem("relay_made"), sem("relay_out"), sem("relay_in")
        lin_in, lin_ps, lin_sb, lin_mm, lin_read = (sem(n) for n in ("lin_in", "lin_ps", "lin_sb", "lin_mm", "lin_read"))
        upd_ps, upd_read = sem("upd_ps"), sem("upd_read")
        xtj_set, rel_ps, rel_act, rel_dve = (sem(n) for n in ("xtj_set", "rel_ps", "rel_act", "rel_dve"))
        row_free = [sem(f"row_free{h}") for h in range(2)]
        rel_row_out = [sem(f"rel_row_out{h}") for h in range(2)]
        m_made, sig_made, sq_made, tanh_made = (sem(n) for n in ("m_made", "sig_made", "sq_made", "tanh_made"))
        hid_made, hidT_ps, hidT_sb, v_ps, v_read = (sem(n) for n in ("hid_made", "hidT_ps", "hidT_sb", "v_ps", "v_read"))
        hyp_made = sem("hyp_made")
        gathers_begun = sem("gathers_begun")
        rows_used = sem("rows_used")
        x_made, x_out = sem("x_made"), sem("x_out")

        block = ctx.enter_context(nc.Block())

        def nodes(dr):
            return (dr[0:(NJ - 1) * NP_, :].rearrange("(j p) d -> p j d", p=NP_), dr[(NJ - 1) * NP_:N, :])

        SCATTER = {"cn": (Q8, R8, REL, 1), "c1": (Q8, R8, D, 1), "c2": (Q8, R8, D, 1), "l1": (Q7, R7, D + 1, 1),
                   "l2": (Q7, R7, D + 1, 1), "l3": (Q8, R8, D, 2)}
        WINDOW = {"c1": (REL, G), "l1": (DE * D, 4), "l3": (D + 1, G)}
        WIN_COLS = {"c1": REL, "l1": DE * D, "l3": W5W}
        BY_DST = ("cn", "c1", "c2", "l2", "l3")
        PARTS = {"cn": 1, "c1": 3, "c2": 3, "l2": 3, "l3": 3}

        def in_pairs(eng, front, back, early=lambda i, s: None):
            front(0, 0)
            with eng.Fori(0, ITERS - 1, 1) as i:
                early(i, 0)
                front(i, 1)
                back(i, 0)
                early(i, 1)
                front(i + 1, 0)
                back(i, 1)
            early(ITERS - 1, 0)
            front(ITERS - 1, 1)
            back(ITERS - 1, 0)
            early(ITERS - 1, 1)
            back(ITERS - 1, 1)

        def ready_before(t):
            return sum(1 if n % G < ACT_TILES else 2 for n in range(t + 1))

        def acts_of(tiles):
            return 2 * sum(t % G < ACT_TILES for t in range(tiles))

        def two_paths(eng, L, path):
            with eng.If(eng.value_load(flag[0:1, 0:1], min_val=0, max_val=1) > 0):
                path(L, False)
            with eng.Else():
                path(L, True)

        def relay_out_and_in(sp, L, turn):
            d = SCATTER[L][2]
            sp.wait_ge(relay_made, turn)
            sp.dma_start(relay[L].rearrange("(j p) d -> p j d", p=CHUNK7), AGT[:, :, 0:d]).then_inc(relay_out, 16)
            sp.wait_ge(relay_out, 16 * turn)
            sp.dma_start(AGR[:, :, 0:d], relay[L].rearrange("(j p) d -> p j d", p=NP_)).then_inc(relay_in, 16)

        @block.sync
        def _(sp):
            sp.wait_ge(zeroed, 1)
            part, odd = TAIL // G, TAIL % G
            for tile, dr in ((src_i, src), (dst_i, dst), (rel_row, t8), (type_row, t230)):
                sp.dma_start(tile[:, 0:FULL * G].rearrange("p (k g) -> p k g", g=G),
                             dr[0:FULL * GE].rearrange("(k p g) -> p k g", p=P, g=G)).then_inc(edges_in, 16)
                sp.dma_start(tile[0:part, FULL * G:], dr[FULL * GE:FULL * GE + part * G].rearrange("(p g) -> p g", g=G)).then_inc(edges_in, 16)
                sp.dma_start(tile[part:part + 1, FULL * G:FULL * G + odd], dr[E - odd:E].rearrange("(p g) -> p g", p=1)).then_inc(edges_in, 16)
            full, last = nodes(x)
            sp.dma_start(X[:, 0:NJ - 1, :], full).then_inc(x_in, 16)
            sp.dma_start(X[0:NLAST, NJ - 1, :], last).then_inc(x_in, 16)
            sp.dma_start(ea_sb[:, 0:FULL * G, :].rearrange("p (k g) j -> p k (g j)", g=G),
                         ea[0:FULL * GE, :].rearrange("(k p g) j -> p k (g j)", p=P, g=G)).then_inc(ea_in, 16)
            sp.dma_start(ea_sb[0:part, FULL * G:, :], ea[FULL * GE:FULL * GE + part * G, :].rearrange("(p g) j -> p g j", g=G)).then_inc(ea_in, 16)
            sp.dma_start(ea_sb[part:part + 1, FULL * G:FULL * G + odd, :], ea[E - odd:E, :].rearrange("(p g) j -> p g j", p=1)).then_inc(ea_in, 16)
            sp.wait_ge(norm_made, 1)
            sp.dma_start(tabs["norm"].rearrange("(j p) t -> p j t", p=NP_), cnt[:, :, :]).then_inc(norm_out, 16)
            for L, cols, pitch in (("c1", REL * D, REL * D + D), ("c2", REL * D, REL * D + D), ("l1", DE * D, DE * D), ("l3", W5W, W5W)):
                if L == "l3":
                    relay_out_and_in(sp, "l2", 2)
                sp.wait_ge(table_made, nth_tab[L])
                view = tabs[L] if L in ("l1", "l3") else tabs[L].rearrange("(n r) d -> n (r d)", r=REL)
                rows = big[0:NP_, 0:NJ * pitch].rearrange("p (j c) -> p j c", j=NJ)[:, :, 0:cols]
                sp.dma_start(view.rearrange("(j p) c -> p j c", p=NP_), rows).then_inc(table_out, 16)
                if L == "l1":
                    sp.wait_ge(agg_sb, nth[L])
                    sp.dma_start(wrel[0:D, :].rearrange("i (t o) -> i t o", t=TYPES), relw.rearrange("t i o -> i t o")).then_inc(wrel_in, 16)
                    sp.dma_start(wrel[D:D + 1, :], relemb.rearrange("(a t) o -> a (t o)", a=1)).then_inc(wrel_in, 16)
                    relay_out_and_in(sp, "l1", 1)
                    wide = tabs["l2"].rearrange("(j p t) d -> j p (t d)", p=NP_, t=TYPES)
                    for h in range(2):
                        sp.sem_inc(row_free[h], 1)
                    with sp.Fori(0, NJ // 2, 1) as i:
                        for h in range(2):
                            sp.wait_ge(rel_act, i * EC + (EC // 2) * (h + 1) + 2)
                            sp.wait_ge(rel_dve, i * EC + (EC // 2) * (h + 1) + 2)
                            sp.dma_start(wide[bass.ds(i * 2 + h, 1), :, :].rearrange("a p c -> p (a c)"),
                                         big[0:NP_, h * TYPES * D:(h + 1) * TYPES * D]).then_inc(rel_row_out[h], 16)
                            sp.wait_ge(rel_row_out[h], i * 16 + 16)
                            sp.sem_inc(row_free[h], 1)
            sp.wait_ge(x_made, 1)
            full, last = nodes(out)
            sp.dma_start(full, X[:, 0:NJ - 1, :]).then_inc(x_out, 16)
            sp.dma_start(last, X[0:NLAST, NJ - 1, :]).then_inc(x_out, 16)
            sp.wait_ge(x_out, 32)

        @block.gpsimd
        def _(pool):
            nc.gpsimd.iota(iota_r[:, :], pattern=[[1, R7]], base=0, channel_multiplier=0,
                           allow_small_or_imprecise_dtypes=True).then_inc(consts_made, 1)
            nc.gpsimd.iota(iota_q[:, :], pattern=[[1, Q8]], base=0, channel_multiplier=0,
                           allow_small_or_imprecise_dtypes=True).then_inc(consts_made, 1)
            nc.gpsimd.iota(lane, pattern=[[GE, GROUPS], [1, G]], base=0, channel_multiplier=G).then_inc(consts_made, 1)
            nc.gpsimd.iota(iota_p[:, :], pattern=[[0, 1]], base=0, channel_multiplier=1,
                           allow_small_or_imprecise_dtypes=True).then_inc(consts_made, 1)
            nc.gpsimd.memset(ones[:, :], 1.0).then_inc(consts_made, 1)
            nc.gpsimd.memset(ident[:, :], 0.0).then_inc(ident_made, 1)
            pool.wait_ge(ident_made, 1)
            nc.gpsimd.affine_select(out=ident[:, :], in_=ident[:, :], compare_op=ALU.not_equal, fill=1.0, base=0,
                                    pattern=[[-1, P]], channel_multiplier=1).then_inc(ident_made, 1)
            pool.wait_ge(flag_made, 1)
            GATHERS = {"c1": ((rel_row, D, tabs["c1"]), (dst_i, REL, tabs["norm"])), "c2": ((rel_row, D, tabs["c2"]),),
                       "l1": ((dst_i, DE * D, tabs["l1"]),), "l2": ((type_row, D, tabs["l2"]),),
                       "l3": ((src_i, W5, tabs["l3"]), (dst_i, W5, tabs["l3"]))}

            def gather_pass(L, windows):
                by_edge = [n for n, gth in enumerate(GATHERS[L]) if not (windows and gth[0] is dst_i)]
                by_window = [gth for gth in GATHERS[L] if windows and gth[0] is dst_i]
                copies = len(by_edge) + len(by_window)
                with pool.Fori(0, ITERS, 1) as i:
                    for s in range(SLOTS):
                        pool.wait_ge(rows_used, i * SLOTS + s + 1 + GROUPS * (nth[L] - 1))
                        for n in by_edge:
                            nc.gpsimd.tensor_copy(idx[s][:, n, :], GATHERS[L][n][0][:, bass.ds(i * (SLOTS * G) + s * G, G)]).then_inc(idx_set[L], 1)
                        for _ in by_window:
                            nc.gpsimd.tensor_copy(idx_w[s][:, :], win_row[:, bass.ds(i * SLOTS + s, 1)]).then_inc(idx_set[L], 1)
                        pool.wait_ge(idx_set[L], (i * SLOTS + s) * copies + copies)
                        pool.sem_inc(gathers_begun, 1)
                        for _, _, table in by_window:
                            cols = WIN_COLS[L]
                            pool.indirect_dma_start(
                                out=win[s][:, 0:cols], out_offset=None, in_=table,
                                in_offset=bass.IndirectOffsetOnAxis(ap=idx_w[s][:, 0:1], axis=0)).then_inc(win_in[L, s], 16)
                        for n in by_edge:
                            _, cols, table = GATHERS[L][n]
                            to = gb[s] if L == "l1" else (ga, gb)[n][s]
                            for g in range(G):
                                pool.indirect_dma_start(
                                    out=to[:, g, 0:cols], out_offset=None, in_=table,
                                    in_offset=bass.IndirectOffsetOnAxis(ap=idx[s][:, n, g:g + 1], axis=0)).then_inc(gathered[L, s], 16)

            for L in LAYERS[1:]:
                if L == "l2":
                    for h in range(2):
                        pool.wait_ge(rel_row_out[h], 16 * NJ // 2)
                else:
                    pool.wait_ge(table_out, 16 * nth_tab[L])
                if L == "c1":
                    pool.wait_ge(norm_out, 16)
                two_paths(pool, L, gather_pass)

        act_calls, lin_calls = [0], [0]

        def node_functions(act, L, where):
            for fn, o, a, scale in NODE_FUNCS.get((L, where), ()):
                if fn == "T":
                    for k in range(NJ // 4):
                        lin_calls[0] += 1
                        act.wait_ge(lin_ps, lin_calls[0])
                        nc.scalar.copy(XT[:, k * 4 * NP_:(k + 1) * 4 * NP_], psT[k % 2][0:D + 1, 0:4 * NP_]).then_inc(lin_sb, 1)
                    continue
                act_calls[0] += 1
                act.wait_ge(act_in, act_calls[0])
                t = {"n1": n1[:, :], "n2": n2[:, :], "n3": n3[:, :], "B": B[:, :, :], "C": C_[:, :, :]}
                nc.scalar.activation(t[o], t[a], fn, scale=scale).then_inc(act_out, 1)

        @block.scalar
        def _(act):
            def act_aggregate(L):
                q, r, d, per_edge = SCATTER[L]
                act.wait_ge(agg_done, nth[L])
                nc.scalar.copy(AG[0:q * d, 0:r], agg[0:q * d, 0:r]).then_inc(agg_sb, 1)

            def act_edges(L, windows):
                names = {"cn": ("dst8",), "c1": ("dst8",), "c2": ("dst8",), "l1": ("src7",), "l2": ("dst7",), "l3": ("src8", "dst8")}[L]
                if windows:
                    names = tuple(n for n in names if n[:3] == "src")
                if windows and L in WINDOW:
                    act.sem_inc(rows_sb[L], 1)
                full_tiles = G * (SCATTER[L][3] - (1 if windows and L in BY_DST else 0))
                per_key = 2 if L == "l3" else 1

                def front(i, s):
                    k = i * SLOTS + s
                    act.wait_ge(key_used[L], k + 1)
                    for a, name in enumerate(names):
                        nc.scalar.copy(kf[s][:, 2 * a:2 * a + 2, :], keys[name][:, bass.ds(k, 1), :, :].rearrange("p a k g -> p (a k) g")).then_inc(key_set[L], 1)
                    if windows and L in BY_DST:
                        nc.scalar.copy(kw[s][:, :, :], win_key[str(SCATTER[L][0])][:, bass.ds(k, 1), :]).then_inc(key_set[L], 1)
                    if windows and L in WINDOW:
                        for c in range(2):
                            act.wait_ge(hotT_ps, (groups_before[L] + k) * 2 + c + 1)
                            nc.scalar.copy(hotT[s][:, c * (G // 2):(c + 1) * (G // 2), :],
                                           psTb[c].rearrange("p (g e) -> p g e", e=P)).then_inc(hotT_sb, 1)
                        cols, per = WINDOW[L]
                        n = -(-G // per)
                        for c in range(n):
                            m = min(per, G - c * per)
                            act.wait_ge(rows_ps[L], k * n + c + 1)
                            nc.scalar.copy(gb[s][:, c * per:c * per + m, 0:cols],
                                           psM[1 + c % 3][:, 0:m * cols].rearrange("p (g c) -> p g c", g=m)).then_inc(rows_sb[L], 1)
                        if L == "l3":
                            relu_hidden(k)

                def relu_hidden(k):
                    for c in range(4):
                        m = min(4, G - 4 * c)
                        act.wait_ge(hidT_ps, k * 4 + c + 1)
                        nc.scalar.activation(hidT[:, c % 2, 0:m, :], psT[c % 2][:, 0:m * P].rearrange("p (g e) -> p g e", g=m), ACT.Relu).then_inc(hidT_sb, 1)

                def functions(i, s):
                    k = i * SLOTS + s
                    if L == "l1":
                        act.wait_ge(m_made, k + 1)
                        nc.scalar.activation(sg[s][:, :, :], sq[:, :, :], ACT.Sigmoid, scale=NORM_MSG).then_inc(sig_made, 1)
                    if L == "l2":
                        act.wait_ge(sq_made, k + 1)
                        nc.scalar.activation(sm[s][:, 2, :], sm[s][:, 1, :], ACT.Sqrt).then_inc(tanh_made, 1)
                        act.wait_ge(tanh_made, k * 2 + 1)
                        nc.scalar.activation(sm[s][:, 3, :], sm[s][:, 2, :], ACT.Tanh, scale=SC).then_inc(tanh_made, 1)
                    if L == "l3" and not windows:
                        relu_hidden(k)

                def one_hots(i, s):
                    k = i * SLOTS + s
                    n = 0
                    if full_tiles:
                        act.wait_ge(key_set[L], k * per_key + per_key)
                    for t in range(full_tiles):
                        if t % G >= ACT_TILES:
                            continue
                        act.wait_ge(tile_free[L], k * full_tiles + t + 1)
                        o = O[:, t % RING, 0:SCATTER[L][1]]
                        nc.scalar.activation(o, iota_r[:, 0:SCATTER[L][1]], ACT.Abs, scale=-1.0,
                                             bias=kf[s][:, 2 * (t // G) + 1, t % G:t % G + 1]).then_inc(tile_act[L], 1)
                        act.wait_ge(tile_act[L], k * acts_of(full_tiles) + 2 * n + 1)
                        nc.scalar.activation(o, o, ACT.Relu, scale=-1.0, bias=1.0).then_inc(tile_act[L], 1)
                        n += 1

                def functions_and_one_hots(i, s):
                    functions(i, s)
                    one_hots(i, s)

                if windows:
                    in_pairs(act, front, functions, early=one_hots)
                else:
                    in_pairs(act, front, functions_and_one_hots)

            act.wait_ge(zeroed, 2)
            for k, (W, root, b) in enumerate(((cW1, croot1, cb1), (cW2, croot2, cb2))):
                act.dma_start(wc[k][0:D, 0:REL * D].rearrange("i (r o) -> i r o", r=REL), W.rearrange("r i o -> i r o")).then_inc(weights_in, 16)
                act.dma_start(wc[k][0:D, REL * D:], root).then_inc(weights_in, 16)
                act.dma_start(wc[k][D:D + 1, REL * D:], b.rearrange("(a n) -> a n", a=1)).then_inc(weights_in, 16)
            act.dma_start(wl1[0:D, :], mtp.rearrange("i j h -> i (j h)")).then_inc(weights_in, 16)
            act.dma_start(wupd[0:D, :], utp.rearrange("i h k -> i (h k)")).then_inc(weights_in, 16)
            for w, dr in ((wlin, mlin), (wulin, ulin), (wloop, loopw)):
                act.dma_start(w[0:D, :], dr).then_inc(weights_in, 16)
            for k in range(2):
                act.dma_start(wpq[0:D, k * HID:(k + 1) * HID], sW1[k * D:(k + 1) * D, :]).then_inc(weights_in, 16)
                act.dma_start(w2[k * HID:(k + 1) * HID, (1 - k) * D:(2 - k) * D], sW2).then_inc(weights_in, 16)
            act.dma_start(wpq[D:D + 1, HID:], sb1.rearrange("(a n) -> a n", a=1)).then_inc(weights_in, 16)
            for k in range(2):
                act.dma_start(b2[:, k * D:(k + 1) * D], sb2.rearrange("(a n) -> a n", a=1).broadcast_to([P, D])).then_inc(weights_in, 16)

            act.wait_ge(flag_made, 1)
            nth_std = 0
            for L in LAYERS:
                if L == "cn":
                    two_paths(act, L, act_edges)
                    act_aggregate(L)
                    continue
                if L != "c2":
                    nth_std += 1
                    act.wait_ge(var_made, nth_std)
                    nc.scalar.activation(n2[:, :], n1[:, :], ACT.Sqrt).then_inc(std_made, 1)
                node_functions(act, L, "start")
                for k in range(NJ // 4):
                    act.wait_ge(xt_ps, xt_before[L] + k + 1)
                    nc.scalar.copy(XT[:, k * 4 * NP_:(k + 1) * 4 * NP_], psT[k % 2][0:D + 1, 0:4 * NP_]).then_inc(xt_sb, 1)
                if L != "l2":
                    cols, per = PROJ[L]
                    for k in range(-(-NJ // per)):
                        m = min(per, NJ - k * per)
                        act.wait_ge(proj_ps, proj_before[L] + k + 1)
                        pitch = W5W if L == "l3" else cols
                        rows = big[0:NP_, 0:NJ * pitch].rearrange("p (j c) -> p j c", j=NJ)
                        first = XD if L == "l3" else 0
                        nc.scalar.copy(rows[:, k * per:k * per + m, first:first + cols],
                                       psM[k % 4][0:NP_, 0:m * cols].rearrange("p (j c) -> p j c", j=m)).then_inc(proj_sb, 1)
                else:
                    act.sem_inc(rel_act, 2)
                    nc.scalar.copy(XTj[:, 0, :], XT[:, 0:NP_]).then_inc(xtj_set, 1)
                    with act.Fori(0, NJ // 2, 1) as i:
                        for h in range(2):
                            act.wait_ge(row_free[h], i + 1)
                            for c in range(0, EC, 2):
                                act.wait_ge(rel_ps, i * (2 * EC) + h * EC + c + 1)
                                nc.scalar.copy(big[0:NP_, (h * EC + c) * ECOLS:(h * EC + c + 1) * ECOLS], psM[c % 4][0:NP_, 0:ECOLS]).then_inc(rel_act, 1)
                                if c == 0:
                                    nc.scalar.copy(XTj[:, 1 - h, :], XT[:, bass.ds(i * (2 * NP_) + (h + 1) * NP_, NP_)]).then_inc(xtj_set, 1)
                node_functions(act, L, "table")
                two_paths(act, L, act_edges)
                act_aggregate(L)
                node_functions(act, L, "end")

        def second_layer(pe, k, c):
            m = min(4, G - 4 * c)
            pe.wait_ge(hidT_sb, k * 4 + c + 1)
            if c == 0:
                pe.wait_ge(v_read, k + 1)
            for g in range(m):
                last = nc.tensor.matmul(psV[:, (4 * c + g) * 2 * D:(4 * c + g + 1) * 2 * D], hidT[:, c % 2, g, :], w2[:, :], start=True, stop=True)
            last.then_inc(v_ps, 1)

        @block.tensor
        def _(pe):
            pe.wait_ge(ident_made, 2)
            pe.wait_ge(weights_in, 16 * WEIGHT_LOADS)

            pe.wait_ge(prep_dve, 1)
            nc.tensor.transpose(psT[0][0:GROUPS, 0:P], wa[:, :], ident[:, :]).then_inc(prep_pe, 1)
            pe.wait_ge(prep_dve, 2)
            pe.wait_ge(consts_made, 5)
            nc.tensor.matmul(psT[1][:, 0:GROUPS], ones[:, :], wb[0:GROUPS, :], start=True, stop=True).then_inc(prep_pe, 1)
            pe.wait_ge(prep_dve, 3)
            nc.tensor.transpose(psT[0][0:1, 0:P], wc_[:, 0:1], ident[:, :]).then_inc(prep_pe, 1)
            pe.wait_ge(flag_made, 1)

            def pe_edges(L, windows):
                q, r, d, per_edge = SCATTER[L]
                two_level = windows and L in BY_DST
                full_tiles = G * (per_edge - (1 if two_level else 0))
                if two_level:
                    pe.sem_inc(tile2_free[L], SLOTS)
                def front(i, s):
                    k = i * SLOTS + s
                    if not (windows and L in WINDOW):
                        return
                    pe.wait_ge(hot_made, groups_before[L] + k + 1)
                    for g in range(G):
                        last = nc.tensor.transpose(psTb[g // (G // 2)][:, (g % (G // 2)) * P:(g % (G // 2) + 1) * P],
                                                   hot[s][:, g, :], ident_b[:, :])
                        if g % (G // 2) == G // 2 - 1:
                            last.then_inc(hotT_ps, 1)
                    pe.wait_ge(win_split, groups_before[L] + k + 1)
                    cols, per = WINDOW[L]
                    n = -(-G // per)
                    for c in range(n):
                        if c == 0:
                            pe.wait_ge(rows_sb[L], k * n + 1)
                        if c >= 3:
                            pe.wait_ge(rows_sb[L], k * n + c - 1)
                        pe.wait_ge(hotT_sb, (groups_before[L] + k) * 2 + min(G - 1, (c + 1) * per - 1) // (G // 2) + 1)
                        for g in range(c * per, min(G, (c + 1) * per)):
                            for part in range(3):
                                last = nc.tensor.matmul(psM[1 + c % 3][:, (g - c * per) * cols:(g - c * per + 1) * cols],
                                                        hotT[s][:, g, :], win_parts[s][:, part, 0:cols], start=part == 0, stop=part == 2)
                        last.then_inc(rows_ps[L], 1)
                    if L == "l3":
                        hidden(i, s)

                def hidden(i, s):
                    k = i * SLOTS + s
                    if windows:
                        pe.wait_ge(gathered[L, s], i * (G * 16) + G * 16)
                    else:
                        pe.wait_ge(hid_made, k + 1)
                    for c in range(4):
                        m = min(4, G - 4 * c)
                        if c >= 2:
                            pe.wait_ge(hidT_sb, k * 4 + c - 1)
                        for g in range(m):
                            out = psT[c % 2][:, g * P:(g + 1) * P]
                            if windows:
                                nc.tensor.matmul(out, ga[s][:, 4 * c + g, XD:XD + 2 * HID], ident[:, :], start=True, stop=False, skip_group_check=True)
                                for part in range(3):
                                    last = nc.tensor.matmul(out, win_parts[s][:, part, XD + HID:XD + 3 * HID], hotT[s][:, 4 * c + g, :],
                                                            start=False, stop=part == 2, skip_group_check=True)
                            else:
                                last = nc.tensor.transpose(out, hid[:, 4 * c + g, :], ident[:, :])
                        last.then_inc(hidT_ps, 1)
                        if c >= 1:
                            second_layer(pe, k, c - 1)
                    second_layer(pe, k, 3)

                def back(i, s):
                    k = i * SLOTS + s
                    if L == "l3" and not windows:
                        hidden(i, s)
                    if two_level:
                        w = PARTS[L] * d
                        pe.wait_ge(parts_made[L], k + 1)
                        pe.wait_ge(wsum_read[L], k + 1)
                        for g in range(G):
                            last = nc.tensor.matmul(psM[0][:, 0:w], hot[s][:, g, :], msg_parts[s][:, g, 0:w], start=g == 0, stop=g == G - 1)
                        last.then_inc(wsum_ps[L], 1)
                    n = 0
                    for t in range(full_tiles):
                        pe.wait_ge(tile_ready[L], k * ready_before(full_tiles - 1) + ready_before(t))
                        if t % G < ACT_TILES:
                            n += 2
                            pe.wait_ge(tile_act[L], k * acts_of(full_tiles) + n)
                        nc.tensor.matmul(agg[0:q * d, 0:r], S[:, t % RING, 0:q * d], O[:, t % RING, 0:r], start=False, stop=False,
                                         skip_group_check=True).then_inc(tile_free[L], 1)
                    if two_level:
                        pe.wait_ge(tile2_ready[L], k * 2 + 2)
                        nc.tensor.matmul(agg[0:q * d, 0:r], S2[s][:, 0:q * d], O2[s][:, 0:r], start=False, stop=False,
                                         skip_group_check=True).then_inc(tile2_free[L], 1)

                in_pairs(pe, front, back)

            lin = [0, 0]

            def linear(src17, w):
                pe.wait_ge(lin_in, lin[1] + 1)
                for k in range(NJ // 4):
                    if k >= 2:
                        pe.wait_ge(lin_sb, lin[0] + k - 1)
                    for j in range(4):
                        last = nc.tensor.transpose(psT[k % 2][0:D + 1, j * NP_:(j + 1) * NP_], src17[:, 4 * k + j, 0:D + 1], ident[0:NP_, 0:NP_])
                    last.then_inc(lin_ps, 1)
                pe.wait_ge(lin_sb, lin[0] + NJ // 4)
                for j in range(NJ):
                    last = nc.tensor.matmul(psV[0:NP_, j * D:(j + 1) * D], XT[:, j * NP_:(j + 1) * NP_], w[:, :], start=True, stop=True)
                last.then_inc(lin_mm, 1)
                lin[0] += NJ // 4
                lin[1] += 1

            def pe_scatter(L):
                q, r, d, per_edge = SCATTER[L]
                nc.tensor.matmul(agg[0:q * d, 0:r], zeros[:, 0:q * d], zeros[:, 0:r], start=True, stop=False,
                                 skip_group_check=True).then_inc(tile_free[L], RING)
                two_paths(pe, L, pe_edges)
                nc.tensor.matmul(agg[0:q * d, 0:r], zeros[:, 0:q * d], zeros[:, 0:r], start=False, stop=True,
                                 skip_group_check=True).then_inc(agg_done, 1)
                pe.wait_ge(agg_sb, nth[L])
                for c in range(4):
                    last = nc.tensor.transpose(psT[0][0:r // 4, c * q * d:(c + 1) * q * d], AG[0:q * d, c * (r // 4):(c + 1) * (r // 4)],
                                               ident[0:q * d, 0:q * d])
                last.then_inc(aggT, 1)

            for L in LAYERS:
                if L == "cn":
                    pe_scatter(L)
                    continue
                pe.wait_ge(xt_in, nth_xt[L])
                for k in range(NJ // 4):
                    if k >= 2:
                        pe.wait_ge(xt_sb, xt_before[L] + k - 1)
                    for j in range(4):
                        last = nc.tensor.transpose(psT[k % 2][0:D + 1, j * NP_:(j + 1) * NP_],
                                                   (HT if L == "l2" else H17)[:, 4 * k + j, :], ident[0:NP_, 0:NP_])
                    last.then_inc(xt_ps, 1)
                pe.wait_ge(xt_sb, xt_before[L] + NJ // 4)
                if L != "l2":
                    cols, per = PROJ[L]
                    w = {"c1": wc[0], "c2": wc[1], "l1": wl1, "l3": wpq}[L]
                    for k in range(-(-NJ // per)):
                        if k >= 4:
                            pe.wait_ge(proj_sb, proj_before[L] + k - 3)
                        for j in range(k * per, min(NJ, (k + 1) * per)):
                            last = nc.tensor.matmul(psM[k % 4][0:NP_, (j % per) * cols:(j % per + 1) * cols],
                                                    XT[:, j * NP_:(j + 1) * NP_], w[:, :], start=True, stop=True)
                        last.then_inc(proj_ps, 1)
                else:
                    for j in range(NJ):
                        last = nc.tensor.matmul(psV[0:NP_, j * D:(j + 1) * D], XT[:, j * NP_:(j + 1) * NP_], wloop[:, :], start=True, stop=True)
                    last.then_inc(loop_ps, 1)
                    pe.wait_ge(wrel_in, 32)
                    with pe.Fori(0, NJ // 2, 1) as i:
                        for h in range(2):
                            pe.wait_ge(xtj_set, i * 2 + h + 1)
                            for c in range(EC):
                                pe.wait_ge((rel_act, rel_dve)[c % 2], i * EC + h * (EC // 2) + c // 2 + 1)
                                last = nc.tensor.matmul(psM[c % 4][0:NP_, 0:ECOLS], XTj[:, h, :], wrel[:, c * ECOLS:(c + 1) * ECOLS],
                                                        start=True, stop=True)
                                last.then_inc(rel_ps, 1)
                pe_scatter(L)
                if L == "l1":
                    linear(HT, wlin)
                    pe.wait_ge(lin_in, lin[1] + 1)
                    for k in range(NJ // 4):
                        if k >= 2:
                            pe.wait_ge(lin_sb, lin[0] + k - 1)
                        for j in range(4):
                            last = nc.tensor.transpose(psT[k % 2][0:D + 1, j * NP_:(j + 1) * NP_], H17[:, 4 * k + j, :], ident[0:NP_, 0:NP_])
                        last.then_inc(lin_ps, 1)
                    pe.wait_ge(lin_sb, lin[0] + NJ // 4)
                    lin[0] += NJ // 4
                    lin[1] += 1
                    for j in range(NJ):
                        if j >= 4:
                            pe.wait_ge(upd_read, j - 3)
                        nc.tensor.matmul(psM[j % 4][0:NP_, 0:D * D], XT[:, j * NP_:(j + 1) * NP_], wupd[:, :], start=True, stop=True).then_inc(upd_ps, 1)
                    linear(HT, wulin)

        def relay_back(dve, v, link, L, turn):
            q, r, d, _ = SCATTER[L]
            dve.wait_ge(aggT, nth[L])
            v.tensor_copy(AGT[:, :, 0:d].rearrange("p (q c) d -> p q c d", q=q),
                          psT[0][0:CHUNK7, 0:4 * q * d].rearrange("p (c q d) -> p q c d", c=4, q=q)).then_inc(relay_made, 1)
            dve.wait_ge(relay_in, 16 * turn)


        @block.vector
        def _(dve):
            v = nc.vector
            step = [0, None, 0]

            def link(ins):
                if step[1] is None:
                    step[0] += 1
                    ins.then_inc(dve_step, 1)
                    dve.wait_ge(dve_step, step[0])
                else:
                    counter, before = step[1]
                    step[2] += 1
                    ins.then_inc(counter, 1)
                    dve.wait_ge(counter, before + step[2])

            def bc(ap2, n, d):
                return ap2.rearrange("p (n a) -> p n a", a=1).broadcast_to([ap2.shape[0], n, d])

            def tt(o, a, b, op):
                link(v.tensor_tensor(o, a, b, op))

            def ts(o, a, s1, op0, s2=None, op1=None):
                link(v.tensor_scalar(o, a, s1, s2, op0, op1) if op1 is not None else v.tensor_scalar(o, a, s1, None, op0))

            def red(o, a, op=ALU.add):
                link(v.tensor_reduce(o, a, axis=AX, op=op))

            for free in (rows_used, *key_used.values()):
                dve.sem_inc(free, SLOTS)
            for t in (src_i, dst_i, rel_row, type_row, X):
                link(v.memset(t[tuple(slice(None) for _ in t.shape)], 0))
            link(v.memset(ea_sb[:, :, :], 0.0))
            v.memset(zeros[:, 0:1], 0.0).then_inc(zeroed, 1)
            for t in (wc[0], wc[1], wl1, wupd, wlin, wulin, wloop, wpq, w2):
                link(v.memset(t[:, :], 0.0))
            link(v.memset(H17[:, :, D:D + 1], 1.0))
            link(v.memset(HT[:, :, :], 1.0))
            link(v.memset(XT[:, NPAD:], 0.0))
            for s in range(SLOTS):
                link(v.memset(msg[s][:, :, :, D:D + 1], 1.0))
            v.memset(zeros[:, :], 0.0).then_inc(zeroed, 1)
            dve.wait_ge(zeroed, 2)

            sf, df, pad, hi, lo, t_f, t_l, t_m = (big[:, k * T:(k + 1) * T] for k in range(8))

            def grp(a):
                return a.rearrange("p (k g) -> p k g", g=G)

            dve.wait_ge(consts_made, 5)
            dve.wait_ge(edges_in, 16 * 12)
            ts(pad, lane, float(E), ALU.is_ge, PAD_KEY, ALU.mult)
            link(v.tensor_copy(sf, src_i[:, :]))
            link(v.tensor_copy(df, dst_i[:, :]))
            link(v.tensor_copy(t_f, rel_row[:, :]))

            def split(val, q, r):
                ts(hi, val, float(r), ALU.is_ge)
                for k in range(2, q):
                    link(v.scalar_tensor_tensor(out=hi, in0=val, scalar=float(k * r), in1=hi, op0=ALU.is_ge, op1=ALU.add))
                link(v.scalar_tensor_tensor(out=lo, in0=hi, scalar=float(-r), in1=val, op0=ALU.mult, op1=ALU.add))

            for name, val, q, r in (("src8", sf, Q8, R8), ("src7", sf, Q7, R7), ("dst7", df, Q7, R7), ("dst8", df, Q8, R8)):
                split(val, q, r)
                link(v.tensor_tensor(keys[name][:, :, 0, :], grp(hi), grp(pad), ALU.add))
                link(v.tensor_copy(keys[name][:, :, 1, :], grp(lo)))
            link(v.tensor_copy(typ[:, :, :], grp(t_f)))
            link(v.scalar_tensor_tensor(out=rel_row[:, :], in0=sf, scalar=float(REL), in1=t_f, op0=ALU.mult, op1=ALU.add))
            link(v.tensor_copy(t_f, type_row[:, :]))
            link(v.scalar_tensor_tensor(out=type_row[:, :], in0=sf, scalar=float(TYPES), in1=t_f, op0=ALU.mult, op1=ALU.add))

            link(v.scalar_tensor_tensor(out=t_l, in0=pad, scalar=-4.0, in1=df, op0=ALU.mult, op1=ALU.add))
            v.tensor_reduce(wa[:, :], grp(t_l), axis=AX, op=ALU.min).then_inc(prep_dve, 1)
            dve.wait_ge(ident_made, 2)
            link(v.tensor_copy(ident_b[:, :], ident[:, :]))
            dve.wait_ge(prep_pe, 1)
            red(wc_[0:GROUPS, 0:1], psT[0][0:GROUPS, 0:P], ALU.min)
            ts(wc_[0:GROUPS, 0:1], wc_[0:GROUPS, 0:1], float(NPAD - WIN), ALU.min)
            v.tensor_scalar(wb[0:GROUPS, :], ident[0:GROUPS, 0:GROUPS], wc_[0:GROUPS, 0:1], None, ALU.mult).then_inc(prep_dve, 1)
            dve.wait_ge(prep_pe, 2)
            link(v.tensor_copy(wa[:, :], psT[1][:, 0:GROUPS]))
            tt(grp(t_l), grp(df), wa[:, :].rearrange("p (k a) -> p k a", a=1).broadcast_to([P, GROUPS, G]), ALU.subtract)
            tt(t_l, t_l, pad, ALU.add)
            link(v.tensor_copy(loc[:, :, :], grp(t_l)))
            v.tensor_reduce(wc_[:, 0:1], t_l, axis=AX, op=ALU.max).then_inc(prep_dve, 1)
            ts(wb[:, :], wa[:, :], iota_p[:, 0:1], ALU.add)
            link(v.tensor_copy(win_row[:, :], wb[:, :]))
            for name, q, r in (("8", Q8, R8), ("7", Q7, R7)):
                key = win_key[name]
                ts(key[:, :, 0], wb[:, :], float(r), ALU.is_ge)
                for n in range(2, q):
                    link(v.scalar_tensor_tensor(out=key[:, :, 0], in0=wb[:, :], scalar=float(n * r), in1=key[:, :, 0], op0=ALU.is_ge, op1=ALU.add))
                link(v.scalar_tensor_tensor(out=key[:, :, 1], in0=key[:, :, 0], scalar=float(-r), in1=wb[:, :], op0=ALU.mult, op1=ALU.add))
            dve.wait_ge(prep_pe, 3)
            red(n1[0:1, 0:1], psT[0][0:1, 0:P], ALU.max)
            v.tensor_scalar(flag[:, :], n1[0:1, 0:1], float(WIN - 1), None, ALU.is_gt).then_inc(flag_made, 1)
            dve.wait_ge(flag_made, 1)

            n_std = [0]
            n_act = [0]
            n_lin = [0]

            def relu_layernorm(dest):
                red(n3[:, :], X[:, :, :])
                ts(n3[:, :], n3[:, :], 1.0 / D, ALU.mult)
                tt(A[:, :, :], X[:, :, :], bc(n3[:, :], NJ, D), ALU.subtract)
                tt(B[:, :, :], A[:, :, :], A[:, :, :], ALU.mult)
                red(n4[:, :], B[:, :, :])
                v.tensor_scalar(n1[:, :], n4[:, :], 1.0 / D, 1e-5, ALU.mult, ALU.add).then_inc(var_made, 1)
                n_std[0] += 1
                dve.wait_ge(std_made, n_std[0])
                link(v.reciprocal(n3[:, :], n2[:, :]))
                tt(A[:, :, :], A[:, :, :], bc(n3[:, :], NJ, D), ALU.mult)
                ts(dest, A[:, :, :], 0.0, ALU.max)

            def call_act():
                n_act[0] += 1
                dve.sem_inc(act_in, 1)
                dve.wait_ge(act_out, n_act[0])

            def norm_of(o, val, sq_buf=B):
                tt(sq_buf[:, :, :], val, val, ALU.mult)
                red(o, sq_buf[:, :, :])

            def fill_tiles(L, i, s, a, of):
                q, r, d, per_edge = SCATTER[L]
                for g in range(G):
                    dve.wait_ge(tile_free[L], i * (SLOTS * of * G) + (s * of + a) * G + g + 1)
                    v.scalar_tensor_tensor(
                        out=S[:, g % RING, 0:q * d].rearrange("p (q d) -> p q d", q=q), in0=bc(iota_q[:, 0:q], q, d),
                        scalar=kf[s][:, 2 * a, g:g + 1],
                        in1=msg[s][:, a, g, 0:d].rearrange("p (a d) -> p a d", a=1).broadcast_to([P, q, d]),
                        op0=ALU.is_equal, op1=ALU.mult).then_inc(tile_ready[L], 1)
                    if g >= ACT_TILES:
                        v.tensor_scalar(O[:, g % RING, 0:r], iota_r[:, 0:r], kf[s][:, 2 * a + 1, g:g + 1], None,
                                        ALU.is_equal).then_inc(tile_ready[L], 1)
                dve.wait_ge(tile_ready[L], (i * SLOTS + s) * ready_before(of * G - 1) + ready_before((a + 1) * G - 1))
                dve.wait_ge(tile_act[L], (i * SLOTS + s) * acts_of(of * G) + acts_of((a + 1) * G))

            def split3(parts, val, rest):
                link(v.tensor_copy(parts[0], val))
                tt(rest, val, parts[0], ALU.subtract)
                link(v.tensor_copy(parts[1], rest))
                tt(parts[2], rest, parts[1], ALU.subtract)

            steps_before = [0]

            def dve_edges(L, windows):
                q, r, d, per_edge = SCATTER[L]
                two_level = windows and L in BY_DST
                windowed = windows and L in WINDOW
                gathers = {"cn": 0, "c1": 2, "c2": 1, "l1": 1, "l2": 1, "l3": 2}[L] - (1 if windowed else 0)
                per_key = 2 if L == "l3" else 1
                scatters = range(per_edge - (1 if two_level else 0))
                steps_front = 4 if windowed else 1 if two_level else 0
                steps_back = ({"cn": 1, "c1": 5, "c2": 1, "l1": 2, "l2": 10, "l3": 22 if windows else 23}[L]
                              + ((1 + (4 if PARTS[L] == 3 else 0)) if two_level else 0))
                if two_level:
                    dve.sem_inc(wsum_read[L], 1)
                if L == "l3":
                    dve.sem_inc(v_read, 1)

                def front(i, s):
                    k = i * SLOTS + s
                    group = bass.ds(k, 1)
                    step[1:] = [(step_front, steps_before[0] + k * steps_front), 0]
                    if windows and (two_level or L in WINDOW):
                        made = v.tensor_tensor(hot[s][:, :, :], iota_r[:, 0:WIN].rearrange("p (a n) -> p a n", a=1).broadcast_to([P, G, WIN]),
                                               loc[:, group, :].rearrange("p a (g b) -> p (a g) b", b=1).broadcast_to([P, G, WIN]), ALU.is_equal)
                        if L in WINDOW:
                            made.then_inc(hot_made, 1)
                        else:
                            link(made)
                    if windows and L in WINDOW:
                        cols, per = WINDOW[L]
                        dve.wait_ge(win_in[L, s], i * 16 + 16)
                        split3([win_parts[s][:, n, 0:WIN_COLS[L]] for n in range(3)], win[s][:, 0:WIN_COLS[L]], win[s][:, 0:WIN_COLS[L]])
                        dve.sem_inc(win_split, 1)
                    assert step[2] == steps_front, (L, windows, step[2])

                def back(i, s):
                    k = i * SLOTS + s
                    here = bass.ds(i * (SLOTS * G) + s * G, G)
                    group = bass.ds(k, 1)
                    m = msg[s]
                    step[1:] = [(step_of[L], k * steps_back), 0]
                    if gathers:
                        dve.wait_ge(gathered[L, s], i * (gathers * G * 16) + gathers * G * 16)
                    if windows and L in WINDOW:
                        n = -(-G // WINDOW[L][1])
                        dve.wait_ge(rows_sb[L], k * n + n + 1)
                    if L == "cn":
                        tt(msg_parts[s][:, :, 0:REL] if windows else m[:, 0, :, 0:REL], *type_hot(group), ALU.is_equal)
                    if L == "c1":
                        tt(res[:, :, 0:REL], *type_hot(group), ALU.is_equal)
                        tt(res[:, :, 0:REL], res[:, :, 0:REL], gb[s][:, :, 0:REL], ALU.mult)
                        red(sm[s][:, 0, :], res[:, :, 0:REL])
                        link(v.tensor_copy(norm_sb[:, here], sm[s][:, 0, :]))
                        tt(m[:, 0, :, 0:D], ga[s][:, :, 0:D], bc(sm[s][:, 0, :], G, D), ALU.mult)
                    if L == "c2":
                        tt(m[:, 0, :, 0:D], ga[s][:, :, 0:D], norm_sb[:, here].rearrange("p (g a) -> p g a", a=1).broadcast_to([P, G, D]), ALU.mult)
                    if L == "l1":
                        z = gb[s][:, :, 0:DE * D].rearrange("p g (j h) -> p g j h", j=DE)
                        tt(z, z, ea_sb[:, here, :].rearrange("p g (j a) -> p g j a", a=1).broadcast_to([P, G, DE, D]), ALU.mult)
                        v.tensor_reduce(sq[:, :, :], z.rearrange("p g j h -> p g h j"), axis=AX, op=ALU.add).then_inc(m_made, 1)
                        dve.wait_ge(sig_made, k + 1)
                        link(v.scalar_tensor_tensor(out=m[:, 0, :, 0:D], in0=sq[:, :, :], scalar=NORM_MSG, in1=sg[s][:, :, :], op0=ALU.mult, op1=ALU.mult))
                    if L == "l2":
                        hyperbolic_messages(i, s, k, m)
                    if L == "l3":
                        sheaf_messages(i, s, k, m, windows)
                    if two_level:
                        if PARTS[L] == 3:
                            split3([msg_parts[s][:, :, n * d:(n + 1) * d] for n in range(3)], m[:, per_edge - 1, :, 0:d], res[:, :, 0:d])
                        dve.sem_inc(parts_made[L], 1)
                    dve.sem_inc(rows_used, 1)
                    dve.wait_ge(key_set[L], k * per_key + per_key)
                    for a in scatters:
                        fill_tiles(L, i, s, a, len(scatters))
                    if two_level:
                        dve.wait_ge(wsum_ps[L], k + 1)
                        red(wsum[s][:, 0:d], psM[0][:, 0:PARTS[L] * d].rearrange("p (n d) -> p d n", d=d))
                        dve.sem_inc(wsum_read[L], 1)
                        dve.wait_ge(tile2_free[L], k + 1)
                        v.scalar_tensor_tensor(
                            out=S2[s][:, 0:q * d].rearrange("p (q d) -> p q d", q=q), in0=bc(iota_q[:, 0:q], q, d), scalar=kw[s][:, 0, 0:1],
                            in1=wsum[s][:, 0:d].rearrange("p (a d) -> p a d", a=1).broadcast_to([P, q, d]),
                            op0=ALU.is_equal, op1=ALU.mult).then_inc(tile2_ready[L], 1)
                        v.tensor_scalar(O2[s][:, 0:r], iota_r[:, 0:r], kw[s][:, 0, 1:2], None, ALU.is_equal).then_inc(tile2_ready[L], 1)
                        dve.wait_ge(tile2_ready[L], k * 2 + 2)
                    dve.sem_inc(key_used[L], 1)
                    assert step[2] == steps_back, (L, windows, step[2])

                in_pairs(dve, front, back)
                if windows:
                    steps_before[0] += GROUPS * steps_front
                step[1:] = [None, 0]

            def type_hot(group):
                return (iota_q[:, :].rearrange("p (a t) -> p a t", a=1).broadcast_to([P, G, REL]),
                        typ[:, group, :].rearrange("p a (g b) -> p (a g) b", b=1).broadcast_to([P, G, REL]))

            def edge_pass(L):
                two_paths(dve, L, dve_edges)

            def hyperbolic_messages(i, s, k, m):
                row, z = ga[s][:, :, 0:D], sm[s]
                tt(sq[:, :, :], row, row, ALU.mult)
                red(z[:, 0, :], sq[:, :, :])
                v.tensor_scalar(z[:, 1, :], z[:, 0, :], 1e-10, None, ALU.max).then_inc(sq_made, 1)
                dve.wait_ge(tanh_made, k * 2 + 2)
                ts(z[:, 4, :], z[:, 2, :], SC, ALU.mult)
                link(v.reciprocal(z[:, 4, :], z[:, 4, :]))
                tt(z[:, 4, :], z[:, 4, :], z[:, 3, :], ALU.mult)
                tt(z[:, 5, :], z[:, 4, :], z[:, 4, :], ALU.mult)
                tt(z[:, 5, :], z[:, 5, :], z[:, 0, :], ALU.mult)
                ts(z[:, 5, :], z[:, 5, :], -0.5 * C, ALU.mult, 0.5 * (1.0 + EPS), ALU.add)
                link(v.reciprocal(m[:, 0, :, D], z[:, 5, :]))
                tt(z[:, 4, :], z[:, 4, :], m[:, 0, :, D], ALU.mult)
                v.tensor_tensor(m[:, 0, :, 0:D], row, bc(z[:, 4, :], G, D), ALU.mult).then_inc(hyp_made, 1)
                dve.wait_ge(hyp_made, k + 1)

            def sheaf_messages(i, s, k, m, windows):
                rs, rd, z = ga[s], gb[s], sm[s]
                if not windows:
                    p_, q_ = slice(XD, XD + HID), slice(XD + HID, XD + 2 * HID)
                    tt(hid[:, :, 0:HID], rs[:, :, p_], rd[:, :, q_], ALU.add)
                    v.tensor_tensor(hid[:, :, HID:], rd[:, :, p_], rs[:, :, q_], ALU.add).then_inc(hid_made, 1)
                dve.wait_ge(v_ps, k * 4 + 4)
                tt(vec[:, :, :, :].rearrange("p g a d -> p g (a d)"), psV[:, 0:G * 2 * D].rearrange("p (g c) -> p g c", g=G),
                   b2[:, :].rearrange("p (a c) -> p a c", a=1).broadcast_to([P, G, 2 * D]), ALU.add)
                dve.sem_inc(v_read, 1)
                whole = lambda t: t[:, :, :, :].rearrange("p g a d -> p (g a) d")
                tt(whole(sq2), whole(vec), whole(vec), ALU.mult)
                red(c2[:, 0, :], whole(sq2))
                ts(c2[:, 0, :], c2[:, 0, :], 1e-24, ALU.max, 0.5, ALU.mult)
                link(v.reciprocal(c2[:, 0, :], c2[:, 0, :]))
                x_of = (rd[:, :, 0:D], rs[:, :, 0:D])
                coef = lambda n, a: c2[:, n, :].rearrange("p (g a) -> p g a", a=2)[:, :, a]
                for a in range(2):
                    tt(sq2[:, :, a, :], vec[:, :, a, :], x_of[a], ALU.mult)
                red(c2[:, 1, :], whole(sq2))
                tt(c2[:, 1, :], c2[:, 1, :], c2[:, 0, :], ALU.mult)
                tt(whole(sq2), whole(vec), bc(c2[:, 1, :], 2 * G, D), ALU.mult)
                for a in range(2):
                    tt(y2[:, :, a, :], x_of[a], sq2[:, :, a, :], ALU.subtract)
                for a in range(2):
                    tt(sq2[:, :, a, :], vec[:, :, 1 - a, :], y2[:, :, a, :], ALU.mult)
                red(c2[:, 1, :], whole(sq2))
                for a in range(2):
                    tt(coef(1, a), coef(1, a), coef(0, 1 - a), ALU.mult)
                for a in range(2):
                    tt(sq2[:, :, a, :], vec[:, :, 1 - a, :], c2[:, 1, :].rearrange("p (g a b) -> p g a b", a=2, b=1)[:, :, a, :].broadcast_to([P, G, D]), ALU.mult)
                tt(whole(y2), whole(y2), whole(sq2), ALU.subtract)
                for a in range(2):
                    tt(m[:, a, :, 0:D], y2[:, :, a, :], (rd, rs)[a][:, :, D:D + 1].broadcast_to([P, G, D]), ALU.mult)

            def agg_nodes(L):
                return psT[0][0:CHUNK8, 0:4 * Q8 * D].rearrange("p (c q d) -> p q c d", c=4, q=Q8)

            def j4(t):
                return t[:, :, 0:D].rearrange("p (q c) d -> p q c d", q=Q8)

            rows = lambda pitch: big[0:NP_, 0:NJ * pitch].rearrange("p (j c) -> p j c", j=NJ)

            dve.wait_ge(x_in, 32)
            edge_pass("cn")
            dve.wait_ge(aggT, nth["cn"])
            link(v.tensor_copy(cnt[:, :, :].rearrange("p (q c) t -> p q c t", q=Q8),
                               psT[0][0:CHUNK8, 0:4 * Q8 * REL].rearrange("p (c q t) -> p q c t", c=4, q=Q8)))
            red(deg_dst[:, :], cnt[:, :, :])
            ts(cnt[:, :, :], cnt[:, :, :], 1.0, ALU.max)
            v.reciprocal(cnt[:, :, :], cnt[:, :, :]).then_inc(norm_made, 1)
            for L in ("c1", "c2"):
                if L == "c1":
                    relu_layernorm(H17[:, :, 0:D])
                dve.sem_inc(xt_in, 1)
                dve.wait_ge(proj_sb, proj_before[L] + proj_banks[L])
                dve.sem_inc(table_made, 1)
                link(v.tensor_copy(A[:, :, :], rows(REL * D + D)[:, :, REL * D:]))
                edge_pass(L)
                dve.wait_ge(aggT, nth[L])
                tt(j4(B), agg_nodes(L), j4(A), ALU.add)
                if L == "c1":
                    ts(H17[:, :, 0:D], B[:, :, :], 0.0, ALU.max)
            red(n3[:, :], B[:, :, :], ALU.max)
            tt(B[:, :, :], B[:, :, :], bc(n3[:, :], NJ, D), ALU.subtract)
            call_act()
            red(n1[:, :], C_[:, :, :])
            call_act()
            tt(B[:, :, :], B[:, :, :], bc(n2[:, :], NJ, D), ALU.subtract)
            tt(X[:, :, :], X[:, :, :], B[:, :, :], ALU.add)

            L = "l1"
            relu_layernorm(H17[:, :, 0:D])
            dve.sem_inc(xt_in, 1)
            dve.wait_ge(proj_sb, proj_before[L] + proj_banks[L])
            dve.sem_inc(table_made, 1)
            dve.wait_ge(ea_in, 48)
            edge_pass(L)
            relay_back(dve, v, link, L, 1)
            link(v.tensor_copy(degs[:, :], AGR[:, :, D]))
            link(v.tensor_copy(HT[:, :, 0:D], AGR[:, :, 0:D]))
            dve.sem_inc(lin_in, 1)
            dve.wait_ge(lin_mm, 1)
            psVn = psV[0:NP_, 0:NJ * D].rearrange("p (j d) -> p j d", j=NJ)
            ts(A[:, :, :], psVn, NORM_LIN, ALU.mult)
            dve.sem_inc(lin_in, 1)
            for j in range(NJ):
                dve.wait_ge(upd_ps, j + 1)
                v.tensor_tensor(prod[:, j % 2, :].rearrange("p (h k) -> p h k", h=D), psM[j % 4][0:NP_, 0:D * D].rearrange("p (h k) -> p h k", h=D),
                                A[:, j, :].rearrange("p (h a) -> p h a", a=1).broadcast_to([NP_, D, D]), ALU.mult).then_inc(upd_read, 1)
                dve.wait_ge(upd_read, j + 1)
                link(v.tensor_reduce(B[:, j, :], prod[:, j % 2, :].rearrange("p (h k) -> p k h", h=D), axis=AX, op=ALU.add))
            call_act()
            link(v.scalar_tensor_tensor(out=HT[:, :, 0:D], in0=B[:, :, :], scalar=NORM_UPD, in1=C_[:, :, :], op0=ALU.mult, op1=ALU.mult))
            dve.sem_inc(lin_in, 1)
            tt(X[:, :, :], X[:, :, :], H17[:, :, 0:D], ALU.add)
            dve.wait_ge(lin_mm, 2)
            link(v.scalar_tensor_tensor(out=X[:, :, :], in0=psVn, scalar=NORM_LIN, in1=X[:, :, :], op0=ALU.mult, op1=ALU.add))

            L = "l2"
            relu_layernorm(H17[:, :, 0:D])
            norm_of(n1[:, :], H17[:, :, 0:D])
            ts(n1[:, :], n1[:, :], 1e-10, ALU.max)
            call_act()
            ts(n2[:, :], n2[:, :], SC, ALU.mult)
            ts(n3[:, :], n2[:, :], -1.0 + BALL, ALU.max, 1.0 - BALL, ALU.min)
            tt(n4[:, :], n3[:, :], n3[:, :], ALU.mult)
            ts(n5[:, :], n4[:, :], 1.0 / 23, ALU.mult, 1.0 / 21, ALU.add)
            for t in range(19, 0, -2):
                tt(n5[:, :], n5[:, :], n4[:, :], ALU.mult)
                ts(n5[:, :], n5[:, :], 1.0 / t, ALU.add)
            tt(HT[:, :, 0:D], H17[:, :, 0:D], bc(n5[:, :], NJ, D), ALU.mult)
            dve.sem_inc(xt_in, 1)
            dve.wait_ge(loop_ps, 1)
            link(v.tensor_copy(V[:, :, :], psVn))
            dve.sem_inc(rel_dve, 2)
            with dve.Fori(0, NJ // 2, 1) as i:
                for h in range(2):
                    dve.wait_ge(row_free[h], i + 1)
                    for c in range(1, EC, 2):
                        dve.wait_ge(rel_ps, i * (2 * EC) + h * EC + c + 1)
                        v.tensor_copy(big[0:NP_, (h * EC + c) * ECOLS:(h * EC + c + 1) * ECOLS], psM[c % 4][0:NP_, 0:ECOLS]).then_inc(rel_dve, 1)
            edge_pass(L)
            relay_back(dve, v, link, L, 2)
            deg = deg_dst[:, :]
            ts(n1[:, :], deg, 1.0, ALU.max)
            call_act()
            link(v.reciprocal(n2[:, :], n2[:, :]))
            tt(n3[:, :], deg, n2[:, :], ALU.mult)
            ts(n3[:, :], n3[:, :], EPS, ALU.add)
            link(v.reciprocal(n3[:, :], n3[:, :]))
            tt(n3[:, :], n3[:, :], n2[:, :], ALU.mult)
            tt(n4[:, :], n3[:, :], AGR[:, :, D], ALU.mult)
            ts(n4[:, :], n4[:, :], EPS, ALU.add)
            link(v.reciprocal(n4[:, :], n4[:, :]))
            tt(A[:, :, :], AGR[:, :, 0:D], bc(n3[:, :], NJ, D), ALU.mult)
            tt(A[:, :, :], A[:, :, :], bc(n4[:, :], NJ, D), ALU.mult)
            tt(degs[:, :], degs[:, :], deg, ALU.add)
            norm_of(n1[:, :], A[:, :, :])
            ts(n1[:, :], n1[:, :], 1e-10, ALU.max)
            call_act()
            link(v.reciprocal(n2[:, :], n2[:, :]))
            ts(n2[:, :], n2[:, :], (1.0 - BALL) / SC, ALU.mult, 1.0, ALU.min)
            tt(A[:, :, :], A[:, :, :], bc(n2[:, :], NJ, D), ALU.mult)
            norm_of(n1[:, :], V[:, :, :])
            ts(n1[:, :], n1[:, :], 1e-10, ALU.max)
            call_act()
            ts(n2[:, :], n2[:, :], SC, ALU.mult)
            call_act()
            link(v.reciprocal(n2[:, :], n2[:, :]))
            tt(n3[:, :], n3[:, :], n2[:, :], ALU.mult)
            tt(V[:, :, :], V[:, :, :], bc(n3[:, :], NJ, D), ALU.mult)
            norm_of(n1[:, :], A[:, :, :])
            norm_of(n2[:, :], V[:, :, :])
            tt(B[:, :, :], A[:, :, :], V[:, :, :], ALU.mult)
            red(n3[:, :], B[:, :, :])
            ts(n3[:, :], n3[:, :], 2.0 * C, ALU.mult, 1.0, ALU.add)
            link(v.scalar_tensor_tensor(out=n4[:, :], in0=n2[:, :], scalar=C, in1=n3[:, :], op0=ALU.mult, op1=ALU.add))
            ts(n5[:, :], n1[:, :], -C, ALU.mult, 1.0, ALU.add)
            tt(n6[:, :], n1[:, :], n2[:, :], ALU.mult)
            link(v.scalar_tensor_tensor(out=n6[:, :], in0=n6[:, :], scalar=C * C, in1=n3[:, :], op0=ALU.mult, op1=ALU.add))
            ts(n6[:, :], n6[:, :], 1e-10, ALU.max)
            link(v.reciprocal(n6[:, :], n6[:, :]))
            tt(A[:, :, :], A[:, :, :], bc(n4[:, :], NJ, D), ALU.mult)
            tt(V[:, :, :], V[:, :, :], bc(n5[:, :], NJ, D), ALU.mult)
            tt(A[:, :, :], A[:, :, :], V[:, :, :], ALU.add)
            tt(A[:, :, :], A[:, :, :], bc(n6[:, :], NJ, D), ALU.mult)
            tt(X[:, :, :], X[:, :, :], A[:, :, :], ALU.add)

            L = "l3"
            relu_layernorm(H17[:, :, 0:D])
            dve.sem_inc(xt_in, 1)
            ts(n1[:, :], degs[:, :], 1e-5, ALU.max)
            dve.wait_ge(proj_sb, proj_before[L] + proj_banks[L])
            call_act()
            link(v.reciprocal(n2[:, :], n2[:, :]))
            link(v.tensor_copy(rows(W5W)[:, :, 0:D], H17[:, :, 0:D]))
            link(v.tensor_copy(rows(W5W)[:, :, D], n2[:, :]))
            link(v.tensor_copy(rows(W5W)[:, :, W5:], rows(W5W)[:, :, XD:XD + HID]))
            dve.sem_inc(table_made, 1)
            edge_pass(L)
            dve.wait_ge(aggT, nth[L])
            link(v.tensor_copy(j4(A), agg_nodes(L)))
            tt(A[:, :, :], A[:, :, :], bc(n2[:, :], NJ, D), ALU.mult)
            tt(A[:, :, :], A[:, :, :], H17[:, :, 0:D], ALU.add)
            ts(A[:, :, :], A[:, :, :], 0.0, ALU.max)
            v.tensor_tensor(X[:, :, :], X[:, :, :], A[:, :, :], ALU.add).then_inc(x_made, 1)

NORM_MSG = float(np.float32(1.0) / np.float32(np.sqrt(D * DE)))
NORM_UPD = float(np.float32(1.0) / np.float32(np.sqrt(D * D)))
NORM_LIN = float(np.float32(1.0) / np.float32(np.sqrt(D)))
SC, C, EPS, BALL = 0.1, 0.01, 1e-6, 1e-5
PROJ = {"c1": (REL * D + D, 3), "c2": (REL * D + D, 3), "l1": (DE * D, 4), "l3": (2 * HID, 4)}
WEIGHT_LOADS = 6 + 2 + 3 + 4 + 3
_A = mybir.ActivationFunctionType
SQ = (_A.Sqrt, "n2", "n1", 1.0)
LIN = ("T", None, None, None)
NODE_FUNCS = {("c2", "end"): [(_A.Exp, "C", "B", 1.0), (_A.Ln, "n2", "n1", 1.0)],
              ("l1", "end"): [LIN, LIN, (_A.Sigmoid, "C", "B", NORM_UPD), LIN],
              ("l2", "start"): [SQ], ("l2", "end"): [SQ, SQ, SQ, (_A.Tanh, "n3", "n2", 1.0)], ("l3", "table"): [SQ]}

_INS = ["x", "src", "dst", "edge_attr_8", "edge_type_230", "edge_type_8",
        "L0_gnn_W1", "L0_gnn_root1", "L0_gnn_b1", "L0_gnn_W2", "L0_gnn_root2", "L0_gnn_b2",
        "L1_gnn_W_msg_tp", "L1_gnn_W_msg_lin", "L1_gnn_W_upd_tp", "L1_gnn_W_upd_lin",
        "L2_gnn_rel_weight", "L2_gnn_loop_weight", "L2_gnn_rel_emb",
        "L3_gnn_W1", "L3_gnn_b1", "L3_gnn_W2", "L3_gnn_b2"]

_TRANSPOSED = ("L3_gnn_W1", "L3_gnn_W2")


def kernel(**inputs):
    import numpy as _np
    import concourse.bacc as _bacc
    from concourse import mybir as _mybir
    from concourse.bass_utils import run_bass_kernel_spmd as _run

    nc = _bacc.Bacc("TRN2", target_bir_lowering=False, num_devices=1)
    arrays, args = {}, []
    for name in _INS:
        a = _np.ascontiguousarray(inputs[name].T if name in _TRANSPOSED else inputs[name])
        arrays[f"in_{name}"] = a
        args.append(nc.dram_tensor(f"in_{name}", a.shape, _mybir.dt.from_np(a.dtype), kind="ExternalInput").ap())
    args.append(nc.dram_tensor("out_x", (N, D), _mybir.dt.float32, kind="ExternalOutput").ap())
    gnn(nc, *args)
    r = _run(nc, [arrays], core_ids=[0])
    return r.results[0]["out_x"]
```

```python
import concourse.bass as bass
from concourse import mybir
from contextlib import ExitStack
import numpy as np

N, E, D = 3125, 100000, 16
P = 128
T = 784
G = 14
SLOTS = 2
GROUPS = T // G
ITERS = GROUPS // SLOTS
GE = P * G
FULL = E // GE
TAIL = E - FULL * GE
WIN = P
NP_, NJ = 98, 32
NPAD = NP_ * NJ
NLAST = N - (NJ - 1) * NP_
REL, TYPES, DE, HID = 8, 230, 8, 64
Q8, R8 = 8, 392
Q7, R7 = 7, 448
CHUNK8, CHUNK7 = R8 // 4, R7 // 4
W5 = D + 1 + 2 * HID
W5W = W5 + HID
XD = D + 1
EC = 8
ECOLS = TYPES * D // EC
KA, KB = 6 * (D + 1), 3 * (D + 1)
PAD_KEY = -1000.0
BIG = 2 * TYPES * D
BY_ACT = {"l1": (1, 3, 5, 8, 10, 12)}
BY_ACT.update((L, (0, 1, 2, 3, 4)) for L in ("cn", "c1", "c2", "l2", "l3"))
RING = 7
HIDDEN_AT = {4: 2, 8: 3}
TRANSPOSE_AT, ROWS_AT = 3, 7


def gnn(nc, x, src, dst, ea, t230, t8, cW1, croot1, cb1, cW2, croot2, cb2,
        mtp, mlin, utp, ulin, relw, loopw, relemb, sW1, sb1, sW2, sb2, out):
    f32, i32, bf16, f16 = mybir.dt.float32, mybir.dt.int32, mybir.dt.bfloat16, mybir.dt.float16
    ALU, ACT, AX = mybir.AluOpType, mybir.ActivationFunctionType, mybir.AxisListType.X

    with ExitStack() as ctx:
        def sb(name, shape, dt=f32):
            return ctx.enter_context(nc.sbuf_tensor(name, shape, dt))

        def dram(name, shape):
            return nc.dram_tensor(name, shape, f32).ap()

        def sem(name):
            return ctx.enter_context(nc.semaphore(name))

        tabs = {"c1": dram("tab_c1", (NPAD * REL, D)), "c2": dram("tab_c2", (NPAD * REL, D)),
                "l1": dram("tab_l1", (NPAD, DE * D)), "l2": dram("tab_l2", (NPAD * TYPES, D)),
                "l3": dram("tab_l3", (NPAD, W5W)), "norm": dram("tab_norm", (NPAD, REL))}
        relay = {"l1": dram("relay_l1", (NPAD, D + 1)), "l2": dram("relay_l2", (NPAD, D + 1))}

        ident, ident_b = sb("ident", [P, P]), sb("ident_b", [P, P], bf16)
        iota_r = sb("iota_r", [P, R7])
        iota_q = sb("iota_q", [P, Q8])
        zeros = sb("zeros", [P, R7], bf16)
        src_i, dst_i = sb("src_i", [P, T], i32), sb("dst_i", [P, T], i32)
        rel_row = sb("rel_row", [P, T], i32)
        type_row = sb("type_row", [P, T], i32)
        ea_sb = sb("ea_sb", [P, T, DE])
        norm_sb = sb("norm_sb", [P, T])
        keys = {k: sb("key_" + k, [P, GROUPS, 2, G], f16) for k in ("dst8", "dst7", "src7", "src8")}
        loc = sb("loc", [P, GROUPS, G], f16)
        typ = sb("typ", [P, GROUPS, G], f16)
        win_row = sb("win_row", [P, GROUPS], i32)
        win_key = {k: sb("win_key" + k, [P, GROUPS, 2]) for k in ("8", "7")}
        flag = sb("flag", [1, 1], i32)
        iota_p = sb("iota_p", [P, 1])
        ones = sb("ones", [GROUPS, P])
        wa, wb, wc_ = (sb(f"wtmp{k}", [P, GROUPS]) for k in range(3))
        idx = [sb(f"idx{s}", [P, 2, G], i32) for s in range(SLOTS)]
        kf = [sb(f"kf{s}", [P, 4, G]) for s in range(SLOTS)]
        idx_w = [sb(f"idx_w{s}", [P, 1], i32) for s in range(SLOTS)]
        kw = [sb(f"kw{s}", [P, 1, 2]) for s in range(SLOTS)]
        win = [sb(f"win{s}", [P, W5W]) for s in range(SLOTS)]
        win_parts = [sb(f"win_parts{s}", [P, 3, W5W], bf16) for s in range(SLOTS)]
        hot = [sb(f"hot{s}", [P, G, WIN], bf16) for s in range(SLOTS)]
        hotT = [sb(f"hotT{s}", [P, G, P], bf16) for s in range(SLOTS)]
        msg_parts = [sb(f"msg_parts{s}", [P, G, 3 * (D + 1)], bf16) for s in range(SLOTS)]
        res = sb("res", [P, G, D + 1])
        vec, sq2, y2 = (sb(n, [P, G, 2, D]) for n in ("vec", "sq2", "y2"))
        c2 = sb("c2", [P, 2, 2 * G])
        wsum = [sb(f"wsum{s}", [P, D + 1]) for s in range(SLOTS)]
        S2 = [sb(f"S2{s}", [P, P]) for s in range(SLOTS)]
        O2 = [sb(f"O2{s}", [P, R7]) for s in range(SLOTS)]
        ga = [sb(f"ga{s}", [P, G, W5]) for s in range(SLOTS)]
        gb = [sb(f"gb{s}", [P, G, W5]) for s in range(SLOTS)]
        msg = [sb(f"msg{s}", [P, 2, G, D + 1]) for s in range(SLOTS)]
        sq = sb("sq", [P, G, D])
        sg = [sb(f"sg{s}", [P, G, D]) for s in range(SLOTS)]
        sm = [sb(f"sm{s}", [P, 8, G]) for s in range(SLOTS)]
        ea_flat = ea_sb[:, :, :].rearrange("p t j -> p (t j)")
        hid = ea_flat[:, 0:G * 2 * HID].rearrange("p (g c) -> p g c", g=G)
        hidT = ea_flat[:, G * 2 * HID:G * 2 * HID + 8 * P].rearrange("p (a g e) -> p a g e", a=2, g=4)
        S = sb("S", [P, RING, P])
        O_XT = sb("O_XT", [P, NPAD + NP_])
        O = O_XT[:, 0:RING * R7].rearrange("p (g r) -> p g r", g=RING)
        XT = O_XT[0:D + 1, :]
        wrel = ea_flat[0:D + 1, 0:TYPES * D]
        wrel_b = ea_flat[0:KA, TYPES * D:TYPES * D * 3 // 2].bitcast(bf16)
        h_parts = [ga[a][:, :, :].rearrange("p g c -> p (g c)").bitcast(bf16)[0:NP_, 0:NJ * (K + 1)].rearrange("p (j k) -> p j k", j=NJ)
                   for a, K in enumerate((KA, KB))]
        XTab = O_XT[0:KA, :].bitcast(bf16)
        big = sb("big", [P, BIG])
        X, H17, HT = sb("X", [NP_, NJ, D]), sb("H17", [NP_, NJ, D + 1]), sb("HT", [NP_, NJ, D + 1])
        A, B, C_, V = (sb(n, [NP_, NJ, D]) for n in ("A", "B", "C_", "V"))
        AGR = sb("AGR", [NP_, NJ, D + 1])
        degs, deg_dst = sb("degs", [NP_, NJ]), sb("deg_dst", [NP_, NJ])
        cnt = sb("cnt", [NP_, NJ, REL])
        n1, n2, n3, n4, n5, n6 = (sb(f"n{k}", [NP_, NJ]) for k in range(1, 7))
        AG = sb("AG", [P, R7])
        AGT = sb("AGT", [CHUNK7, 4 * Q7, D + 1])
        XTj = sb("XTj", [P, 2, 2, NP_], bf16)
        w_parts = [big[0:D + 1, (k + 1) * TYPES * D // 2:(k + 2) * TYPES * D // 2].bitcast(bf16) for k in range(3)]
        prod = big[0:NP_, 0:2 * D * D].rearrange("p (a c) -> p a c", a=2)
        lane = big[:, 8 * T:9 * T].bitcast(i32)
        wc = [sb(f"wc{k}", [D + 1, REL * D + D]) for k in range(2)]
        wl1 = sb("wl1", [D + 1, DE * D])
        wupd = sb("wupd", [D + 1, D * D])
        wlin, wulin, wloop = (sb(n, [D + 1, D]) for n in ("wlin", "wulin", "wloop"))
        wpq = sb("wpq", [D + 1, 2 * HID])
        w2 = sb("w2", [P, 2 * D])
        b2 = sb("b2", [P, 2 * D])

        agg = ctx.enter_context(nc.psum_tensor("agg", [P, 512], f32))
        psT = [ctx.enter_context(nc.psum_tensor(f"psT{k}", [P, 512], f32)) for k in range(2)]
        psM = [ctx.enter_context(nc.psum_tensor(f"psM{k}", [P, 512], f32)) for k in range(4)]
        psTb = [t[:, 0:G // 2 * P // 2].bitcast(bf16) for t in psT]
        psV = ctx.enter_context(nc.psum_tensor("psV", [P, 512], f32))

        LAYERS = ("cn", "c1", "c2", "l1", "l2", "l3")
        consts_made, ident_made = sem("consts_made"), sem("ident_made")
        zeroed, edges_in, ea_in, weights_in, x_in = (sem(n) for n in ("zeroed", "edges_in", "ea_in", "weights_in", "x_in"))
        dve_step = sem("dve_step")
        norm_made, norm_out, flag_made, wrel_in = (sem(n) for n in ("norm_made", "norm_out", "flag_made", "wrel_in"))
        wrel_step = sem("wrel_step")
        prep_dve, prep_pe = sem("prep_dve"), sem("prep_pe")
        step_front = sem("step_front")
        tile_act = {L: sem(f"tile_act_{L}") for L in LAYERS}
        step_of = {L: sem(f"step_{L}") for L in LAYERS}
        win_in = {(L, s): sem(f"win_in_{L}{s}") for L in ("c1", "l1", "l3") for s in range(SLOTS)}
        hot_made, win_split, hotT_ps, hotT_sb = (sem(n) for n in ("hot_made", "win_split", "hotT_ps", "hotT_sb"))
        rows_ps, rows_sb = ({L: sem(f"{n}_{L}") for L in ("c1", "l1", "l3")} for n in ("rows_ps", "rows_sb"))
        groups_before = {"c1": 0, "l1": GROUPS, "l3": 2 * GROUPS}
        parts_made, wsum_ps, wsum_read, tile2_free, tile2_ready = ({L: sem(f"{n}_{L}") for L in LAYERS if L != "l1"} for n in (
            "parts_made", "wsum_ps", "wsum_read", "tile2_free", "tile2_ready"))
        TABLES = LAYERS[1:]
        xt_in, xt_ps, xt_sb, table_made, table_out, agg_done, agg_sb, aggT = (sem(n) for n in (
            "xt_in", "xt_ps", "xt_sb", "table_made", "table_out", "agg_done", "agg_sb", "aggT"))
        nth = {L: n + 1 for n, L in enumerate(LAYERS)}
        nth_xt = {L: n + 1 for n, L in enumerate(TABLES)}
        nth_tab = {L: n + 1 for n, L in enumerate(("c1", "c2", "l1", "l3"))}
        xt_before = {L: (n + (L == "l3")) * (NJ // 4) for n, L in enumerate(TABLES)}
        idx_set = {L: sem(f"idx_set_{L}") for L in TABLES}
        proj_ps, proj_sb, loop_ps = sem("proj_ps"), sem("proj_sb"), sem("loop_ps")
        proj_banks = {L: -(-NJ // PROJ[L][1]) for L in nth_tab}
        proj_before = {L: sum(proj_banks[M] for M in nth_tab if nth_tab[M] < nth_tab[L]) for L in nth_tab}
        gathered = {(L, s): sem(f"gathered_{L}{s}") for L in TABLES for s in range(SLOTS)}
        key_set, key_used, tile_free, tile_ready = ({L: sem(f"{n}_{L}") for L in LAYERS} for n in (
            "key_set", "key_used", "tile_free", "tile_ready"))
        var_made, std_made = sem("var_made"), sem("std_made")
        act_in, act_out = sem("act_in"), sem("act_out")
        relay_made, relay_out, relay_in = sem("relay_made"), sem("relay_out"), sem("relay_in")
        lin_in, lin_ps, lin_sb, lin_mm, lin_read = (sem(n) for n in ("lin_in", "lin_ps", "lin_sb", "lin_mm", "lin_read"))
        upd_ps, upd_read = sem("upd_ps"), sem("upd_read")
        xtj_set, rel_ps, rel_act, rel_dve = (sem(n) for n in ("xtj_set", "rel_ps", "rel_act", "rel_dve"))
        row_free = [sem(f"row_free{h}") for h in range(2)]
        rel_row_out = [sem(f"rel_row_out{h}") for h in range(2)]
        m_made, sig_made, sq_made, tanh_made = (sem(n) for n in ("m_made", "sig_made", "sq_made", "tanh_made"))
        hid_made, hidT_ps, hidT_sb, v_ps, v_read = (sem(n) for n in ("hid_made", "hidT_ps", "hidT_sb", "v_ps", "v_read"))
        hyp_made = sem("hyp_made")
        gathers_begun = sem("gathers_begun")
        rows_used = sem("rows_used")
        x_made, x_out = sem("x_made"), sem("x_out")

        block = ctx.enter_context(nc.Block())

        def nodes(dr):
            return (dr[0:(NJ - 1) * NP_, :].rearrange("(j p) d -> p j d", p=NP_), dr[(NJ - 1) * NP_:N, :])

        SCATTER = {"cn": (Q8, R8, REL, 1), "c1": (Q8, R8, D, 1), "c2": (Q8, R8, D, 1), "l1": (Q7, R7, D + 1, 1),
                   "l2": (Q7, R7, D + 1, 1), "l3": (Q8, R8, D, 2)}
        WINDOW = {"c1": (REL, G), "l1": (DE * D, 4), "l3": (D + 1, G)}
        WIN_COLS = {"c1": REL, "l1": DE * D, "l3": W5W}
        BY_DST = ("cn", "c1", "c2", "l2", "l3")
        PARTS = {"cn": 1, "c1": 3, "c2": 3, "l2": 3, "l3": 3}

        def in_pairs(eng, front, back, early=lambda i, s: None, middle=lambda i, s: None):
            front(0, 0)
            middle(0, 0)
            with eng.Fori(0, ITERS - 1, 1) as i:
                early(i, 0)
                front(i, 1)
                back(i, 0, (i, 1))
                early(i, 1)
                front(i + 1, 0)
                back(i, 1, (i + 1, 0))
            early(ITERS - 1, 0)
            front(ITERS - 1, 1)
            back(ITERS - 1, 0, (ITERS - 1, 1))
            early(ITERS - 1, 1)
            back(ITERS - 1, 1, None)

        def ready_before(L, t):
            return sum(1 if n % G in BY_ACT[L] else 2 for n in range(t + 1))

        def acts_of(L, tiles):
            return 2 * sum(t % G in BY_ACT[L] for t in range(tiles))

        def two_paths(eng, L, path):
            with eng.If(eng.value_load(flag[0:1, 0:1], min_val=0, max_val=1) > 0):
                path(L, False)
            with eng.Else():
                path(L, True)

        def relay_out_and_in(sp, L, turn):
            d = SCATTER[L][2]
            sp.wait_ge(relay_made, turn)
            sp.dma_start(relay[L].rearrange("(j p) d -> p j d", p=CHUNK7), AGT[:, :, 0:d]).then_inc(relay_out, 16)
            sp.wait_ge(relay_out, 16 * turn)
            sp.dma_start(AGR[:, :, 0:d], relay[L].rearrange("(j p) d -> p j d", p=NP_)).then_inc(relay_in, 16)

        @block.sync
        def _(sp):
            sp.wait_ge(zeroed, 1)
            part, odd = TAIL // G, TAIL % G
            for tile, dr in ((src_i, src), (dst_i, dst), (rel_row, t8), (type_row, t230)):
                sp.dma_start(tile[:, 0:FULL * G].rearrange("p (k g) -> p k g", g=G),
                             dr[0:FULL * GE].rearrange("(k p g) -> p k g", p=P, g=G)).then_inc(edges_in, 16)
                sp.dma_start(tile[0:part, FULL * G:], dr[FULL * GE:FULL * GE + part * G].rearrange("(p g) -> p g", g=G)).then_inc(edges_in, 16)
                sp.dma_start(tile[part:part + 1, FULL * G:FULL * G + odd], dr[E - odd:E].rearrange("(p g) -> p g", p=1)).then_inc(edges_in, 16)
            full, last = nodes(x)
            sp.dma_start(X[:, 0:NJ - 1, :], full).then_inc(x_in, 16)
            sp.dma_start(X[0:NLAST, NJ - 1, :], last).then_inc(x_in, 16)
            sp.dma_start(ea_sb[:, 0:FULL * G, :].rearrange("p (k g) j -> p k (g j)", g=G),
                         ea[0:FULL * GE, :].rearrange("(k p g) j -> p k (g j)", p=P, g=G)).then_inc(ea_in, 16)
            sp.dma_start(ea_sb[0:part, FULL * G:, :], ea[FULL * GE:FULL * GE + part * G, :].rearrange("(p g) j -> p g j", g=G)).then_inc(ea_in, 16)
            sp.dma_start(ea_sb[part:part + 1, FULL * G:FULL * G + odd, :], ea[E - odd:E, :].rearrange("(p g) j -> p g j", p=1)).then_inc(ea_in, 16)
            for L, cols, pitch in (("c1", REL * D, REL * D + D), ("c2", REL * D, REL * D + D), ("l1", DE * D, DE * D), ("l3", W5W, W5W)):
                if L == "l3":
                    relay_out_and_in(sp, "l2", 2)
                sp.wait_ge(table_made, nth_tab[L])
                view = tabs[L] if L in ("l1", "l3") else tabs[L].rearrange("(n r) d -> n (r d)", r=REL)
                rows = big[0:NP_, 0:NJ * pitch].rearrange("p (j c) -> p j c", j=NJ)[:, :, 0:cols]
                sp.dma_start(view.rearrange("(j p) c -> p j c", p=NP_), rows).then_inc(table_out, 16)
                if L == "c1":
                    sp.wait_ge(norm_made, 1)
                    sp.dma_start(tabs["norm"].rearrange("(j p) t -> p j t", p=NP_), cnt[:, :, :]).then_inc(norm_out, 16)
                if L == "l1":
                    sp.wait_ge(agg_sb, nth[L])
                    sp.dma_start(wrel[0:D, :].rearrange("i (t o) -> i t o", t=TYPES), relw.rearrange("t i o -> i t o")).then_inc(wrel_in, 16)
                    sp.dma_start(wrel[D:D + 1, :], relemb.rearrange("(a t) o -> a (t o)", a=1)).then_inc(wrel_in, 16)
                    relay_out_and_in(sp, "l1", 1)
                    sp.wait_ge(wrel_step, WREL_STEPS)
                    for b in range(6):
                        sp.dma_start(wrel_b[b * (D + 1):(b + 1) * (D + 1), :], w_parts[b % 3]).then_inc(wrel_in, 16)
                    wide = tabs["l2"].rearrange("(j p t) d -> j p (t d)", p=NP_, t=TYPES)
                    for h in range(2):
                        sp.sem_inc(row_free[h], 1)
                    with sp.Fori(0, NJ // 2, 1) as i:
                        for h in range(2):
                            sp.wait_ge(rel_act, i * EC + (EC // 2) * (h + 1) + 2)
                            sp.wait_ge(rel_dve, i * EC + (EC // 2) * (h + 1) + 2)
                            sp.dma_start(wide[bass.ds(i * 2 + h, 1), :, :].rearrange("a p c -> p (a c)"),
                                         big[0:NP_, h * TYPES * D:(h + 1) * TYPES * D]).then_inc(rel_row_out[h], 16)
                            sp.wait_ge(rel_row_out[h], i * 16 + 16)
                            sp.sem_inc(row_free[h], 1)
            sp.wait_ge(x_made, 1)
            full, last = nodes(out)
            sp.dma_start(full, X[:, 0:NJ - 1, :]).then_inc(x_out, 16)
            sp.dma_start(last, X[0:NLAST, NJ - 1, :]).then_inc(x_out, 16)
            sp.wait_ge(x_out, 32)

        @block.gpsimd
        def _(pool):
            nc.gpsimd.iota(iota_r[:, :], pattern=[[1, R7]], base=0, channel_multiplier=0,
                           allow_small_or_imprecise_dtypes=True).then_inc(consts_made, 1)
            nc.gpsimd.iota(iota_q[:, :], pattern=[[1, Q8]], base=0, channel_multiplier=0,
                           allow_small_or_imprecise_dtypes=True).then_inc(consts_made, 1)
            nc.gpsimd.iota(lane, pattern=[[GE, GROUPS], [1, G]], base=0, channel_multiplier=G).then_inc(consts_made, 1)
            nc.gpsimd.iota(iota_p[:, :], pattern=[[0, 1]], base=0, channel_multiplier=1,
                           allow_small_or_imprecise_dtypes=True).then_inc(consts_made, 1)
            nc.gpsimd.memset(ones[:, :], 1.0).then_inc(consts_made, 1)
            nc.gpsimd.memset(ident[:, :], 0.0).then_inc(ident_made, 1)
            pool.wait_ge(ident_made, 1)
            nc.gpsimd.affine_select(out=ident[:, :], in_=ident[:, :], compare_op=ALU.not_equal, fill=1.0, base=0,
                                    pattern=[[-1, P]], channel_multiplier=1).then_inc(ident_made, 1)
            pool.wait_ge(flag_made, 1)
            GATHERS = {"c1": ((rel_row, D, tabs["c1"]), (dst_i, REL, tabs["norm"])), "c2": ((rel_row, D, tabs["c2"]),),
                       "l1": ((dst_i, DE * D, tabs["l1"]),), "l2": ((type_row, D, tabs["l2"]),),
                       "l3": ((src_i, W5, tabs["l3"]), (dst_i, W5, tabs["l3"]))}

            def gather_pass(L, windows):
                by_edge = [n for n, gth in enumerate(GATHERS[L]) if not (windows and gth[0] is dst_i)]
                by_window = [gth for gth in GATHERS[L] if windows and gth[0] is dst_i]
                copies = len(by_edge) + len(by_window)
                with pool.Fori(0, ITERS, 1) as i:
                    for s in range(SLOTS):
                        pool.wait_ge(rows_used, i * SLOTS + s + 1 + GROUPS * (nth[L] - 1))
                        for n in by_edge:
                            nc.gpsimd.tensor_copy(idx[s][:, n, :], GATHERS[L][n][0][:, bass.ds(i * (SLOTS * G) + s * G, G)]).then_inc(idx_set[L], 1)
                        for _ in by_window:
                            nc.gpsimd.tensor_copy(idx_w[s][:, :], win_row[:, bass.ds(i * SLOTS + s, 1)]).then_inc(idx_set[L], 1)
                        pool.wait_ge(idx_set[L], (i * SLOTS + s) * copies + copies)
                        pool.sem_inc(gathers_begun, 1)
                        for _, _, table in by_window:
                            cols = WIN_COLS[L]
                            pool.indirect_dma_start(
                                out=win[s][:, 0:cols], out_offset=None, in_=table,
                                in_offset=bass.IndirectOffsetOnAxis(ap=idx_w[s][:, 0:1], axis=0)).then_inc(win_in[L, s], 16)
                        for n in by_edge:
                            _, cols, table = GATHERS[L][n]
                            to = gb[s] if L == "l1" else (ga, gb)[n][s]
                            for g in range(G):
                                pool.indirect_dma_start(
                                    out=to[:, g, 0:cols], out_offset=None, in_=table,
                                    in_offset=bass.IndirectOffsetOnAxis(ap=idx[s][:, n, g:g + 1], axis=0)).then_inc(gathered[L, s], 16)

            def split_weights():
                steps = [0]

                def done(ins):
                    steps[0] += 1
                    ins.then_inc(wrel_step, 1)
                    pool.wait_ge(wrel_step, steps[0])

                pool.wait_ge(wrel_in, 32)
                for n, part in enumerate(w_parts):
                    done(nc.gpsimd.tensor_copy(part, wrel))
                    if n < 2:
                        done(nc.gpsimd.tensor_tensor(wrel, wrel, part, ALU.subtract))
                assert steps[0] == WREL_STEPS

            for L in LAYERS[1:]:
                if L == "l2":
                    split_weights()
                    for h in range(2):
                        pool.wait_ge(rel_row_out[h], 16 * NJ // 2)
                else:
                    pool.wait_ge(table_out, 16 * nth_tab[L])
                if L == "c1":
                    pool.wait_ge(norm_out, 16)
                two_paths(pool, L, gather_pass)

        act_calls, lin_calls = [0], [0]

        def node_functions(act, L, where):
            for fn, o, a, scale in NODE_FUNCS.get((L, where), ()):
                if fn == "T":
                    for k in range(NJ // 4):
                        lin_calls[0] += 1
                        act.wait_ge(lin_ps, lin_calls[0])
                        nc.scalar.copy(XT[:, k * 4 * NP_:(k + 1) * 4 * NP_], psT[k % 2][0:D + 1, 0:4 * NP_]).then_inc(lin_sb, 1)
                    continue
                act_calls[0] += 1
                act.wait_ge(act_in, act_calls[0])
                t = {"n1": n1[:, :], "n2": n2[:, :], "n3": n3[:, :], "B": B[:, :, :], "C": C_[:, :, :]}
                nc.scalar.activation(t[o], t[a], fn, scale=scale).then_inc(act_out, 1)

        @block.scalar
        def _(act):
            def act_aggregate(L):
                q, r, d, per_edge = SCATTER[L]
                act.wait_ge(agg_done, nth[L])
                nc.scalar.copy(AG[0:q * d, 0:r], agg[0:q * d, 0:r]).then_inc(agg_sb, 1)

            def act_edges(L, windows):
                names = {"cn": ("dst8",), "c1": ("dst8",), "c2": ("dst8",), "l1": ("src7",), "l2": ("dst7",), "l3": ("src8", "dst8")}[L]
                if windows:
                    names = tuple(n for n in names if n[:3] == "src")
                if windows and L in WINDOW:
                    act.sem_inc(rows_sb[L], 1)
                full_tiles = G * (SCATTER[L][3] - (1 if windows and L in BY_DST else 0))
                per_key = 2 if L == "l3" else 1

                def front(i, s):
                    k = i * SLOTS + s
                    act.wait_ge(key_used[L], k + 1)
                    for a, name in enumerate(names):
                        nc.scalar.copy(kf[s][:, 2 * a:2 * a + 2, :], keys[name][:, bass.ds(k, 1), :, :].rearrange("p a k g -> p (a k) g")).then_inc(key_set[L], 1)
                    if windows and L in BY_DST:
                        nc.scalar.copy(kw[s][:, :, :], win_key[str(SCATTER[L][0])][:, bass.ds(k, 1), :]).then_inc(key_set[L], 1)
                    if windows and L in WINDOW and L != "l1":
                        copy_hotT(i, s)
                        copy_rows(i, s)
                        if L == "l3":
                            relu_hidden(k)

                def copy_hotT(i, s):
                    k = i * SLOTS + s
                    for c in range(2):
                        act.wait_ge(hotT_ps, (groups_before[L] + k) * 2 + c + 1)
                        nc.scalar.copy(hotT[s][:, c * (G // 2):(c + 1) * (G // 2), :],
                                       psTb[c].rearrange("p (g e) -> p g e", e=P)).then_inc(hotT_sb, 1)

                def copy_hotT_and_rows(i, s):
                    copy_hotT(i, s)
                    copy_rows(i, s)

                def copy_rows(i, s):
                    k = i * SLOTS + s
                    cols, per = WINDOW[L]
                    n = -(-G // per)
                    for c in range(n):
                        m = min(per, G - c * per)
                        act.wait_ge(rows_ps[L], k * n + c + 1)
                        nc.scalar.copy(gb[s][:, c * per:c * per + m, 0:cols],
                                       psM[1 + c % 3][:, 0:m * cols].rearrange("p (g c) -> p g c", g=m)).then_inc(rows_sb[L], 1)

                def relu_hidden(k):
                    for c in range(4):
                        m = min(4, G - 4 * c)
                        act.wait_ge(hidT_ps, k * 4 + c + 1)
                        nc.scalar.activation(hidT[:, c % 2, 0:m, :], psT[c % 2][:, 0:m * P].rearrange("p (g e) -> p g e", g=m), ACT.Relu).then_inc(hidT_sb, 1)

                def functions(i, s, following):
                    k = i * SLOTS + s
                    if L == "l1":
                        act.wait_ge(m_made, k + 1)
                        nc.scalar.activation(sg[s][:, :, :], sq[:, :, :], ACT.Sigmoid, scale=NORM_MSG).then_inc(sig_made, 1)
                        if windows:
                            one_hots(i, s, 0, RING)
                            if following:
                                copy_hotT(*following)
                            one_hots(i, s, RING, G)
                            if following:
                                copy_rows(*following)
                    if L == "l2":
                        act.wait_ge(sq_made, k + 1)
                        nc.scalar.activation(sm[s][:, 2, :], sm[s][:, 1, :], ACT.Sqrt).then_inc(tanh_made, 1)
                        act.wait_ge(tanh_made, k * 2 + 1)
                        nc.scalar.activation(sm[s][:, 3, :], sm[s][:, 2, :], ACT.Tanh, scale=SC).then_inc(tanh_made, 1)
                    if L == "l3" and not windows:
                        relu_hidden(k)

                def one_hots(i, s, first=0, end=2 * G):
                    k = i * SLOTS + s
                    n = acts_of(L, first) // 2
                    if full_tiles:
                        act.wait_ge(key_set[L], k * per_key + per_key)
                    for t in range(full_tiles):
                        if t % G not in BY_ACT[L] or not first <= t < end:
                            continue
                        act.wait_ge(tile_free[L], k * full_tiles + t + 1)
                        o = O[:, t % RING, 0:SCATTER[L][1]]
                        nc.scalar.activation(o, iota_r[:, 0:SCATTER[L][1]], ACT.Abs, scale=-1.0,
                                             bias=kf[s][:, 2 * (t // G) + 1, t % G:t % G + 1]).then_inc(tile_act[L], 1)
                        act.wait_ge(tile_act[L], k * acts_of(L, full_tiles) + 2 * n + 1)
                        nc.scalar.activation(o, o, ACT.Relu, scale=-1.0, bias=1.0).then_inc(tile_act[L], 1)
                        n += 1

                def functions_and_one_hots(i, s, following):
                    functions(i, s, following)
                    one_hots(i, s)

                if windows:
                    in_pairs(act, front, functions, **({"middle": copy_hotT_and_rows} if L == "l1" else {"early": one_hots}))
                else:
                    in_pairs(act, front, functions_and_one_hots)

            act.wait_ge(zeroed, 2)
            for k, (W, root, b) in enumerate(((cW1, croot1, cb1), (cW2, croot2, cb2))):
                act.dma_start(wc[k][0:D, 0:REL * D].rearrange("i (r o) -> i r o", r=REL), W.rearrange("r i o -> i r o")).then_inc(weights_in, 16)
                act.dma_start(wc[k][0:D, REL * D:], root).then_inc(weights_in, 16)
                act.dma_start(wc[k][D:D + 1, REL * D:], b.rearrange("(a n) -> a n", a=1)).then_inc(weights_in, 16)
            act.dma_start(wl1[0:D, :], mtp.rearrange("i j h -> i (j h)")).then_inc(weights_in, 16)
            act.dma_start(wupd[0:D, :], utp.rearrange("i h k -> i (h k)")).then_inc(weights_in, 16)
            for w, dr in ((wlin, mlin), (wulin, ulin), (wloop, loopw)):
                act.dma_start(w[0:D, :], dr).then_inc(weights_in, 16)
            for k in range(2):
                act.dma_start(wpq[0:D, k * HID:(k + 1) * HID], sW1[k * D:(k + 1) * D, :]).then_inc(weights_in, 16)
                act.dma_start(w2[k * HID:(k + 1) * HID, (1 - k) * D:(2 - k) * D], sW2).then_inc(weights_in, 16)
            act.dma_start(wpq[D:D + 1, HID:], sb1.rearrange("(a n) -> a n", a=1)).then_inc(weights_in, 16)
            for k in range(2):
                act.dma_start(b2[:, k * D:(k + 1) * D], sb2.rearrange("(a n) -> a n", a=1).broadcast_to([P, D])).then_inc(weights_in, 16)

            act.wait_ge(flag_made, 1)

            def act_table(L):
                if L != "c2":
                    act.wait_ge(var_made, ("c1", "l1", "l2", "l3").index(L) + 1)
                    nc.scalar.activation(n2[:, :], n1[:, :], ACT.Sqrt).then_inc(std_made, 1)
                node_functions(act, L, "start")
                for k in range(NJ // 4):
                    act.wait_ge(xt_ps, xt_before[L] + k + 1)
                    nc.scalar.copy(XT[:, k * 4 * NP_:(k + 1) * 4 * NP_], psT[k % 2][0:D + 1, 0:4 * NP_]).then_inc(xt_sb, 1)
                if L != "l2":
                    cols, per = PROJ[L]
                    for k in range(-(-NJ // per)):
                        m = min(per, NJ - k * per)
                        act.wait_ge(proj_ps, proj_before[L] + k + 1)
                        pitch = W5W if L == "l3" else cols
                        rows = big[0:NP_, 0:NJ * pitch].rearrange("p (j c) -> p j c", j=NJ)
                        first = XD if L == "l3" else 0
                        nc.scalar.copy(rows[:, k * per:k * per + m, first:first + cols],
                                       psM[k % 4][0:NP_, 0:m * cols].rearrange("p (j c) -> p j c", j=m)).then_inc(proj_sb, 1)
                else:
                    act.sem_inc(rel_act, 2)
                    act.wait_ge(loop_ps, 1)
                    for k in range(NJ // 4):
                        act.wait_ge(xt_ps, xt_before[L] + NJ // 4 + k + 1)
                        for a, K in enumerate((KA, KB)):
                            copied = nc.scalar.copy(XTab[0:K, k * 8 * NP_:(k + 1) * 8 * NP_].rearrange("p (j a n) -> p j a n", j=4, a=2)[:, :, a, :],
                                                    psTb[k % 2][0:K, 0:8 * NP_].rearrange("p (j a n) -> p j a n", j=4, a=2)[:, :, a, :])
                        copied.then_inc(xt_sb, 1)
                    act.wait_ge(xt_sb, xt_before[L] + 2 * (NJ // 4))
                    nc.scalar.copy(XTj[0:KA, 0, :, :], XTab[:, 0:2 * NP_].rearrange("p (a n) -> p a n", a=2)).then_inc(xtj_set, 1)
                    with act.Fori(0, NJ // 2, 1) as i:
                        for h in range(2):
                            act.wait_ge(row_free[h], i + 1)
                            for c in range(0, EC, 2):
                                act.wait_ge(rel_ps, i * (2 * EC) + h * EC + c + 1)
                                nc.scalar.copy(big[0:NP_, (h * EC + c) * ECOLS:(h * EC + c + 1) * ECOLS], psM[c % 4][0:NP_, 0:ECOLS]).then_inc(rel_act, 1)
                                if c == 0:
                                    nc.scalar.copy(XTj[0:KA, 1 - h, :, :], XTab[:, bass.ds(i * (4 * NP_) + (h + 1) * 2 * NP_, 2 * NP_)].rearrange("p (a n) -> p a n", a=2)).then_inc(xtj_set, 1)
                node_functions(act, L, "table")

            for L in LAYERS:
                if L != "c1":
                    act_table("c1" if L == "cn" else L)
                two_paths(act, L, act_edges)
                act_aggregate(L)
                node_functions(act, L, "end")

        def second_layer(pe, k, c):
            m = min(4, G - 4 * c)
            pe.wait_ge(hidT_sb, k * 4 + c + 1)
            if c == 0:
                pe.wait_ge(v_read, k + 1)
            for g in range(m):
                last = nc.tensor.matmul(psV[:, (4 * c + g) * 2 * D:(4 * c + g + 1) * 2 * D], hidT[:, c % 2, g, :], w2[:, :], start=True, stop=True)
            last.then_inc(v_ps, 1)

        @block.tensor
        def _(pe):
            pe.wait_ge(ident_made, 2)
            pe.wait_ge(weights_in, 16 * WEIGHT_LOADS)

            pe.wait_ge(prep_dve, 1)
            nc.tensor.transpose(psT[0][0:GROUPS, 0:P], wa[:, :], ident[:, :]).then_inc(prep_pe, 1)
            pe.wait_ge(prep_dve, 2)
            pe.wait_ge(consts_made, 5)
            nc.tensor.matmul(psT[1][:, 0:GROUPS], ones[:, :], wb[0:GROUPS, :], start=True, stop=True).then_inc(prep_pe, 1)
            pe.wait_ge(prep_dve, 3)
            nc.tensor.transpose(psT[0][0:1, 0:P], wc_[:, 0:1], ident[:, :]).then_inc(prep_pe, 1)
            pe.wait_ge(flag_made, 1)

            def pe_edges(L, windows):
                q, r, d, per_edge = SCATTER[L]
                two_level = windows and L in BY_DST
                full_tiles = G * (per_edge - (1 if two_level else 0))
                if two_level:
                    pe.sem_inc(tile2_free[L], SLOTS)
                def front(i, s):
                    if windows and L in ("c1", "l3"):
                        transpose_hot(i, s)
                        rows(i, s)
                    if windows and L == "l3":
                        hidden(i, s, (0, 1))

                def transpose_hot(i, s):
                    k = i * SLOTS + s
                    pe.wait_ge(hot_made, groups_before[L] + k + 1)
                    for g in range(G):
                        last = nc.tensor.transpose(psTb[g // (G // 2)][:, (g % (G // 2)) * P:(g % (G // 2) + 1) * P],
                                                   hot[s][:, g, :], ident_b[:, :])
                        if g % (G // 2) == G // 2 - 1:
                            last.then_inc(hotT_ps, 1)

                def transpose_and_rows(i, s):
                    transpose_hot(i, s)
                    rows(i, s)

                def rows(i, s):
                    k = i * SLOTS + s
                    pe.wait_ge(win_split, groups_before[L] + k + 1)
                    cols, per = WINDOW[L]
                    n = -(-G // per)
                    for c in range(n):
                        if c == 0:
                            pe.wait_ge(rows_sb[L], k * n + 1)
                        if c >= 3:
                            pe.wait_ge(rows_sb[L], k * n + c - 1)
                        pe.wait_ge(hotT_sb, (groups_before[L] + k) * 2 + min(G - 1, (c + 1) * per - 1) // (G // 2) + 1)
                        for g in range(c * per, min(G, (c + 1) * per)):
                            for part in range(3):
                                last = nc.tensor.matmul(psM[1 + c % 3][:, (g - c * per) * cols:(g - c * per + 1) * cols],
                                                        hotT[s][:, g, :], win_parts[s][:, part, 0:cols], start=part == 0, stop=part == 2)
                        last.then_inc(rows_ps[L], 1)

                def hidden_rest(i, s):
                    hidden(i, s, (2, 3))

                def hidden(i, s, chunks):
                    k = i * SLOTS + s
                    if windows:
                        pe.wait_ge(gathered[L, s], i * (G * 16) + G * 16)
                    else:
                        pe.wait_ge(hid_made, k + 1)
                    for c in chunks:
                        m = min(4, G - 4 * c)
                        if c >= 2:
                            pe.wait_ge(hidT_sb, k * 4 + c - 1)
                        for g in range(m):
                            out = psT[c % 2][:, g * P:(g + 1) * P]
                            if windows:
                                nc.tensor.matmul(out, ga[s][:, 4 * c + g, XD:XD + 2 * HID], ident[:, :], start=True, stop=False, skip_group_check=True)
                                for part in range(3):
                                    last = nc.tensor.matmul(out, win_parts[s][:, part, XD + HID:XD + 3 * HID], hotT[s][:, 4 * c + g, :],
                                                            start=False, stop=part == 2, skip_group_check=True)
                            else:
                                last = nc.tensor.transpose(out, hid[:, 4 * c + g, :], ident[:, :])
                        last.then_inc(hidT_ps, 1)
                        if c >= 1:
                            second_layer(pe, k, c - 1)
                        if c == 3:
                            second_layer(pe, k, c)

                def first_level(i, s):
                    k = i * SLOTS + s
                    w = PARTS[L] * d
                    pe.wait_ge(parts_made[L], k + 1)
                    pe.wait_ge(wsum_read[L], k + 1)
                    for g in range(G):
                        last = nc.tensor.matmul(psM[0][:, 0:w], hot[s][:, g, :], msg_parts[s][:, g, 0:w], start=g == 0, stop=g == G - 1)
                    last.then_inc(wsum_ps[L], 1)

                def back(i, s, following):
                    k = i * SLOTS + s
                    if L == "l3" and not windows:
                        hidden(i, s, range(4))
                    if two_level and L != "cn":
                        first_level(i, s)
                    n = 0
                    for t in range(full_tiles):
                        if L == "l1" and windows and following:
                            if t == TRANSPOSE_AT:
                                transpose_hot(*following)
                            if t == ROWS_AT:
                                rows(*following)
                        if L == "l3" and windows and following and t in HIDDEN_AT:
                            hidden(*following, (HIDDEN_AT[t],))
                        pe.wait_ge(tile_ready[L], k * ready_before(L, full_tiles - 1) + ready_before(L, t))
                        if t % G in BY_ACT[L]:
                            n += 2
                            pe.wait_ge(tile_act[L], k * acts_of(L, full_tiles) + n)
                        nc.tensor.matmul(agg[0:q * d, 0:r], S[:, t % RING, 0:q * d], O[:, t % RING, 0:r], start=False, stop=False,
                                         skip_group_check=True).then_inc(tile_free[L], 1)
                    if two_level:
                        pe.wait_ge(tile2_ready[L], k * 2 + 2)
                        nc.tensor.matmul(agg[0:q * d, 0:r], S2[s][:, 0:q * d], O2[s][:, 0:r], start=False, stop=False,
                                         skip_group_check=True).then_inc(tile2_free[L], 1)

                in_pairs(pe, first_level if L == "cn" and windows else front, back, **({"middle": {"l1": transpose_and_rows, "l3": hidden_rest}[L]} if L in ("l1", "l3") and windows else {}))

            lin = [0, 0]

            def linear(src17, w):
                pe.wait_ge(lin_in, lin[1] + 1)
                for k in range(NJ // 4):
                    if k >= 2:
                        pe.wait_ge(lin_sb, lin[0] + k - 1)
                    for j in range(4):
                        last = nc.tensor.transpose(psT[k % 2][0:D + 1, j * NP_:(j + 1) * NP_], src17[:, 4 * k + j, 0:D + 1], ident[0:NP_, 0:NP_])
                    last.then_inc(lin_ps, 1)
                pe.wait_ge(lin_sb, lin[0] + NJ // 4)
                for j in range(NJ):
                    last = nc.tensor.matmul(psV[0:NP_, j * D:(j + 1) * D], XT[:, j * NP_:(j + 1) * NP_], w[:, :], start=True, stop=True)
                last.then_inc(lin_mm, 1)
                lin[0] += NJ // 4
                lin[1] += 1

            def pe_scatter(L):
                q, r, d, per_edge = SCATTER[L]
                nc.tensor.matmul(agg[0:q * d, 0:r], zeros[:, 0:q * d], zeros[:, 0:r], start=True, stop=False,
                                 skip_group_check=True).then_inc(tile_free[L], RING)
                two_paths(pe, L, pe_edges)
                nc.tensor.matmul(agg[0:q * d, 0:r], zeros[:, 0:q * d], zeros[:, 0:r], start=False, stop=True,
                                 skip_group_check=True).then_inc(agg_done, 1)
                pe.wait_ge(agg_sb, nth[L])
                for c in range(4):
                    last = nc.tensor.transpose(psT[0][0:r // 4, c * q * d:(c + 1) * q * d], AG[0:q * d, c * (r // 4):(c + 1) * (r // 4)],
                                               ident[0:q * d, 0:q * d])
                last.then_inc(aggT, 1)

            def pe_table(L):
                pe.wait_ge(xt_in, nth_xt[L])
                for k in range(NJ // 4):
                    if k >= 2:
                        pe.wait_ge(xt_sb, xt_before[L] + k - 1)
                    for j in range(4):
                        last = nc.tensor.transpose(psT[k % 2][0:D + 1, j * NP_:(j + 1) * NP_],
                                                   (HT if L == "l2" else H17)[:, 4 * k + j, :], ident[0:NP_, 0:NP_])
                    last.then_inc(xt_ps, 1)
                pe.wait_ge(xt_sb, xt_before[L] + NJ // 4)
                if L != "l2":
                    cols, per = PROJ[L]
                    w = {"c1": wc[0], "c2": wc[1], "l1": wl1, "l3": wpq}[L]
                    for k in range(-(-NJ // per)):
                        if k >= 4:
                            pe.wait_ge(proj_sb, proj_before[L] + k - 3)
                        for j in range(k * per, min(NJ, (k + 1) * per)):
                            last = nc.tensor.matmul(psM[k % 4][0:NP_, (j % per) * cols:(j % per + 1) * cols],
                                                    XT[:, j * NP_:(j + 1) * NP_], w[:, :], start=True, stop=True)
                        last.then_inc(proj_ps, 1)
                else:
                    for j in range(NJ):
                        last = nc.tensor.matmul(psV[0:NP_, j * D:(j + 1) * D], XT[:, j * NP_:(j + 1) * NP_], wloop[:, :], start=True, stop=True)
                    last.then_inc(loop_ps, 1)
                    for k in range(NJ // 4):
                        pe.wait_ge(xt_sb, xt_before[L] + NJ // 4 + k - 1)
                        for j in range(4):
                            for a, K in enumerate((KA, KB)):
                                last = nc.tensor.transpose(psTb[k % 2][0:K, (2 * j + a) * NP_:(2 * j + a + 1) * NP_], h_parts[a][:, 4 * k + j, 0:K], ident_b[0:NP_, 0:NP_])
                        last.then_inc(xt_ps, 1)
                    pe.wait_ge(wrel_in, 16 * (2 + 6))
                    with pe.Fori(0, NJ // 2, 1) as i:
                        for h in range(2):
                            pe.wait_ge(xtj_set, i * 2 + h + 1)
                            for c in range(EC):
                                pe.wait_ge((rel_act, rel_dve)[c % 2], i * EC + h * (EC // 2) + c // 2 + 1)
                                for a, K in enumerate((KA, KB)):
                                    last = nc.tensor.matmul(psM[c % 4][0:NP_, 0:ECOLS], XTj[0:K, h, a, :], wrel_b[0:K, c * ECOLS:(c + 1) * ECOLS],
                                                            start=a == 0, stop=a == 1)
                                last.then_inc(rel_ps, 1)

            for L in LAYERS:
                if L == "cn":
                    pe_table("c1")
                    pe.wait_ge(proj_sb, proj_banks["c1"])
                elif L != "c1":
                    pe_table(L)
                pe_scatter(L)
                if L == "l1":
                    linear(HT, wlin)
                    pe.wait_ge(lin_in, lin[1] + 1)
                    for k in range(NJ // 4):
                        if k >= 2:
                            pe.wait_ge(lin_sb, lin[0] + k - 1)
                        for j in range(4):
                            last = nc.tensor.transpose(psT[k % 2][0:D + 1, j * NP_:(j + 1) * NP_], H17[:, 4 * k + j, :], ident[0:NP_, 0:NP_])
                        last.then_inc(lin_ps, 1)
                    pe.wait_ge(lin_sb, lin[0] + NJ // 4)
                    lin[0] += NJ // 4
                    lin[1] += 1
                    for j in range(NJ):
                        if j >= 4:
                            pe.wait_ge(upd_read, j - 3)
                        nc.tensor.matmul(psM[j % 4][0:NP_, 0:D * D], XT[:, j * NP_:(j + 1) * NP_], wupd[:, :], start=True, stop=True).then_inc(upd_ps, 1)
                    linear(HT, wulin)

        def relay_back(dve, v, link, L, turn):
            q, r, d, _ = SCATTER[L]
            dve.wait_ge(aggT, nth[L])
            v.tensor_copy(AGT[:, :, 0:d].rearrange("p (q c) d -> p q c d", q=q),
                          psT[0][0:CHUNK7, 0:4 * q * d].rearrange("p (c q d) -> p q c d", c=4, q=q)).then_inc(relay_made, 1)
            dve.wait_ge(relay_in, 16 * turn)

        @block.vector
        def _(dve):
            v = nc.vector
            step = [0, None, 0]

            def link(ins):
                if step[1] is None:
                    step[0] += 1
                    ins.then_inc(dve_step, 1)
                    dve.wait_ge(dve_step, step[0])
                else:
                    counter, before = step[1]
                    step[2] += 1
                    ins.then_inc(counter, 1)
                    dve.wait_ge(counter, before + step[2])

            def bc(ap2, n, d):
                return ap2.rearrange("p (n a) -> p n a", a=1).broadcast_to([ap2.shape[0], n, d])

            def tt(o, a, b, op):
                link(v.tensor_tensor(o, a, b, op))

            def ts(o, a, s1, op0, s2=None, op1=None):
                link(v.tensor_scalar(o, a, s1, s2, op0, op1) if op1 is not None else v.tensor_scalar(o, a, s1, None, op0))

            def red(o, a, op=ALU.add):
                link(v.tensor_reduce(o, a, axis=AX, op=op))

            for free in (rows_used, *key_used.values()):
                dve.sem_inc(free, SLOTS)
            for t in (src_i, dst_i, rel_row, type_row, X):
                link(v.memset(t[tuple(slice(None) for _ in t.shape)], 0))
            link(v.memset(ea_sb[:, :, :], 0.0))
            v.memset(zeros[:, 0:1], 0.0).then_inc(zeroed, 1)
            for t in (wc[0], wc[1], wl1, wupd, wlin, wulin, wloop, wpq, w2):
                link(v.memset(t[:, :], 0.0))
            link(v.memset(H17[:, :, D:D + 1], 1.0))
            link(v.memset(HT[:, :, :], 1.0))
            link(v.memset(O_XT[:, NPAD:], 0.0))
            for s in range(SLOTS):
                link(v.memset(msg[s][:, :, :, D:D + 1], 1.0))
            v.memset(zeros[:, :], 0.0).then_inc(zeroed, 1)
            dve.wait_ge(zeroed, 2)

            sf, df, pad, hi, lo, t_f, t_l, t_m = (big[:, k * T:(k + 1) * T] for k in range(8))

            def grp(a):
                return a.rearrange("p (k g) -> p k g", g=G)

            dve.wait_ge(consts_made, 5)
            dve.wait_ge(edges_in, 16 * 12)
            ts(pad, lane, float(E), ALU.is_ge, PAD_KEY, ALU.mult)
            link(v.tensor_copy(sf, src_i[:, :]))
            link(v.tensor_copy(df, dst_i[:, :]))
            link(v.tensor_copy(t_f, rel_row[:, :]))

            def split(val, q, r):
                ts(hi, val, float(r), ALU.is_ge)
                for k in range(2, q):
                    link(v.scalar_tensor_tensor(out=hi, in0=val, scalar=float(k * r), in1=hi, op0=ALU.is_ge, op1=ALU.add))
                link(v.scalar_tensor_tensor(out=lo, in0=hi, scalar=float(-r), in1=val, op0=ALU.mult, op1=ALU.add))

            for name, val, q, r in (("src8", sf, Q8, R8), ("src7", sf, Q7, R7), ("dst7", df, Q7, R7), ("dst8", df, Q8, R8)):
                split(val, q, r)
                link(v.tensor_tensor(keys[name][:, :, 0, :], grp(hi), grp(pad), ALU.add))
                link(v.tensor_copy(keys[name][:, :, 1, :], grp(lo)))
            link(v.tensor_copy(typ[:, :, :], grp(t_f)))
            link(v.scalar_tensor_tensor(out=rel_row[:, :], in0=sf, scalar=float(REL), in1=t_f, op0=ALU.mult, op1=ALU.add))
            link(v.tensor_copy(t_f, type_row[:, :]))
            link(v.scalar_tensor_tensor(out=type_row[:, :], in0=sf, scalar=float(TYPES), in1=t_f, op0=ALU.mult, op1=ALU.add))

            link(v.scalar_tensor_tensor(out=t_l, in0=pad, scalar=-4.0, in1=df, op0=ALU.mult, op1=ALU.add))
            v.tensor_reduce(wa[:, :], grp(t_l), axis=AX, op=ALU.min).then_inc(prep_dve, 1)
            dve.wait_ge(ident_made, 2)
            link(v.tensor_copy(ident_b[:, :], ident[:, :]))
            dve.wait_ge(prep_pe, 1)
            red(wc_[0:GROUPS, 0:1], psT[0][0:GROUPS, 0:P], ALU.min)
            ts(wc_[0:GROUPS, 0:1], wc_[0:GROUPS, 0:1], float(NPAD - WIN), ALU.min)
            v.tensor_scalar(wb[0:GROUPS, :], ident[0:GROUPS, 0:GROUPS], wc_[0:GROUPS, 0:1], None, ALU.mult).then_inc(prep_dve, 1)
            dve.wait_ge(prep_pe, 2)
            link(v.tensor_copy(wa[:, :], psT[1][:, 0:GROUPS]))
            tt(grp(t_l), grp(df), wa[:, :].rearrange("p (k a) -> p k a", a=1).broadcast_to([P, GROUPS, G]), ALU.subtract)
            tt(t_l, t_l, pad, ALU.add)
            link(v.tensor_copy(loc[:, :, :], grp(t_l)))
            v.tensor_reduce(wc_[:, 0:1], t_l, axis=AX, op=ALU.max).then_inc(prep_dve, 1)
            ts(wb[:, :], wa[:, :], iota_p[:, 0:1], ALU.add)
            link(v.tensor_copy(win_row[:, :], wb[:, :]))
            for name, q, r in (("8", Q8, R8), ("7", Q7, R7)):
                key = win_key[name]
                ts(key[:, :, 0], wb[:, :], float(r), ALU.is_ge)
                for n in range(2, q):
                    link(v.scalar_tensor_tensor(out=key[:, :, 0], in0=wb[:, :], scalar=float(n * r), in1=key[:, :, 0], op0=ALU.is_ge, op1=ALU.add))
                link(v.scalar_tensor_tensor(out=key[:, :, 1], in0=key[:, :, 0], scalar=float(-r), in1=wb[:, :], op0=ALU.mult, op1=ALU.add))
            dve.wait_ge(prep_pe, 3)
            red(n1[0:1, 0:1], psT[0][0:1, 0:P], ALU.max)
            v.tensor_scalar(flag[:, :], n1[0:1, 0:1], float(WIN - 1), None, ALU.is_gt).then_inc(flag_made, 1)
            dve.wait_ge(flag_made, 1)

            n_std = [0]
            n_act = [0]
            n_lin = [0]

            def relu_layernorm(dest):
                red(n3[:, :], X[:, :, :])
                ts(n3[:, :], n3[:, :], 1.0 / D, ALU.mult)
                tt(A[:, :, :], X[:, :, :], bc(n3[:, :], NJ, D), ALU.subtract)
                tt(B[:, :, :], A[:, :, :], A[:, :, :], ALU.mult)
                red(n4[:, :], B[:, :, :])
                v.tensor_scalar(n1[:, :], n4[:, :], 1.0 / D, 1e-5, ALU.mult, ALU.add).then_inc(var_made, 1)
                n_std[0] += 1
                dve.wait_ge(std_made, n_std[0])
                link(v.reciprocal(n3[:, :], n2[:, :]))
                tt(A[:, :, :], A[:, :, :], bc(n3[:, :], NJ, D), ALU.mult)
                ts(dest, A[:, :, :], 0.0, ALU.max)

            def call_act():
                n_act[0] += 1
                dve.sem_inc(act_in, 1)
                dve.wait_ge(act_out, n_act[0])

            def norm_of(o, val, sq_buf=B):
                tt(sq_buf[:, :, :], val, val, ALU.mult)
                red(o, sq_buf[:, :, :])

            def fill_tiles(L, i, s, a, of, middle=lambda: None):
                q, r, d, per_edge = SCATTER[L]
                for g in range(G):
                    if g == RING:
                        middle()
                    dve.wait_ge(tile_free[L], i * (SLOTS * of * G) + (s * of + a) * G + g + 1)
                    v.scalar_tensor_tensor(
                        out=S[:, g % RING, 0:q * d].rearrange("p (q d) -> p q d", q=q), in0=bc(iota_q[:, 0:q], q, d),
                        scalar=kf[s][:, 2 * a, g:g + 1],
                        in1=msg[s][:, a, g, 0:d].rearrange("p (a d) -> p a d", a=1).broadcast_to([P, q, d]),
                        op0=ALU.is_equal, op1=ALU.mult).then_inc(tile_ready[L], 1)
                    if g not in BY_ACT[L]:
                        v.tensor_scalar(O[:, g % RING, 0:r], iota_r[:, 0:r], kf[s][:, 2 * a + 1, g:g + 1], None,
                                        ALU.is_equal).then_inc(tile_ready[L], 1)
                dve.wait_ge(tile_ready[L], (i * SLOTS + s) * ready_before(L, of * G - 1) + ready_before(L, (a + 1) * G - 1))
                dve.wait_ge(tile_act[L], (i * SLOTS + s) * acts_of(L, of * G) + acts_of(L, (a + 1) * G))

            def split3(parts, val, rest):
                link(v.tensor_copy(parts[0], val))
                tt(rest, val, parts[0], ALU.subtract)
                link(v.tensor_copy(parts[1], rest))
                tt(parts[2], rest, parts[1], ALU.subtract)

            steps_before = [0]

            def dve_edges(L, windows):
                q, r, d, per_edge = SCATTER[L]
                two_level = windows and L in BY_DST
                windowed = windows and L in WINDOW
                gathers = {"cn": 0, "c1": 2, "c2": 1, "l1": 1, "l2": 1, "l3": 2}[L] - (1 if windowed else 0)
                per_key = 2 if L == "l3" else 1
                scatters = range(per_edge - (1 if two_level else 0))
                steps_front = 4 if windowed else 2 if L == "cn" and windows else 1 if two_level else 0
                steps_back = ({"cn": 1, "c1": 5, "c2": 1, "l1": 2, "l2": 10, "l3": 16 if windows else 17}[L]
                              + ((1 + (4 if PARTS[L] == 3 else 0)) if two_level else 0))
                if two_level:
                    dve.sem_inc(wsum_read[L], 1)
                if L == "l3":
                    dve.sem_inc(v_read, 1)

                def front(i, s):
                    k = i * SLOTS + s
                    group = bass.ds(k, 1)
                    step[1:] = [(step_front, steps_before[0] + k * steps_front), 0]
                    if windows and (two_level or L in WINDOW):
                        made = v.tensor_tensor(hot[s][:, :, :], iota_r[:, 0:WIN].rearrange("p (a n) -> p a n", a=1).broadcast_to([P, G, WIN]),
                                               loc[:, group, :].rearrange("p a (g b) -> p (a g) b", b=1).broadcast_to([P, G, WIN]), ALU.is_equal)
                        if L in WINDOW:
                            made.then_inc(hot_made, 1)
                        else:
                            link(made)
                    if windows and L in WINDOW:
                        cols, per = WINDOW[L]
                        dve.wait_ge(win_in[L, s], i * 16 + 16)
                        split3([win_parts[s][:, n, 0:WIN_COLS[L]] for n in range(3)], win[s][:, 0:WIN_COLS[L]], win[s][:, 0:WIN_COLS[L]])
                        dve.sem_inc(win_split, 1)
                    assert step[2] == steps_front, (L, windows, step[2])

                def second_level(i, s):
                    k = i * SLOTS + s
                    dve.wait_ge(wsum_ps[L], k + 1)
                    red(wsum[s][:, 0:d], psM[0][:, 0:PARTS[L] * d].rearrange("p (n d) -> p d n", d=d))
                    dve.sem_inc(wsum_read[L], 1)
                    dve.wait_ge(tile2_free[L], k + 1)
                    v.scalar_tensor_tensor(
                        out=S2[s][:, 0:q * d].rearrange("p (q d) -> p q d", q=q), in0=bc(iota_q[:, 0:q], q, d), scalar=kw[s][:, 0, 0:1],
                        in1=wsum[s][:, 0:d].rearrange("p (a d) -> p a d", a=1).broadcast_to([P, q, d]),
                        op0=ALU.is_equal, op1=ALU.mult).then_inc(tile2_ready[L], 1)
                    v.tensor_scalar(O2[s][:, 0:r], iota_r[:, 0:r], kw[s][:, 0, 1:2], None, ALU.is_equal).then_inc(tile2_ready[L], 1)
                    dve.wait_ge(tile2_ready[L], k * 2 + 2)

                def count_front(i, s):
                    k = i * SLOTS + s
                    step[1:] = [(step_front, steps_before[0] + k * steps_front), 0]
                    hot_of_group(i, s)
                    link(v.tensor_tensor(msg_parts[s][:, :, 0:REL], *type_hot(bass.ds(k, 1)), ALU.is_equal))
                    dve.sem_inc(parts_made[L], 1)
                    dve.sem_inc(rows_used, 1)

                def count_back(i, s, following):
                    k = i * SLOTS + s
                    step[1:] = [(step_of[L], k), 0]
                    dve.wait_ge(key_set[L], k + 1)
                    second_level(i, s)
                    dve.sem_inc(key_used[L], 1)

                def hot_of_group(i, s):
                    return link(v.tensor_tensor(hot[s][:, :, :], iota_r[:, 0:WIN].rearrange("p (a n) -> p a n", a=1).broadcast_to([P, G, WIN]),
                                                loc[:, bass.ds(i * SLOTS + s, 1), :].rearrange("p a (g b) -> p (a g) b", b=1).broadcast_to([P, G, WIN]),
                                                ALU.is_equal))

                def back(i, s, ahead):
                    k = i * SLOTS + s

                    def front_ahead():
                        if two_level:
                            dve.wait_ge(wsum_ps[L], k + 1)
                        if ahead:
                            now = step[1:]
                            front(i + 1, s)
                            step[1:] = now

                    here = bass.ds(i * (SLOTS * G) + s * G, G)
                    group = bass.ds(k, 1)
                    m = msg[s]
                    step[1:] = [(step_of[L], k * steps_back), 0]
                    if gathers:
                        dve.wait_ge(gathered[L, s], i * (gathers * G * 16) + gathers * G * 16)
                    if windows and L in WINDOW:
                        n = -(-G // WINDOW[L][1])
                        dve.wait_ge(rows_sb[L], k * n + n + 1)
                    if L == "cn":
                        tt(msg_parts[s][:, :, 0:REL] if windows else m[:, 0, :, 0:REL], *type_hot(group), ALU.is_equal)
                    if L == "c1":
                        tt(res[:, :, 0:REL], *type_hot(group), ALU.is_equal)
                        tt(res[:, :, 0:REL], res[:, :, 0:REL], gb[s][:, :, 0:REL], ALU.mult)
                        red(sm[s][:, 0, :], res[:, :, 0:REL])
                        link(v.tensor_copy(norm_sb[:, here], sm[s][:, 0, :]))
                        tt(m[:, 0, :, 0:D], ga[s][:, :, 0:D], bc(sm[s][:, 0, :], G, D), ALU.mult)
                    if L == "c2":
                        tt(m[:, 0, :, 0:D], ga[s][:, :, 0:D], norm_sb[:, here].rearrange("p (g a) -> p g a", a=1).broadcast_to([P, G, D]), ALU.mult)
                    if L == "l1":
                        z = gb[s][:, :, 0:DE * D].rearrange("p g (j h) -> p g j h", j=DE)
                        tt(z, z, ea_sb[:, here, :].rearrange("p g (j a) -> p g j a", a=1).broadcast_to([P, G, DE, D]), ALU.mult)
                        v.tensor_reduce(sq[:, :, :], z.rearrange("p g j h -> p g h j"), axis=AX, op=ALU.add).then_inc(m_made, 1)
                        dve.wait_ge(sig_made, k + 1)
                        link(v.scalar_tensor_tensor(out=m[:, 0, :, 0:D], in0=sq[:, :, :], scalar=NORM_MSG, in1=sg[s][:, :, :], op0=ALU.mult, op1=ALU.mult))
                    if L == "l2":
                        hyperbolic_messages(i, s, k, m)
                    if L == "l3":
                        sheaf_messages(i, s, k, m, windows)
                    if two_level:
                        if PARTS[L] == 3:
                            split3([msg_parts[s][:, :, n * d:(n + 1) * d] for n in range(3)], m[:, per_edge - 1, :, 0:d], res[:, :, 0:d])
                        dve.sem_inc(parts_made[L], 1)
                    dve.sem_inc(rows_used, 1)
                    dve.wait_ge(key_set[L], k * per_key + per_key)
                    for a in scatters:
                        fill_tiles(L, i, s, a, len(scatters), *((front_ahead,) if windows else ()))
                    if two_level:
                        if not scatters:
                            front_ahead()
                        second_level(i, s)
                    dve.sem_inc(key_used[L], 1)
                    assert step[2] == steps_back, (L, windows, step[2])

                if L == "cn" and windows:
                    in_pairs(dve, count_front, count_back)
                    steps_before[0] += GROUPS * steps_front
                    step[1:] = [None, 0]
                    return
                for s in range(SLOTS):
                    front(0, s)
                with dve.Fori(0, ITERS - 1, 1) as i:
                    for s in range(SLOTS):
                        back(i, s, True)
                for s in range(SLOTS):
                    back(ITERS - 1, s, False)
                if windows:
                    steps_before[0] += GROUPS * steps_front
                step[1:] = [None, 0]

            def type_hot(group):
                return (iota_q[:, :].rearrange("p (a t) -> p a t", a=1).broadcast_to([P, G, REL]),
                        typ[:, group, :].rearrange("p a (g b) -> p (a g) b", b=1).broadcast_to([P, G, REL]))

            def edge_pass(L):
                two_paths(dve, L, dve_edges)

            def hyperbolic_messages(i, s, k, m):
                row, z = ga[s][:, :, 0:D], sm[s]
                tt(sq[:, :, :], row, row, ALU.mult)
                red(z[:, 0, :], sq[:, :, :])
                v.tensor_scalar(z[:, 1, :], z[:, 0, :], 1e-10, None, ALU.max).then_inc(sq_made, 1)
                dve.wait_ge(tanh_made, k * 2 + 2)
                ts(z[:, 4, :], z[:, 2, :], SC, ALU.mult)
                link(v.reciprocal(z[:, 4, :], z[:, 4, :]))
                tt(z[:, 4, :], z[:, 4, :], z[:, 3, :], ALU.mult)
                tt(z[:, 5, :], z[:, 4, :], z[:, 4, :], ALU.mult)
                tt(z[:, 5, :], z[:, 5, :], z[:, 0, :], ALU.mult)
                ts(z[:, 5, :], z[:, 5, :], -0.5 * C, ALU.mult, 0.5 * (1.0 + EPS), ALU.add)
                link(v.reciprocal(m[:, 0, :, D], z[:, 5, :]))
                tt(z[:, 4, :], z[:, 4, :], m[:, 0, :, D], ALU.mult)
                v.tensor_tensor(m[:, 0, :, 0:D], row, bc(z[:, 4, :], G, D), ALU.mult).then_inc(hyp_made, 1)
                dve.wait_ge(hyp_made, k + 1)

            def sheaf_messages(i, s, k, m, windows):
                rs, rd, z = ga[s], gb[s], sm[s]

                def both(a, *operands):
                    half = v.tensor_tensor(*operands)
                    if a == 1:
                        link(half)

                if not windows:
                    p_, q_ = slice(XD, XD + HID), slice(XD + HID, XD + 2 * HID)
                    tt(hid[:, :, 0:HID], rs[:, :, p_], rd[:, :, q_], ALU.add)
                    v.tensor_tensor(hid[:, :, HID:], rd[:, :, p_], rs[:, :, q_], ALU.add).then_inc(hid_made, 1)
                dve.wait_ge(v_ps, k * 4 + 4)
                tt(vec[:, :, :, :].rearrange("p g a d -> p g (a d)"), psV[:, 0:G * 2 * D].rearrange("p (g c) -> p g c", g=G),
                   b2[:, :].rearrange("p (a c) -> p a c", a=1).broadcast_to([P, G, 2 * D]), ALU.add)
                dve.sem_inc(v_read, 1)
                whole = lambda t: t[:, :, :, :].rearrange("p g a d -> p (g a) d")
                tt(whole(sq2), whole(vec), whole(vec), ALU.mult)
                red(c2[:, 0, :], whole(sq2))
                ts(c2[:, 0, :], c2[:, 0, :], 1e-24, ALU.max, 0.5, ALU.mult)
                link(v.reciprocal(c2[:, 0, :], c2[:, 0, :]))
                x_of = (rd[:, :, 0:D], rs[:, :, 0:D])
                coef = lambda n, a: c2[:, n, :].rearrange("p (g a) -> p g a", a=2)[:, :, a]
                for a in range(2):
                    both(a, sq2[:, :, a, :], vec[:, :, a, :], x_of[a], ALU.mult)
                red(c2[:, 1, :], whole(sq2))
                tt(c2[:, 1, :], c2[:, 1, :], c2[:, 0, :], ALU.mult)
                tt(whole(sq2), whole(vec), bc(c2[:, 1, :], 2 * G, D), ALU.mult)
                for a in range(2):
                    both(a, y2[:, :, a, :], x_of[a], sq2[:, :, a, :], ALU.subtract)
                for a in range(2):
                    both(a, sq2[:, :, a, :], vec[:, :, 1 - a, :], y2[:, :, a, :], ALU.mult)
                red(c2[:, 1, :], whole(sq2))
                for a in range(2):
                    both(a, coef(1, a), coef(1, a), coef(0, 1 - a), ALU.mult)
                for a in range(2):
                    both(a, sq2[:, :, a, :], vec[:, :, 1 - a, :], c2[:, 1, :].rearrange("p (g a b) -> p g a b", a=2, b=1)[:, :, a, :].broadcast_to([P, G, D]), ALU.mult)
                tt(whole(y2), whole(y2), whole(sq2), ALU.subtract)
                for a in range(2):
                    both(a, m[:, a, :, 0:D], y2[:, :, a, :], (rd, rs)[a][:, :, D:D + 1].broadcast_to([P, G, D]), ALU.mult)

            def agg_nodes(L):
                return psT[0][0:CHUNK8, 0:4 * Q8 * D].rearrange("p (c q d) -> p q c d", c=4, q=Q8)

            def j4(t):
                return t[:, :, 0:D].rearrange("p (q c) d -> p q c d", q=Q8)

            rows = lambda pitch: big[0:NP_, 0:NJ * pitch].rearrange("p (j c) -> p j c", j=NJ)

            dve.wait_ge(x_in, 32)
            relu_layernorm(H17[:, :, 0:D])
            dve.sem_inc(xt_in, 1)
            dve.wait_ge(proj_sb, proj_banks["c1"])
            dve.sem_inc(table_made, 1)
            link(v.tensor_copy(A[:, :, :], rows(REL * D + D)[:, :, REL * D:]))
            edge_pass("cn")
            dve.wait_ge(aggT, nth["cn"])
            link(v.tensor_copy(cnt[:, :, :].rearrange("p (q c) t -> p q c t", q=Q8),
                               psT[0][0:CHUNK8, 0:4 * Q8 * REL].rearrange("p (c q t) -> p q c t", c=4, q=Q8)))
            red(deg_dst[:, :], cnt[:, :, :])
            ts(cnt[:, :, :], cnt[:, :, :], 1.0, ALU.max)
            v.reciprocal(cnt[:, :, :], cnt[:, :, :]).then_inc(norm_made, 1)
            for L in ("c1", "c2"):
                if L == "c2":
                    dve.sem_inc(xt_in, 1)
                    dve.wait_ge(proj_sb, proj_before[L] + proj_banks[L])
                    dve.sem_inc(table_made, 1)
                    link(v.tensor_copy(A[:, :, :], rows(REL * D + D)[:, :, REL * D:]))
                edge_pass(L)
                dve.wait_ge(aggT, nth[L])
                tt(j4(B), agg_nodes(L), j4(A), ALU.add)
                if L == "c1":
                    ts(H17[:, :, 0:D], B[:, :, :], 0.0, ALU.max)
            red(n3[:, :], B[:, :, :], ALU.max)
            tt(B[:, :, :], B[:, :, :], bc(n3[:, :], NJ, D), ALU.subtract)
            call_act()
            red(n1[:, :], C_[:, :, :])
            call_act()
            tt(B[:, :, :], B[:, :, :], bc(n2[:, :], NJ, D), ALU.subtract)
            tt(X[:, :, :], X[:, :, :], B[:, :, :], ALU.add)

            L = "l1"
            relu_layernorm(H17[:, :, 0:D])
            dve.sem_inc(xt_in, 1)
            dve.wait_ge(proj_sb, proj_before[L] + proj_banks[L])
            dve.sem_inc(table_made, 1)
            dve.wait_ge(ea_in, 48)
            edge_pass(L)
            relay_back(dve, v, link, L, 1)
            link(v.tensor_copy(degs[:, :], AGR[:, :, D]))
            link(v.tensor_copy(HT[:, :, 0:D], AGR[:, :, 0:D]))
            dve.sem_inc(lin_in, 1)
            dve.wait_ge(lin_mm, 1)
            psVn = psV[0:NP_, 0:NJ * D].rearrange("p (j d) -> p j d", j=NJ)
            ts(A[:, :, :], psVn, NORM_LIN, ALU.mult)
            dve.sem_inc(lin_in, 1)
            for j in range(NJ):
                dve.wait_ge(upd_ps, j + 1)
                v.tensor_tensor(prod[:, j % 2, :].rearrange("p (h k) -> p h k", h=D), psM[j % 4][0:NP_, 0:D * D].rearrange("p (h k) -> p h k", h=D),
                                A[:, j, :].rearrange("p (h a) -> p h a", a=1).broadcast_to([NP_, D, D]), ALU.mult).then_inc(upd_read, 1)
                dve.wait_ge(upd_read, j + 1)
                link(v.tensor_reduce(B[:, j, :], prod[:, j % 2, :].rearrange("p (h k) -> p k h", h=D), axis=AX, op=ALU.add))
            call_act()
            link(v.scalar_tensor_tensor(out=HT[:, :, 0:D], in0=B[:, :, :], scalar=NORM_UPD, in1=C_[:, :, :], op0=ALU.mult, op1=ALU.mult))
            dve.sem_inc(lin_in, 1)
            tt(X[:, :, :], X[:, :, :], H17[:, :, 0:D], ALU.add)
            dve.wait_ge(lin_mm, 2)
            link(v.scalar_tensor_tensor(out=X[:, :, :], in0=psVn, scalar=NORM_LIN, in1=X[:, :, :], op0=ALU.mult, op1=ALU.add))

            L = "l2"
            relu_layernorm(H17[:, :, 0:D])
            norm_of(n1[:, :], H17[:, :, 0:D])
            ts(n1[:, :], n1[:, :], 1e-10, ALU.max)
            call_act()
            ts(n2[:, :], n2[:, :], SC, ALU.mult)
            ts(n3[:, :], n2[:, :], -1.0 + BALL, ALU.max, 1.0 - BALL, ALU.min)
            tt(n4[:, :], n3[:, :], n3[:, :], ALU.mult)
            ts(n5[:, :], n4[:, :], 1.0 / 23, ALU.mult, 1.0 / 21, ALU.add)
            for t in range(19, 0, -2):
                tt(n5[:, :], n5[:, :], n4[:, :], ALU.mult)
                ts(n5[:, :], n5[:, :], 1.0 / t, ALU.add)
            tt(HT[:, :, 0:D], H17[:, :, 0:D], bc(n5[:, :], NJ, D), ALU.mult)
            pa, pb = h_parts
            block = lambda p_, b: p_[:, :, b * (D + 1):(b + 1) * (D + 1)]
            for b in range(3):
                link(v.tensor_copy(block(pa, b), HT[:, :, :]))

            tt(AGR[:, :, :], HT[:, :, :], block(pa, 0), ALU.subtract)
            for b in range(3, 6):
                link(v.tensor_copy(block(pa, b), AGR[:, :, :]))
            tt(AGR[:, :, :], AGR[:, :, :], block(pa, 3), ALU.subtract)
            for b in range(3):
                link(v.tensor_copy(block(pb, b), AGR[:, :, :]))
            dve.sem_inc(xt_in, 1)
            dve.wait_ge(loop_ps, 1)
            link(v.tensor_copy(V[:, :, :], psVn))
            dve.sem_inc(rel_dve, 2)
            with dve.Fori(0, NJ // 2, 1) as i:
                for h in range(2):
                    dve.wait_ge(row_free[h], i + 1)
                    for c in range(1, EC, 2):
                        dve.wait_ge(rel_ps, i * (2 * EC) + h * EC + c + 1)
                        v.tensor_copy(big[0:NP_, (h * EC + c) * ECOLS:(h * EC + c + 1) * ECOLS], psM[c % 4][0:NP_, 0:ECOLS]).then_inc(rel_dve, 1)
            edge_pass(L)
            relay_back(dve, v, link, L, 2)
            deg = deg_dst[:, :]
            ts(n1[:, :], deg, 1.0, ALU.max)
            call_act()
            link(v.reciprocal(n2[:, :], n2[:, :]))
            tt(n3[:, :], deg, n2[:, :], ALU.mult)
            ts(n3[:, :], n3[:, :], EPS, ALU.add)
            link(v.reciprocal(n3[:, :], n3[:, :]))
            tt(n3[:, :], n3[:, :], n2[:, :], ALU.mult)
            tt(n4[:, :], n3[:, :], AGR[:, :, D], ALU.mult)
            ts(n4[:, :], n4[:, :], EPS, ALU.add)
            link(v.reciprocal(n4[:, :], n4[:, :]))
            tt(A[:, :, :], AGR[:, :, 0:D], bc(n3[:, :], NJ, D), ALU.mult)
            tt(A[:, :, :], A[:, :, :], bc(n4[:, :], NJ, D), ALU.mult)
            tt(degs[:, :], degs[:, :], deg, ALU.add)
            norm_of(n1[:, :], A[:, :, :])
            ts(n1[:, :], n1[:, :], 1e-10, ALU.max)
            call_act()
            link(v.reciprocal(n2[:, :], n2[:, :]))
            ts(n2[:, :], n2[:, :], (1.0 - BALL) / SC, ALU.mult, 1.0, ALU.min)
            tt(A[:, :, :], A[:, :, :], bc(n2[:, :], NJ, D), ALU.mult)
            norm_of(n1[:, :], V[:, :, :])
            ts(n1[:, :], n1[:, :], 1e-10, ALU.max)
            call_act()
            ts(n2[:, :], n2[:, :], SC, ALU.mult)
            call_act()
            link(v.reciprocal(n2[:, :], n2[:, :]))
            tt(n3[:, :], n3[:, :], n2[:, :], ALU.mult)
            tt(V[:, :, :], V[:, :, :], bc(n3[:, :], NJ, D), ALU.mult)
            norm_of(n1[:, :], A[:, :, :])
            norm_of(n2[:, :], V[:, :, :])
            tt(B[:, :, :], A[:, :, :], V[:, :, :], ALU.mult)
            red(n3[:, :], B[:, :, :])
            ts(n3[:, :], n3[:, :], 2.0 * C, ALU.mult, 1.0, ALU.add)
            link(v.scalar_tensor_tensor(out=n4[:, :], in0=n2[:, :], scalar=C, in1=n3[:, :], op0=ALU.mult, op1=ALU.add))
            ts(n5[:, :], n1[:, :], -C, ALU.mult, 1.0, ALU.add)
            tt(n6[:, :], n1[:, :], n2[:, :], ALU.mult)
            link(v.scalar_tensor_tensor(out=n6[:, :], in0=n6[:, :], scalar=C * C, in1=n3[:, :], op0=ALU.mult, op1=ALU.add))
            ts(n6[:, :], n6[:, :], 1e-10, ALU.max)
            link(v.reciprocal(n6[:, :], n6[:, :]))
            tt(A[:, :, :], A[:, :, :], bc(n4[:, :], NJ, D), ALU.mult)
            tt(V[:, :, :], V[:, :, :], bc(n5[:, :], NJ, D), ALU.mult)
            tt(A[:, :, :], A[:, :, :], V[:, :, :], ALU.add)
            tt(A[:, :, :], A[:, :, :], bc(n6[:, :], NJ, D), ALU.mult)
            tt(X[:, :, :], X[:, :, :], A[:, :, :], ALU.add)

            L = "l3"
            relu_layernorm(H17[:, :, 0:D])
            dve.sem_inc(xt_in, 1)
            ts(n1[:, :], degs[:, :], 1e-5, ALU.max)
            dve.wait_ge(proj_sb, proj_before[L] + proj_banks[L])
            call_act()
            link(v.reciprocal(n2[:, :], n2[:, :]))
            link(v.tensor_copy(rows(W5W)[:, :, 0:D], H17[:, :, 0:D]))
            link(v.tensor_copy(rows(W5W)[:, :, D], n2[:, :]))
            link(v.tensor_copy(rows(W5W)[:, :, W5:], rows(W5W)[:, :, XD:XD + HID]))
            dve.sem_inc(table_made, 1)
            edge_pass(L)
            dve.wait_ge(aggT, nth[L])
            link(v.tensor_copy(j4(A), agg_nodes(L)))
            tt(A[:, :, :], A[:, :, :], bc(n2[:, :], NJ, D), ALU.mult)
            tt(A[:, :, :], A[:, :, :], H17[:, :, 0:D], ALU.add)
            ts(A[:, :, :], A[:, :, :], 0.0, ALU.max)
            v.tensor_tensor(X[:, :, :], X[:, :, :], A[:, :, :], ALU.add).then_inc(x_made, 1)

NORM_MSG = float(np.float32(1.0) / np.float32(np.sqrt(D * DE)))
NORM_UPD = float(np.float32(1.0) / np.float32(np.sqrt(D * D)))
NORM_LIN = float(np.float32(1.0) / np.float32(np.sqrt(D)))
SC, C, EPS, BALL = 0.1, 0.01, 1e-6, 1e-5
PROJ = {"c1": (REL * D + D, 3), "c2": (REL * D + D, 3), "l1": (DE * D, 4), "l3": (2 * HID, 4)}
WREL_STEPS = 3 + 2
WEIGHT_LOADS = 6 + 2 + 3 + 4 + 3
_A = mybir.ActivationFunctionType
SQ = (_A.Sqrt, "n2", "n1", 1.0)
LIN = ("T", None, None, None)
NODE_FUNCS = {("c2", "end"): [(_A.Exp, "C", "B", 1.0), (_A.Ln, "n2", "n1", 1.0)],
              ("l1", "end"): [LIN, LIN, (_A.Sigmoid, "C", "B", NORM_UPD), LIN],
              ("l2", "start"): [SQ], ("l2", "end"): [SQ, SQ, SQ, (_A.Tanh, "n3", "n2", 1.0)], ("l3", "table"): [SQ]}

_INS = ["x", "src", "dst", "edge_attr_8", "edge_type_230", "edge_type_8",
        "L0_gnn_W1", "L0_gnn_root1", "L0_gnn_b1", "L0_gnn_W2", "L0_gnn_root2", "L0_gnn_b2",
        "L1_gnn_W_msg_tp", "L1_gnn_W_msg_lin", "L1_gnn_W_upd_tp", "L1_gnn_W_upd_lin",
        "L2_gnn_rel_weight", "L2_gnn_loop_weight", "L2_gnn_rel_emb",
        "L3_gnn_W1", "L3_gnn_b1", "L3_gnn_W2", "L3_gnn_b2"]

_TRANSPOSED = ("L3_gnn_W1", "L3_gnn_W2")


def kernel(**inputs):
    import numpy as _np
    import concourse.bacc as _bacc
    from concourse import mybir as _mybir
    from concourse.bass_utils import run_bass_kernel_spmd as _run

    nc = _bacc.Bacc("TRN2", target_bir_lowering=False, num_devices=1)
    arrays, args = {}, []
    for name in _INS:
        a = _np.ascontiguousarray(inputs[name].T if name in _TRANSPOSED else inputs[name])
        arrays[f"in_{name}"] = a
        args.append(nc.dram_tensor(f"in_{name}", a.shape, _mybir.dt.from_np(a.dtype), kind="ExternalInput").ap())
    args.append(nc.dram_tensor("out_x", (N, D), _mybir.dt.float32, kind="ExternalOutput").ap())
    gnn(nc, *args)
    r = _run(nc, [arrays], core_ids=[0])
    return r.results[0]["out_x"]
```
